# Optimizing a Trainium2 kernel written in Bass

```python
import numpy as np
import jax
import jax.numpy as jnp

def _softmax(x, axis=-1):
    return jax.nn.softmax(x, axis=axis)

def _gelu(x):
    return jax.nn.gelu(x, approximate=True)

def _silu(x):
    return jax.nn.silu(x)

def _sigmoid(x):
    return jax.nn.sigmoid(x)

def _layernorm(x, axis=-1, eps=1e-05):
    m = jnp.mean(x, axis=axis, keepdims=True)
    v = jnp.var(x, axis=axis, keepdims=True)
    return (x - m) / jnp.sqrt(v + eps)

def _scatter_add(tgt, idx, src, axis=0):
    return tgt.at[idx].add(src)

def _segment_sum(src, seg, n):
    return jax.ops.segment_sum(src, seg, n)
kernel_name = 'mk_xattn_ffn_d1_seqx_r4_061976'

def setup_inputs(seed: int=0):
    np.random.seed(seed)
    _w = jnp.asarray

    def _rec_inputs():
        import jax
        import jax.numpy as jnp
        _rk = jax.random.key(seed)
        x = 7.22e-05 + 1 * jax.random.normal(jax.random.fold_in(_rk, 1), (8, 256, 512), jnp.float32)
        _lenS = 256 - jax.random.randint(jax.random.fold_in(_rk, 7), (8,), 0, max(1, 256 // 4) + 1, jnp.int32)
        _lenS2 = 256 - jax.random.randint(jax.random.fold_in(_rk, 8), (8,), 0, max(1, 256 // 4) + 1, jnp.int32)
        _ctx_2048P = jax.random.normal(jax.random.fold_in(_rk, 11), (8, 16, 512), jnp.float32)
        _ctx_2048c = jax.random.dirichlet(jax.random.fold_in(_rk, 511), 0.3 * jnp.ones((16,), jnp.float32), (8, 256))
        _ctx_2048t = jnp.einsum('bsk,bkd->bsd', _ctx_2048c, _ctx_2048P)
        _ctx_2048t = _ctx_2048t * jax.lax.rsqrt(jnp.mean(jnp.square(_ctx_2048t)) + 1e-12) * 0.953939
        ctx_2048 = 4.13588e-05 + 0.999923 * (_ctx_2048t + 0.3 * jax.random.normal(jax.random.fold_in(_rk, 611), (8, 256, 512), jnp.float32))
        return (x, ctx_2048)
    x, ctx_2048 = _rec_inputs()

    def _L0_xattn_setup():
        import jax, jax.numpy as jnp
        import numpy as np
        import math
        EMBED = 512
        HEADS = 32
        GROUPS = 8
        GROUP_HEADS = HEADS // GROUPS
        HEAD_DIM = EMBED // HEADS
        B, S = (4, 256)
        key = jax.random.key(seed)
        ks = jax.random.split(key, 8)
        sc = 0.02
        return {'q': jax.random.normal(ks[0], (B, S, EMBED), jnp.float32), 'k': jax.random.normal(ks[1], (B, S, EMBED), jnp.float32), 'v': jax.random.normal(ks[2], (B, S, EMBED), jnp.float32), 'Wq': jax.random.normal(ks[3], (EMBED, EMBED), jnp.float32) * sc, 'Wk': jax.random.normal(ks[4], (GROUPS * HEAD_DIM, EMBED), jnp.float32) * sc, 'Wv': jax.random.normal(ks[5], (GROUPS * HEAD_DIM, EMBED), jnp.float32) * sc, 'Wfc': jax.random.normal(ks[6], (EMBED, EMBED), jnp.float32) * sc, 'bfc': jnp.zeros((EMBED,), jnp.float32)}
    _L0_xattn_all = _L0_xattn_setup()
    _L0_xattn_in = {k: v for k, v in _L0_xattn_all.items() if k in ('Wq', 'Wk', 'Wv', 'Wfc', 'bfc')}
    del _L0_xattn_all

    def _L0_ffn_setup():
        import jax, jax.numpy as jnp
        import numpy as np
        N_EXPERTS = 8
        TOP_K = 2
        N_GROUP = 4
        TOPK_GROUP = 2
        ROUTED_SCALE = 1.0

        def _group_limited_topk(scores):
            T, N = scores.shape
            E = N // N_GROUP
            group_scores = scores.reshape(T, N_GROUP, E).max(axis=-1)
            _, gidx = jax.lax.top_k(group_scores, TOPK_GROUP)
            gmask = jax.nn.one_hot(gidx, N_GROUP, dtype=scores.dtype).sum(1)
            smask = jnp.repeat(gmask, E, axis=1)
            masked = jnp.where(smask > 0, scores, jnp.zeros((), scores.dtype))
            topk_w, topk_i = jax.lax.top_k(masked, TOP_K)
            return (topk_w, topk_i)
        key = jax.random.key(seed)
        ks = jax.random.split(key, 8)
        B, S, H, F, FS, N = (2, 256, 512, 352, 704, N_EXPERTS)
        std = jnp.float32(0.02)
        return {'hidden_states': jax.random.normal(ks[0], (B, S, H), jnp.float32), 'gate_weight': jax.random.normal(ks[1], (N, H), jnp.float32) * std, 'gate_w': jax.random.normal(ks[2], (N, F, H), jnp.float32) * std, 'up_w': jax.random.normal(ks[3], (N, F, H), jnp.float32) * std, 'down_w': jax.random.normal(ks[4], (N, H, F), jnp.float32) * std, 'sh_gate_w': jax.random.normal(ks[5], (FS, H), jnp.float32) * std, 'sh_up_w': jax.random.normal(ks[6], (FS, H), jnp.float32) * std, 'sh_down_w': jax.random.normal(ks[7], (H, FS), jnp.float32) * std}
    _L0_ffn_all = _L0_ffn_setup()
    _L0_ffn_in = {k: v for k, v in _L0_ffn_all.items() if k in ('gate_weight', 'gate_w', 'up_w', 'down_w', 'sh_gate_w', 'sh_up_w', 'sh_down_w')}
    del _L0_ffn_all
    return {'x': x, 'ctx_2048': ctx_2048, 'L0_xattn_Wq': _L0_xattn_in['Wq'], 'L0_xattn_Wk': _L0_xattn_in['Wk'], 'L0_xattn_Wv': _L0_xattn_in['Wv'], 'L0_xattn_Wfc': _L0_xattn_in['Wfc'], 'L0_xattn_bfc': _L0_xattn_in['bfc'], 'L0_ffn_gate_weight': _L0_ffn_in['gate_weight'], 'L0_ffn_gate_w': _L0_ffn_in['gate_w'], 'L0_ffn_up_w': _L0_ffn_in['up_w'], 'L0_ffn_down_w': _L0_ffn_in['down_w'], 'L0_ffn_sh_gate_w': _L0_ffn_in['sh_gate_w'], 'L0_ffn_sh_up_w': _L0_ffn_in['sh_up_w'], 'L0_ffn_sh_down_w': _L0_ffn_in['sh_down_w']}

def reference(x, ctx_2048, L0_xattn_Wq, L0_xattn_Wk, L0_xattn_Wv, L0_xattn_Wfc, L0_xattn_bfc, L0_ffn_gate_weight, L0_ffn_gate_w, L0_ffn_up_w, L0_ffn_down_w, L0_ffn_sh_gate_w, L0_ffn_sh_up_w, L0_ffn_sh_down_w):
    import jax
    import jax.numpy as jnp

    def _L0_xattn_ref(q, k, v, Wq, Wk, Wv, Wfc, bfc):
        import jax, jax.numpy as jnp
        import numpy as np
        import math
        EMBED = 512
        HEADS = 32
        GROUPS = 8
        GROUP_HEADS = HEADS // GROUPS
        HEAD_DIM = EMBED // HEADS
        B, S = (4, 256)
        N, S_, _ = q.shape
        qh = (q @ Wq.T).reshape(N, S_, HEADS, HEAD_DIM).transpose(0, 2, 1, 3)
        kh = (k @ Wk.T).reshape(N, S_, GROUPS, HEAD_DIM).transpose(0, 2, 1, 3)
        vh = (v @ Wv.T).reshape(N, S_, GROUPS, HEAD_DIM).transpose(0, 2, 1, 3)
        kh = jnp.repeat(kh, GROUP_HEADS, axis=1)
        vh = jnp.repeat(vh, GROUP_HEADS, axis=1)
        score = jnp.einsum('bhqd,bhkd->bhqk', qh, kh) / math.sqrt(HEAD_DIM)
        attn = jax.nn.softmax(score, axis=-1)
        out = jnp.einsum('bhqk,bhkd->bhqd', attn, vh)
        out = out.transpose(0, 2, 1, 3).reshape(N, S_, EMBED)
        return out @ Wfc.T + bfc

    def _L0_ffn_ref(hidden_states, gate_weight, gate_w, up_w, down_w, sh_gate_w, sh_up_w, sh_down_w):
        import jax, jax.numpy as jnp
        import numpy as np
        N_EXPERTS = 8
        TOP_K = 2
        N_GROUP = 4
        TOPK_GROUP = 2
        ROUTED_SCALE = 1.0

        def _group_limited_topk(scores):
            T, N = scores.shape
            E = N // N_GROUP
            group_scores = scores.reshape(T, N_GROUP, E).max(axis=-1)
            _, gidx = jax.lax.top_k(group_scores, TOPK_GROUP)
            gmask = jax.nn.one_hot(gidx, N_GROUP, dtype=scores.dtype).sum(1)
            smask = jnp.repeat(gmask, E, axis=1)
            masked = jnp.where(smask > 0, scores, jnp.zeros((), scores.dtype))
            topk_w, topk_i = jax.lax.top_k(masked, TOP_K)
            return (topk_w, topk_i)
        B, S, H = hidden_states.shape
        h = hidden_states.reshape(-1, H)
        logits = h.astype(jnp.float32) @ gate_weight.astype(jnp.float32).T
        scores = jax.nn.softmax(logits, axis=-1)
        topk_w, topk_i = _group_limited_topk(scores)
        topk_w = (topk_w * ROUTED_SCALE).astype(h.dtype)
        wmat = (jax.nn.one_hot(topk_i, N_EXPERTS, dtype=topk_w.dtype) * topk_w[..., None]).sum(axis=1)
        g = jnp.einsum('th,nfh->ntf', h, gate_w)
        u = jnp.einsum('th,nfh->ntf', h, up_w)
        e = jnp.einsum('ntf,nhf->nth', jax.nn.silu(g) * u, down_w)
        routed = jnp.einsum('nth,tn->th', e, wmat)
        sg = h @ sh_gate_w.T
        su = h @ sh_up_w.T
        shared = jax.nn.silu(sg) * su @ sh_down_w.T
        return (routed + shared).reshape(B, S, H)
    x = x + _L0_xattn_ref(_layernorm(x, axis=-1), ctx_2048, ctx_2048, L0_xattn_Wq, L0_xattn_Wk, L0_xattn_Wv, L0_xattn_Wfc, L0_xattn_bfc)
    x = x + _L0_ffn_ref(_layernorm(x, axis=-1), L0_ffn_gate_weight, L0_ffn_gate_w, L0_ffn_up_w, L0_ffn_down_w, L0_ffn_sh_gate_w, L0_ffn_sh_up_w, L0_ffn_sh_down_w)
    return x

_drawn_inputs = setup_inputs


def setup_inputs(seed=0):
    import zlib

    import numpy as np

    out = dict(_drawn_inputs(seed))
    spreads = {'L0_xattn_bfc': (0.0, 0.1)}
    factors = {'L0_xattn_Wq': 7.54,
     'L0_xattn_Wk': 7.594,
     'L0_ffn_gate_weight': 5.648,
     'L0_ffn_gate_w': 4.899,
     'L0_ffn_up_w': 4.799,
     'L0_ffn_down_w': 4.803,
     'L0_ffn_sh_gate_w': 4.299,
     'L0_ffn_sh_up_w': 4.216,
     'L0_ffn_sh_down_w': 4.208}
    for name, (base, spread) in spreads.items():
        noise = np.random.default_rng([zlib.crc32(name.encode()), seed]).standard_normal(out[name].shape)
        drawn = base * np.exp(spread * noise) if base else spread * noise
        out[name] = jnp.asarray(drawn.astype(out[name].dtype))
    for name, factor in factors.items():
        out[name] = (out[name] * factor).astype(out[name].dtype)
    return out
```

```python
from contextlib import ExitStack

import concourse.bass as bass
from concourse import mybir

F32 = mybir.dt.float32
BF16 = mybir.dt.bfloat16
I32 = mybir.dt.int32
ALU = mybir.AluOpType
ACT = mybir.ActivationFunctionType
AX = mybir.AxisListType

P = 128
D = 512
KD = D // P
BATCH, SEQ = 8, 256
T = BATCH * SEQ
TILES = T // P
HEADS, GROUPS, HD = 32, 8, 16
HPG = HEADS // GROUPS
SCALE = HD ** -0.5
EPS = 1e-5
NE, F = 8, 352
SH = 2
FT = [(0, 128), (128, 128), (256, 96)]
GU_W = KD * 2 * F
DN_W = len(FT) * D
SLOTS = 2 * T // P + NE - 1
BLOCKS, BT = 4, 512
TPB = BT // P
KQ = 1 + KD
PARTS_Q = (0, 0, 1, 1, 0, 2)
PARTS_K = (0, 1, 0, 1, 2, 0)
STACK = len(PARTS_Q) * HD
ROWS = STACK + 3
UH = HEADS // 2
UG = UH // HPG
UNITS = 2 * BATCH
FILLS = 4
VW = 32
FREE = 16
EARLY = TILES // 2
PA, PB, PC = SH * EARLY, SLOTS, SH * (TILES - EARLY)


def build(nc, x, ctxT, wqT, wkvT, wfcT, bfc, gwT, wgu, wdn, wdt, out):
    def dram(name, shape, dt=F32):
        return nc.dram_tensor(name, shape, dt, kind="Internal").ap()

    q_parts = dram("q_parts", (3, D, T), BF16)
    k_parts = dram("k_parts", (3, P, T), BF16)
    v_dram = dram("v_dram", (TILES, P, GROUPS * VW))
    v_blocks = v_dram.rearrange("(n a) p c -> n p a c", a=TPB)
    neg_max = dram("neg_max", (UNITS, 3, 2 * UH, P), BF16)
    attn_dram = dram("attn_dram", (BATCH, 2, P, D))
    x2_dram = dram("x2_dram", (TILES, P, D))
    xn2_dram = dram("xn2_dram", (TILES, P, D))
    xnT_dram = dram("xnT_dram", (TILES, P, D))
    slot_x = dram("slot_x", (SLOTS * P, D))
    slot_y = dram("slot_y", (SLOTS * P, D))
    x_blocks = x.rearrange("(n a p) d -> n p a d", a=TPB, p=P)
    x_tiles = x.rearrange("(t p) d -> t p d", p=P)
    out_tiles = out.rearrange("(t p) d -> t p d", p=P)
    slot_x_tiles = slot_x.rearrange("(t p) d -> t p d", p=P)
    slot_y_tiles = slot_y.rearrange("(t p) d -> t p d", p=P)

    with ExitStack() as ctx:
        def sb(name, shape, dt=F32):
            return ctx.enter_context(nc.sbuf_tensor("sb_" + name, shape, dt))

        def sem(name):
            return ctx.enter_context(nc.semaphore(name))

        bank = [ctx.enter_context(nc.psum_tensor(f"bank{i}", [P, 512], F32)) for i in range(8)]

        weights = sb("weights", [P, (NE + SH) * (GU_W + DN_W)])
        GU0, DN0 = 0, NE * GU_W
        SHGU0 = NE * (GU_W + DN_W)
        SHDN0 = SHGU0 + SH * GU_W

        def words(at, n):
            return weights[:, at:at + n]

        q_words, k_words, v_words, p_words = UH * SEQ // 2, UG * SEQ // 2, 2 * UG * VW, 2 * HPG * SEQ
        at = 0
        q_st = [words(at + s * q_words, q_words).bitcast(BF16).rearrange("p (h t) -> p h t", h=UH) for s in range(4)]
        at += 4 * q_words
        k_st = [words(at + s * k_words, k_words).bitcast(BF16).rearrange("p (g t) -> p g t", g=UG) for s in range(4)]
        at += 4 * k_words
        v_st = [words(at + s * v_words, v_words).rearrange("p (k g c) -> p k g c", k=2, g=UG) for s in range(4)]
        at += 4 * v_words
        probs = [words(at + s * p_words, p_words).rearrange("p (k n) -> p k n", k=2) for s in range(2)]
        at += 2 * p_words
        p2_end = at
        at = 0
        x_in = [words(at + s * TPB * D, TPB * D).rearrange("p (a d) -> p a d", a=TPB) for s in range(2)]
        at += 2 * TPB * D
        xnT = [words(at + s * KD * BT, KD * BT).rearrange("p (k t) -> p k t", k=KD) for s in range(2)]
        at += 2 * KD * BT
        cxT = [words(at + s * KD * BT, KD * BT).rearrange("p (k t) -> p k t", k=KD) for s in range(2)]
        at += 2 * KD * BT
        assert at <= p2_end
        at = p2_end
        wq_sb = words(at, KD * D).rearrange("p (k n) -> p k n", k=KD)
        at += KD * D
        wkv_sb = words(at, KD * 2 * P).rearrange("p (k n) -> p k n", k=KD)
        at += KD * 2 * P
        parts = [words(at + s * 768, 768).bitcast(BF16).rearrange("p (s t) -> p s t", s=3) for s in range(2)]
        at += 2 * 768
        rest = [words(at + s * BT, BT) for s in range(2)]
        at += 2 * BT
        v_blk = [words(at + s * TPB * GROUPS * VW, TPB * GROUPS * VW)
                 .rearrange("p (a g c) -> p a g c", a=TPB, g=GROUPS) for s in range(2)]
        at += 2 * TPB * GROUPS * VW
        at = SHGU0 - (KD * D + 4 * D + D)
        P3_0 = at
        wfc_sb = words(at, KD * D).rearrange("p (k n) -> p k n", k=KD)
        at += KD * D
        a_in = [words(at + s * D, D) for s in range(2)]
        at += 2 * D
        oT = [words(at + s * D, D).rearrange("p (k t) -> p k t", k=KD) for s in range(2)]
        at += 2 * D
        bfc_sb = words(at, D)
        at += D
        assert at == SHGU0
        assert P3_0 >= NE * GU_W

        rows = sb("rows", [P, 8 * D])

        def row(i):
            return rows[:, i * D:(i + 1) * D]

        ident = sb("ident", [P, P])
        tri = sb("tri", [P, P])
        ones = sb("ones", [P, P])
        lower = sb("lower", [P, NE, NE])
        iota_f = sb("iota_f", [P, SLOTS + 1])
        gw_sb = sb("gw_sb", [P, KD, NE])
        zero_row = sb("zero_row", [P, D])
        stats = sb("stats", [P, TPB, 6])
        mv = sb("mv", [P, TPB, 2])
        var_e = sb("var_e", [P, TPB])
        std = sb("std", [P, TPB])
        rs_a = sb("rs_a", [P, TPB])
        rs_b = sb("rs_b", [P, TPB])
        rstd = sb("rstd", [P, TPB])
        attn_u = [row(i).rearrange("p (q n) -> p q n", q=2) for i in range(2)]
        o_raw = [rows[:, 2 * D + s * SEQ:2 * D + (s + 1) * SEQ] for s in range(2)]
        mx = [rows[:, 3 * D + s * 2 * UH:3 * D + (s + 1) * 2 * UH].rearrange("p (h q) -> p h q", h=UH) for s in range(2)]
        o_rec = rows[:, 3 * D + 4 * UH:3 * D + 4 * UH + 2 * HPG].rearrange("p (q h) -> p q h", q=2)
        nm = [rows[0:2 * UH, 4 * D + s * 192:4 * D + (s + 1) * 192].bitcast(BF16)
              .rearrange("p (s t) -> p s t", s=3) for s in range(2)]
        nm_rest = [rows[0:2 * UH, 5 * D + s * P:5 * D + (s + 1) * P] for s in range(2)]
        res_in, x2_sb, xn2_sb = [row(0), row(1)], [row(2), row(3)], [row(4), row(5)]
        lnT = [row(6), row(7)]
        tok_in, xT, mid, late = [row(0), row(1)], [row(2), row(3)], [row(4), row(5)], [row(6), row(7)]
        cmp_a = rows[:, 4 * D:6 * D]
        cmp_b = rows[:, 6 * D:8 * D]
        h_sb = [sb(f"h{i}", [P, F]) for i in range(2)]
        sil = [sb(f"sil{i}", [P, F]) for i in range(2)]
        hT = [sb(f"hT{i}", [P, len(FT), P]) for i in range(2)]
        logits = sb("logits", [P, TILES, NE])
        score = sb("score", [P, TILES, NE])
        wsel = sb("wsel", [P, TILES, NE])
        sel = sb("sel", [P, TILES, NE])
        pos = sb("pos", [P, TILES, NE])
        run_a = sb("run_a", [P, TILES, NE])
        run_b = sb("run_b", [P, TILES, NE])
        t_tile = sb("t_tile", [P, 4, TILES])
        gmax = sb("gmax", [P, TILES, NE // 2])
        grank = sb("grank", [P, TILES, NE // 2])
        cnt = sb("cnt", [P, 6, NE])
        slot_e = sb("slot_e", [P, 2, SLOTS + 1])
        run_c = sb("run_c", [P, TILES])
        tile_cmp = sb("tile_cmp", [P, (SLOTS + 1) * NE])
        w1 = sb("w1", [P, TILES])
        w2 = sb("w2", [P, TILES])
        p1_i = sb("p1_i", [P, TILES], I32)
        p2_i = sb("p2_i", [P, TILES], I32)
        gu_off = sb("gu_off", [P, SLOTS + 1], I32)
        dn_off = sb("dn_off", [P, SLOTS + 1], I32)

        w_kv, w_q, w_fc, w_gate = sem("w_kv"), sem("w_q"), sem("w_fc"), sem("w_gate")
        w_shared, w_routed = sem("w_shared"), sem("w_routed")
        consts = sem("consts")
        zeroed = sem("zeroed")
        step = sem("step")
        pstep = sem("pstep")
        pool_passed, dve_passed = sem("pool_passed"), sem("dve_passed")
        x_ld = [sem(f"x_ld{s}") for s in range(2)]
        c_ld = [sem(f"c_ld{s}") for s in range(2)]
        var_done, std_done, ln_done = sem("var_done"), sem("std_done"), sem("ln_done")
        xT_ready, xT_free = sem("xT_ready"), sem("xT_free")
        kq_ready, v_ready, v_free = sem("kq_ready"), sem("v_ready"), sem("v_free")
        part1, rest_done, part3 = sem("part1"), sem("rest_done"), sem("part3")
        parts_st = [sem(f"parts_st{s}") for s in range(2)]
        v_st_dma = [sem(f"v_st_dma{s}") for s in range(2)]
        st_ld = [sem(f"st_ld{s}") for s in range(4)]
        kones = sem("kones")
        max_ready, max_done, mxt_ready = sem("max_ready"), sem("max_done"), sem("mxt_ready")
        ot_used, ot_ready = sem("ot_used"), sem("ot_ready")
        nm_first, nm_rest_done, nm_done, rec_done = sem("nm_first"), sem("nm_rest_done"), sem("nm_done"), sem("rec_done")
        nm_out = [sem(f"nm_out{s}") for s in range(2)]
        nm_in = [sem(f"nm_in{s}") for s in range(4)]
        st_ready, exp_done, pv_ready, pv_evac = sem("st_ready"), sem("exp_done"), sem("pv_ready"), sem("pv_evac")
        attn_done = sem("attn_done")
        attn_st = [sem(f"attn_st{s}") for s in range(2)]
        a_ld = [sem(f"a_ld{s}") for s in range(2)]
        r_ld = [sem(f"r_ld{s}") for s in range(2)]
        ota_ready, ota_evac, fc_ready, xb_done = sem("ota_ready"), sem("ota_evac"), sem("fc_ready"), sem("xb_done")
        x2_done, var2_done, std2_done, ln2_done = sem("x2_done"), sem("var2_done"), sem("std2_done"), sem("ln2_done")
        lnt_ready, lnt_evac, gate_ready, gate_evac = sem("lnt_ready"), sem("lnt_evac"), sem("gate_ready"), sem("gate_evac")
        x2_stored = [sem(f"x2_stored{s}") for s in range(2)]
        xn2_stored = [sem(f"xn2_stored{s}") for s in range(2)]
        lnt_stored = [sem(f"lnt_stored{s}") for s in range(2)]
        soft_in, soft_exp, sel_done, pre_ready, slots_done, offs_done = (
            sem("soft_in"), sem("soft_exp"), sem("sel_done"), sem("pre_ready"), sem("slots_done"), sem("offs_done"))
        sc_ld = [sem(f"sc_ld{s}") for s in range(2)]
        sc_st = [sem(f"sc_st{s}") for s in range(2)]
        sx_ld = [sem(f"sx_ld{s}") for s in range(2)]
        x2_ld = [sem(f"x2_ld{s}") for s in range(2)]
        base_st = [sem(f"base_st{s}") for s in range(2)]
        g_ready, u_ready, sil_done, h_done = sem("g_ready"), sem("u_ready"), sem("sil_done"), sem("h_done")
        ht_ready, ht_evac, dn_done, y_evac = sem("ht_ready"), sem("ht_evac"), sem("dn_done"), sem("y_evac")
        slot_ld = [sem(f"slot_ld{s}") for s in range(2)]
        xt_ready, xt_evac = sem("xt_ready"), sem("xt_evac")
        y_st = [sem(f"y_st{s}") for s in range(2)]
        cx2_ld = [sem(f"cx2_ld{s}") for s in range(2)]
        gat_ld = [sem(f"gat_ld{s}") for s in range(2)]
        out_done = sem("out_done")
        out_st = [sem(f"out_st{s}") for s in range(2)]

        B0, C0 = PA, PA + PB
        YB0, YC0 = EARLY, EARLY + SLOTS
        GU_BANKS = [(0, 1), (2, 3)]
        Y_BANKS = [4, 5]
        HT_BANK, XT_BANK = 6, 7

        block = ctx.enter_context(nc.Block())

        @block.sync
        def _(sp):
            def load_block(n):
                s = n % 2
                if n >= 2:
                    sp.wait_ge(v_ready, n - 1)
                sp.dma_start(cxT[s], ctxT[n]).then_inc(c_ld[s], 16)
                if n >= 2:
                    sp.wait_ge(xT_ready, TPB * (n - 1))
                sp.dma_start(x_in[s], x_blocks[n]).then_inc(x_ld[s], 16)

            sp.dma_start(wkv_sb, wkvT).then_inc(w_kv, 16)
            load_block(0)
            sp.dma_start(wq_sb, wqT).then_inc(w_q, 16)
            load_block(1)
            def store_parts(n, l):
                sp.wait_ge(part3, KQ * n + l + 1)
                dst = k_parts if l == 0 else q_parts[:, (l - 1) * P:l * P]
                par = (KQ * n + l) % 2
                sp.dma_start(dst[:, :, n * BT:(n + 1) * BT].rearrange("s p t -> p s t"),
                             parts[par]).then_inc(parts_st[par], 16)

            for n in range(BLOCKS):
                if n + 2 < BLOCKS:
                    load_block(n + 2)
                for l in range(KQ):
                    store_parts(n, l)

            for s in range(2):
                sp.wait_ge(parts_st[s], FREE + 16 * BLOCKS * KQ // 2)
                sp.wait_ge(v_st_dma[s], FREE + 16 * BLOCKS // 2)
            sp.wait_ge(kq_ready, KQ * BLOCKS)

            def load_unit(b, half, s):
                for i in range(len(PARTS_Q)):
                    sp.dma_start(
                        q_st[s][HD * i:HD * (i + 1)],
                        q_parts[PARTS_Q[i], half * UH * HD:(half + 1) * UH * HD, bass.ds(b * SEQ, SEQ)]
                        .rearrange("(h d) t -> d h t", d=HD)).then_inc(st_ld[s], 16)
                    sp.dma_start(
                        k_st[s][HD * i:HD * (i + 1)],
                        k_parts[PARTS_K[i], half * UG * HD:(half + 1) * UG * HD, bass.ds(b * SEQ, SEQ)]
                        .rearrange("(g d) t -> d g t", d=HD)).then_inc(st_ld[s], 16)
                for kt in range(2):
                    sp.dma_start(v_st[s][:, kt, :, :].rearrange("p g c -> p (g c)"),
                                 v_dram[bass.ds(b * 2 + kt, 1), :, half * UG * VW:(half + 1) * UG * VW]
                                 .rearrange("o p c -> (o p) c")).then_inc(st_ld[s], 16)

            def neg_max_rows(v, s, par, n):
                sp.wait_ge(nm_out[par], 16 * (n + 1))
                sp.dma_start(q_st[s][STACK:ROWS].rearrange("p h t -> p (h t)"),
                             neg_max[bass.ds(v, 1)].rearrange("o s r c -> (o s) (r c)")).then_inc(nm_in[s], 16)

            def store_attn(u, b, half, n):
                sp.wait_ge(attn_done, UG * (u + 1))
                sp.dma_start(attn_dram[bass.ds(b, 1), :, :, half * UG * HPG * HD:(half + 1) * UG * HPG * HD]
                             .rearrange("o q p c -> p (o q) c"), attn_u[half]).then_inc(attn_st[half], 16)

            for u in range(4):
                load_unit(u // 2, u % 2, u % 4)
            sp.dma_start(wfc_sb, wfcT).then_inc(w_fc, 16)
            sp.dma_start(bfc_sb, bfc.partition_broadcast(P)).then_inc(w_fc, 16)
            sp.dma_start(gw_sb[:], gwT).then_inc(w_gate, 16)
            for v in range(3):
                neg_max_rows(v, v % 4, v % 2, v // 2)
            for e in range(NE, NE + SH):
                gu, dn = SHGU0 + (e - NE) * GU_W, SHDN0 + (e - NE) * DN_W
                sp.dma_start(words(gu, GU_W), wgu[e]).then_inc(w_shared, 16)
                sp.dma_start(words(dn, 2 * D), wdn[e]).then_inc(w_shared, 16)
                sp.dma_start(words(dn + 2 * D, D)[0:FT[2][1]], wdt[e]).then_inc(w_shared, 16)
            with sp.Fori(0, 3) as i:
                sp.dma_start(slot_x_tiles[bass.ds(i * (SLOTS // 3), SLOTS // 3)].rearrange("t p d -> p t d"),
                             zero_row[:].unsqueeze(1).broadcast_to([P, SLOTS // 3, D])).then_inc(zeroed, 16)
                for r in range(4):
                    u = i * 4 + (1 + r)
                    sp.wait_ge(pv_ready, u * UG)
                    load_unit(i * 2 + (4 + r) // 2, r % 2, r % 4)
                    store_attn(i * 4 + r, i * 2 + r // 2, r % 2, None)
                    neg_max_rows(i * 4 + (3 + r), (3 + r) % 4, (3 + r) % 2, i * 2 + (3 + r) // 2)
            for u in range(12, 16):
                store_attn(u, u // 2, u % 2, None)
                if u == 12:
                    neg_max_rows(15, 3, 1, 7)

            for s in range(2):
                sp.wait_ge(attn_st[s], FREE + 16 * BATCH)

            def load_attn(b, s):
                sp.dma_start(a_in[s], attn_dram[bass.ds(b, 1), s].rearrange("o p d -> (o p) d")).then_inc(a_ld[s], 16)

            def load_res_rows(b, s):
                sp.dma_start(res_in[s], x_tiles[bass.ds(b * 2 + s, 1)].rearrange("o p d -> (o p) d")).then_inc(r_ld[s], 16)

            def load_gate_up(e, s):
                half = GU_W // 2
                sp.dma_start(weights[:, bass.ds(e * GU_W + (GU0 + s * half), half)],
                             wgu[bass.ds(e, 1), :, s * half:(s + 1) * half].rearrange("o p n -> (o p) n")
                             ).then_inc(w_routed, 16)

            def tile_of(dram_tiles, t):
                return dram_tiles[bass.ds(t, 1)].rearrange("o p d -> (o p) d")

            def store_lnT(t, s):
                sp.wait_ge(lnt_evac, t + 1)
                sp.dma_start(tile_of(xnT_dram, t), lnT[s]).then_inc(lnt_stored[s], 16)

            def store_x2(t, s):
                sp.wait_ge(x2_done, t + 1)
                sp.dma_start(tile_of(x2_dram, t), x2_sb[s]).then_inc(x2_stored[s], 16)

            def store_xn2(t, s):
                sp.wait_ge(ln2_done, t + 1)
                sp.dma_start(tile_of(xn2_dram, t), xn2_sb[s]).then_inc(xn2_stored[s], 16)

            for s in range(2):
                load_attn(0, s)
                load_res_rows(0, s)
            sp.wait_ge(ota_ready, 1)
            load_attn(1, 0)
            for t in range(2):
                sp.wait_ge(ota_ready, t + 2)
                load_attn((t + 3) // 2, (t + 3) % 2)
                store_x2(t, t)
                load_res_rows(1, t)
                load_gate_up(0, t)
                store_xn2(t, t)

            def token_tile(i, s, more=True):
                if more:
                    sp.wait_ge(ota_ready, i * 2 + (s + 2))
                    load_attn(i + (1 + s), 1 - s)
                store_lnT(i * 2 + s - 2, s)
                store_x2(i * 2 + s, s)
                load_res_rows(i + 1, s)
                load_gate_up(i, s)
                store_xn2(i * 2 + s, s)

            LAST_PAIR = TILES // 2 - 2
            with sp.Fori(1, LAST_PAIR) as i:
                token_tile(i, 0)
                token_tile(i, 1)
            token_tile(LAST_PAIR, 0)
            token_tile(LAST_PAIR, 1, more=False)
            for t in range(TILES - 2, TILES):
                store_lnT(t - 2, t % 2)
                store_x2(t, t % 2)
                load_gate_up(NE - 1, t % 2)
                store_xn2(t, t % 2)
            for t in range(TILES - 2, TILES):
                store_lnT(t, t % 2)

            for s in range(2):
                sp.wait_ge(lnt_stored[s], FREE + 16 * TILES // 2)
                sp.wait_ge(x2_stored[s], FREE + 16 * TILES // 2)
                sp.wait_ge(xn2_stored[s], FREE + 16 * TILES // 2)

            def load_shared(t, s):
                sp.dma_start(xT[s], tile_of(xnT_dram, t)).then_inc(sx_ld[s], 16)
                sp.dma_start(tok_in[s], tile_of(x2_dram, t)).then_inc(x2_ld[s], 16)

            def store_base(t, s):
                sp.wait_ge(y_evac, t + 1)
                sp.dma_start(tile_of(x2_dram, t), tok_in[s]).then_inc(base_st[s], 16)

            def load_scatter(t):
                s = t % 2
                if t == 0:
                    sp.wait_ge(slots_done, 1)
                if t >= 2:
                    sp.wait_ge(sc_st[s], 32 * (t // 2))
                sp.dma_start(mid[s], xn2_dram[t]).then_inc(sc_ld[s], 16)

            def load_down(e):
                dn = DN0 + e * DN_W
                sp.dma_start(words(dn, 2 * D), wdn[e]).then_inc(w_routed, 16)
                sp.dma_start(words(dn + 2 * D, D)[0:FT[2][1]], wdt[e]).then_inc(w_routed, 16)

            def load_slots(n, s):
                sp.dma_start(tok_in[s], tile_of(slot_x_tiles, n)).then_inc(slot_ld[s], 16)

            load_shared(0, 0)
            load_shared(1, 1)
            for t in range(EARLY):
                load_scatter(2 * t)
                load_scatter(2 * t + 1)
                load_down(t)
                if t == EARLY - 1:
                    sp.wait_ge(base_st[0], 16 * EARLY // 2)
                    for s in range(2):
                        sp.wait_ge(sc_st[s], 32 * TILES // 2)
                    load_slots(0, 0)
                store_base(t, t % 2)
                if t + 2 < EARLY:
                    sp.wait_ge(base_st[t % 2], 16 * (t // 2 + 1))
                    load_shared(t + 2, t % 2)

            def store_slots(n, s):
                sp.wait_ge(y_evac, YB0 + 1 + n)
                sp.dma_start(tile_of(slot_y_tiles, n), mid[s]).then_inc(y_st[s], 16)

            sp.wait_ge(base_st[1], 16 * EARLY // 2)
            load_slots(1, 1)
            sp.wait_ge(xt_ready, 1)
            load_slots(2, 0)
            with sp.Fori(0, (SLOTS - 3) // 2) as i:
                for s in range(2):
                    sp.wait_ge(xt_ready, i * 2 + (s + 2))
                    load_slots(i * 2 + (s + 3), 1 - s)
                    store_slots(i * 2 + s, s)
            for n in range(SLOTS - 3, SLOTS - 1):
                store_slots(n, n % 2)

            def load_late(m, s):
                sp.dma_start(xT[s], tile_of(xnT_dram, m + EARLY)).then_inc(sx_ld[s], 16)

            def load_res(t, s):
                sp.dma_start(tok_in[s], tile_of(x2_dram, t)).then_inc(cx2_ld[s], 16)

            def store_out(t, q, s):
                sp.wait_ge(out_done, q + 1)
                sp.dma_start(tile_of(out_tiles, t), late[s]).then_inc(out_st[s], 16)

            sp.wait_ge(u_ready, C0 - 1)
            load_late(0, 1)
            sp.wait_ge(u_ready, C0)
            load_late(1, 0)
            store_slots(SLOTS - 1, (SLOTS - 1) % 2)
            load_res(0, 0)
            load_res(EARLY, 1)
            with sp.Fori(0, EARLY // 2 - 1) as i:
                for r in range(2):
                    for s in range(2):
                        store_out(i * 2 + (r + s * EARLY), i * 4 + (2 * r + s), s)
                        load_res(i * 2 + (r + 1 + s * EARLY), s)
                    load_late(i * 2 + (r + 2), 1 - r)
            for m in range(EARLY - 2, EARLY):
                for s in range(2):
                    store_out(m + s * EARLY, 2 * m + s, s)
                    if m + 1 < EARLY:
                        load_res(m + 1 + s * EARLY, s)
            for s in range(2):
                sp.wait_ge(out_st[s], 16 * EARLY)

        @block.gpsimd
        def _(pool):
            def select(out_, pattern, op, base_, mult_):
                nc.gpsimd.affine_select(out=out_, in_=out_, compare_op=op, fill=0.0, base=base_,
                                        pattern=pattern, channel_multiplier=mult_).then_inc(pstep, 1)

            nc.gpsimd.memset(zero_row[:], 0.0).then_inc(consts, 1)
            for s in range(2):
                nc.gpsimd.memset(v_blk[s], 0.0)
            nc.gpsimd.memset(ident[:], 1.0)
            nc.gpsimd.memset(tri[:], 1.0)
            nc.gpsimd.memset(lower[:], 1.0)
            nc.gpsimd.memset(ones[:], 1.0).then_inc(pstep, 1)
            pool.wait_ge(pstep, 1)
            for s in range(2):
                nc.gpsimd.memset(v_blk[s][:, :, :, HD:HD + 1], 1.0).then_inc(pstep, 1)
            select(ident[:], [[-1, P]], ALU.is_equal, 0, 1)
            select(tri[:], [[1, P]], ALU.is_gt, 0, -1)
            select(lower[:], [[1, NE], [-1, NE]], ALU.is_gt, 0, 0)
            nc.gpsimd.iota(iota_f[:], [[1, SLOTS + 1]], base=0, channel_multiplier=0,
                           allow_small_or_imprecise_dtypes=True).then_inc(pstep, 1)
            pool.wait_ge(pstep, 7)
            nc.gpsimd.engine_nop().then_inc(consts, 1)

            def cut(n, i, s, l):
                par = (KQ * s + l) % 2
                pool.wait_ge(rest_done, KQ * n + (KQ + l + 1))
                pool.sem_inc(pool_passed, 1)
                nc.gpsimd.tensor_copy(parts[par][:, 1, :], rest[par]).then_inc(pstep, 1)
                pool.wait_ge(pstep, KQ * n + (7 + l + 1))
                nc.gpsimd.tensor_tensor(parts[par][:, 2, :], rest[par], parts[par][:, 1, :],
                                        ALU.subtract).then_inc(part3, 1)

            with pool.Fori(0, BLOCKS // 2) as i:
                for s in range(2):
                    for l in range(KQ):
                        cut(i * 2 + s, i, s, l)

            pool.wait_ge(part3, KQ * BLOCKS)
            for s in range(4):
                nc.gpsimd.memset(k_st[s][STACK:ROWS], 1.0).then_inc(kones, 1)
            pstep0 = 7 + KQ * BLOCKS

            def cut_max(v, par):
                pool.wait_ge(nm_rest_done, v + 1)
                pool.sem_inc(pool_passed, 1)
                nc.gpsimd.tensor_copy(nm[par][:, 1, :], nm_rest[par]).then_inc(pstep, 1)
                pool.wait_ge(pstep, v + (pstep0 + 1))
                nc.gpsimd.tensor_tensor(nm[par][:, 2, :], nm_rest[par], nm[par][:, 1, :],
                                        ALU.subtract).then_inc(nm_done, 1)
                pool.wait_ge(nm_done, v + 1)
                pool.sem_inc(pool_passed, 1)
                nc.gpsimd.dma_start(neg_max[bass.ds(v, 1)].rearrange("o s r c -> r (o s) c"),
                                    nm[par]).then_inc(nm_out[par], 16)

            with pool.Fori(0, UNITS // 2) as i:
                for s in range(2):
                    cut_max(i * 2 + s, s)

            pool.wait_ge(w_fc, 32)
            with pool.Fori(0, TILES // 2) as i:
                for s in range(2):
                    pool.wait_ge(r_ld[s], i * 16 + 16)
                    nc.gpsimd.tensor_tensor(res_in[s], res_in[s], bfc_sb, ALU.add).then_inc(xb_done, 1)

            pool.wait_ge(slots_done, 1)
            pool.wait_ge(zeroed, 3 * 16)
            for t in range(TILES):
                s = t % 2
                pool.wait_ge(sc_ld[s], 16 * (t // 2 + 1))
                for idx in (p1_i, p2_i):
                    nc.gpsimd.indirect_dma_start(
                        out=slot_x, out_offset=bass.IndirectOffsetOnAxis(ap=idx[:, t:t + 1], axis=0),
                        in_=mid[s], in_offset=None).then_inc(sc_st[s], 16)

            for s in range(2):
                pool.wait_ge(y_st[s], FREE + 16 * ((SLOTS + 1 - s) // 2))
            for q in range(2 * EARLY):
                s = q % 2
                t = q // 2 + s * EARLY
                if q >= 2:
                    pool.wait_ge(out_st[s], 16 * (q // 2))
                for buf, idx in ((mid[s], p1_i), (late[s], p2_i)):
                    nc.gpsimd.indirect_dma_start(
                        out=buf, out_offset=None, in_=slot_y,
                        in_offset=bass.IndirectOffsetOnAxis(ap=idx[:, t:t + 1], axis=0)).then_inc(gat_ld[s], 16)

        @block.scalar
        def _(act):
            for stored in parts_st + v_st_dma + lnt_stored:
                act.sem_inc(stored, FREE)
            act.wait_ge(consts, 2)

            def cut_first(n, i, s, l):
                par, uses = (KQ * s + l) % 2, (KQ * s + l) // 2
                act.wait_ge(kq_ready, KQ * n + (l + 1))
                act.wait_ge(parts_st[par], i * (16 * KQ) + (FREE + 16 * uses))
                nc.scalar.copy(parts[par][:, 0, :], bank[l][:]).then_inc(part1, 1)

            with act.Fori(0, BLOCKS // 2) as i:
                for s in range(2):
                    n = i * 2 + s
                    act.wait_ge(var_done, n + 1)
                    nc.scalar.activation(std[:], var_e[:], ACT.Sqrt).then_inc(std_done, 1)
                    cut_first(n, i, s, 0)
                    act.wait_ge(v_ready, n + 1)
                    act.wait_ge(v_st_dma[s], i * 16 + FREE)
                    nc.scalar.copy(v_blk[s][:, :, :, 0:HD],
                                   bank[5][:].rearrange("p (a g c) -> p a g c", a=TPB, g=GROUPS)).then_inc(v_free, 1)
                    for a in range(TPB):
                        act.wait_ge(xT_ready, n * TPB + (a + 1))
                        nc.scalar.copy(xnT[s][:, :, a * P:(a + 1) * P],
                                       bank[6 + a % 2][:].rearrange("p (k t) -> p k t", k=KD)).then_inc(xT_free, 1)
                    act.wait_ge(v_free, n + 2)
                    act.dma_start(v_blocks[bass.ds(n, 1)].rearrange("o p a c -> (o p) a c"),
                                  v_blk[s].rearrange("p a g c -> p a (g c)")).then_inc(v_st_dma[s], 16)
                    for l in range(1, KQ):
                        cut_first(n, i, s, l)

            def attn_act(G, fill_G=True, first=False, evac=True, par=0):
                if fill_G:
                    for f in range(FILLS):
                        kt, pair = f // 2, f % 2
                        act.wait_ge(st_ready, G * FILLS + (f + 1))
                        if f == 0 and not first:
                            act.wait_ge(pv_ready, G - 1)
                        nc.scalar.activation(probs[par][:, kt, pair * 512:(pair + 1) * 512], bank[2 + f][:], ACT.Exp,
                                             scale=SCALE).then_inc(exp_done, 1)
                if evac:
                    act.wait_ge(pv_ready, G)
                    if not first:
                        act.wait_ge(ot_ready, G - 2)
                    nc.scalar.copy(o_raw[1 - par], bank[6][:, 0:SEQ]).then_inc(pv_evac, 1)

            for G in range(UG):
                attn_act(G, first=(G < 3), evac=(G > 0), par=G % 2)
            with act.Fori(0, 3) as i:
                for r in range(4 * UG):
                    attn_act(i * (4 * UG) + (UG + r), par=r % 2)
            with act.Fori(0, 3) as i:
                for j in range(UG):
                    attn_act(i * UG + (13 * UG + j), par=j % 2)
            attn_act(UNITS * UG, fill_G=False, par=0)

            def ot_evac(t, s):
                act.wait_ge(ota_ready, t + 1)
                nc.scalar.copy(oT[s], bank[s][:].rearrange("p (k t) -> p k t", k=KD)).then_inc(ota_evac, 1)

            def lnt_out(t, s, stored):
                act.wait_ge(lnt_ready, t + 1)
                act.wait_ge(lnt_stored[s], stored * 16 + FREE)
                nc.scalar.copy(lnT[s], bank[4 + s][:]).then_inc(lnt_evac, 1)

            def gate_out(t, s):
                act.wait_ge(gate_ready, t + 1)
                nc.scalar.copy(logits[:, bass.ds(t, 1), :], bank[6 + s][:, 0:NE].unsqueeze(1)).then_inc(gate_evac, 1)

            def std2(t):
                act.wait_ge(var2_done, t + 1)
                nc.scalar.activation(std[:, 0:1], var_e[:, 0:1], ACT.Sqrt).then_inc(std2_done, 1)

            ot_evac(0, 0)
            for t in range(2):
                ot_evac(t + 1, (t + 1) % 2)
                std2(t)
            with act.Fori(1, TILES // 2 - 1) as i:
                for s in range(2):
                    lnt_out(i * 2 + s - 2, s, i - 1)
                    ot_evac(i * 2 + (s + 1), 1 - s)
                    std2(i * 2 + s)
                    gate_out(i * 2 + s - 2, s)
            for t in range(TILES - 2, TILES):
                lnt_out(t - 2, t % 2, t // 2 - 1)
                if t + 1 < TILES:
                    ot_evac(t + 1, (t + 1) % 2)
                std2(t)
                gate_out(t - 2, t % 2)
            for t in range(TILES - 2, TILES):
                lnt_out(t, t % 2, t // 2)
                gate_out(t, t % 2)

            act.wait_ge(soft_in, 1)
            nc.scalar.activation(score[:], score[:], ACT.Exp).then_inc(soft_exp, 1)

            def silu(w, par):
                act.wait_ge(g_ready, w + 1)
                if not (isinstance(w, int) and w < 2):
                    act.wait_ge(h_done, w - 1)
                nc.scalar.activation(sil[par][:], bank[GU_BANKS[par][0]][:, 0:F], ACT.Silu).then_inc(sil_done, 1)

            def ht_out(w, par):
                act.wait_ge(ht_ready, w + 1)
                if not (isinstance(w, int) and w < 2):
                    act.wait_ge(dn_done, w - 1)
                nc.scalar.copy(hT[par][:, 0:2, :], bank[HT_BANK][:, 0:2 * P].rearrange("p (j t) -> p j t", j=2))
                nc.scalar.copy(hT[par][0:FT[2][1], 2, :], bank[HT_BANK][0:FT[2][1], 2 * P:3 * P]).then_inc(ht_evac, 1)

            silu(0, 0)
            silu(1, 1)
            ht_out(0, 0)
            silu(2, 0)
            ht_out(1, 1)
            TOTAL = PA + PB + PC
            with act.Fori(1, (TOTAL - 1) // 2) as i:
                for par in range(2):
                    silu(i * 2 + (par + 1), 1 - par)
                    ht_out(i * 2 + par, par)
            assert TOTAL % 2 == 1
            ht_out(TOTAL - 1, 0)

        @block.tensor
        def _(pe):
            pe.wait_ge(consts, 2)
            pe.wait_ge(w_kv, 16)

            def project(l, n, lhs, rhs_):
                if not (isinstance(n, int) and n == 0):
                    pe.wait_ge(rest_done, n * KQ + (l + 1))
                for k in range(KD):
                    mm = nc.tensor.matmul(bank[l][:], lhs(k), rhs_[:, k, :], start=(k == 0), stop=(k == KD - 1))
                mm.then_inc(kq_ready, 1)

            with pe.Fori(0, BLOCKS // 2) as i:
                for s in range(2):
                    n = i * 2 + s
                    pe.wait_ge(c_ld[s], i * 16 + 16)
                    project(0, n, lambda k: wkv_sb[:, k, 0:P], cxT[s])
                    pe.wait_ge(v_free, n + 1)
                    for a in range(TPB):
                        for k in range(KD):
                            mm = nc.tensor.matmul(bank[5][:, a * P:(a + 1) * P], cxT[s][:, k, a * P:(a + 1) * P],
                                                  wkv_sb[:, k, P:2 * P], start=(k == 0), stop=(k == KD - 1))
                    mm.then_inc(v_ready, 1)
                    for a in range(TPB):
                        pe.wait_ge(ln_done, n * TPB + (a + 1))
                        pe.wait_ge(xT_free, n * TPB + (a + 1))
                        for k in range(KD):
                            tr = nc.tensor.transpose(bank[6 + a % 2][:, k * P:(k + 1) * P],
                                                     x_in[s][:, a, k * P:(k + 1) * P], ident[:])
                        tr.then_inc(xT_ready, 1)
                    pe.wait_ge(w_q, 16)
                    pe.wait_ge(xT_free, n * TPB + (2 + TPB))
                    for m in range(KD):
                        project(1 + m, n, lambda k: wq_sb[:, k, m * P:(m + 1) * P], xnT[s])

            pe.wait_ge(rest_done, KQ * (BLOCKS + 1))
            pe.wait_ge(xT_free, TILES + 2)
            pe.wait_ge(v_free, BLOCKS + 1)
            pe.wait_ge(kones, 4)

            def max_fill(v, s, j, f, first=False):
                qt, pair = f // 2, f % 2
                if not (first and j == 0 and f < 2):
                    pe.wait_ge(max_done, v * (FILLS * UG) + (FILLS * j + f - 1))
                for c in range(2):
                    mm = nc.tensor.matmul(bank[f % 2][:, c * SEQ:(c + 1) * SEQ],
                                          q_st[s][0:STACK, HPG * j + 2 * pair + c, qt * P:(qt + 1) * P],
                                          k_st[s][0:STACK, j, :], start=True, stop=True)
                mm.then_inc(max_ready, 1)

            def max_transpose(v, par, uses):
                pe.wait_ge(max_done, v * (FILLS * UG) + FILLS * UG)
                pe.wait_ge(ot_used, uses)
                nc.tensor.transpose(bank[7][0:2 * UH, 0:P], mx[par].rearrange("p h q -> p (h q)"),
                                    ident[:]).then_inc(mxt_ready, 1)

            def score_fill(G, s, j, f, first=False):
                kt, pair = f // 2, f % 2
                if not first:
                    pe.wait_ge(exp_done, G * FILLS + (f + 1 - FILLS))
                nc.tensor.matmul(bank[2 + f][:], k_st[s][0:ROWS, j, kt * P:(kt + 1) * P],
                                 q_st[s][0:ROWS, HPG * j + 2 * pair:HPG * j + 2 * pair + 2, :]
                                 .rearrange("p h t -> p (h t)"), start=True, stop=True).then_inc(st_ready, 1)

            def pv_part(G, s, j, f):
                kt = f // 2
                if f == 0:
                    pe.wait_ge(exp_done, G * FILLS + FILLS)
                    pe.wait_ge(pv_evac, G)
                for c in (2 * (f % 2), 2 * (f % 2) + 1):
                    mm = nc.tensor.matmul(bank[6][VW * c:VW * (c + 1), 0:SEQ], v_st[s][:, kt, j, :],
                                          probs[j % 2][:, kt, c * SEQ:(c + 1) * SEQ],
                                          start=(kt == 0), stop=(kt == 1), tile_position=(0, VW * c))
                if f == FILLS - 1:
                    mm.then_inc(pv_ready, 1)

            def attn_transpose(G, par, uses):
                pe.wait_ge(pv_evac, G + 1)
                pe.wait_ge(ot_used, uses)
                for qt in range(2):
                    tr = nc.tensor.transpose(bank[7][:, qt * P:(qt + 1) * P], o_raw[par][:, qt * P:(qt + 1) * P],
                                             ident[:])
                tr.then_inc(ot_ready, 1)

            def unit_ready(v, s, n):
                pe.wait_ge(st_ld[s], (n + 1) * (16 * (2 * len(PARTS_Q) + 2)))

            def attn_step(u, s, n, has_max=True, first=False, uses0=None):
                sv = (s + 2) % 4
                uses0 = u * 5 if uses0 is None else uses0
                if has_max:
                    unit_ready(u + 2, sv, n + (s + 2) // 4)
                pe.wait_ge(nm_in[s], (n + 1) * 16)
                for j in range(UG):
                    G = u * UG + j
                    for f in range(FILLS):
                        if has_max:
                            max_fill(u + 2, sv, j, f)
                        score_fill(G, s, j, f, first=(first and j == 0))
                        if j > 0:
                            pv_part(G - 1, s, j - 1, f)
                        elif not first:
                            pv_part(G - 1, (s - 1) % 4, UG - 1, f)
                        if f == 2 and not (first and j < 2):
                            attn_transpose(G - 2, j % 2, uses0 + j)
                if has_max:
                    max_transpose(u + 2, s % 2, uses0 + 4)

            for v in range(2):
                unit_ready(v, v, 0)
                for j in range(UG):
                    for f in range(FILLS):
                        max_fill(v, v, j, f, first=(v == 0))
                max_transpose(v, v, v)
            attn_step(0, 0, 0, first=True)
            with pe.Fori(0, 3) as i:
                for r in range(4):
                    attn_step(i * 4 + (1 + r), (1 + r) % 4, i + (1 + r) // 4)
            attn_step(13, 1, 3)
            attn_step(14, 2, 3, has_max=False)
            attn_step(15, 3, 3, has_max=False, uses0=74)
            LAST = UNITS * UG - 1
            for f in range(FILLS):
                pv_part(LAST, 3, UG - 1, f)
            attn_transpose(LAST - 1, 0, LAST - 1 + UNITS)
            attn_transpose(LAST, 1, LAST + UNITS)

            pe.wait_ge(ot_used, LAST + 1 + UNITS)
            pe.wait_ge(w_fc, 16)
            pe.wait_ge(w_gate, 16)

            def ot_transpose(t, s, n):
                pe.wait_ge(a_ld[s], n * 16 + 16)
                if not (isinstance(t, int) and t < 2):
                    pe.wait_ge(ota_evac, t - 1)
                for k in range(KD):
                    tr = nc.tensor.transpose(bank[s][:, k * P:(k + 1) * P], a_in[s][:, k * P:(k + 1) * P], ident[:])
                tr.then_inc(ota_ready, 1)

            def out_project(t, s):
                pe.wait_ge(ota_evac, t + 1)
                if not (isinstance(t, int) and t < 2):
                    pe.wait_ge(x2_done, t - 1)
                for k in range(KD):
                    mm = nc.tensor.matmul(bank[2 + s][:], oT[s][:, k, :], wfc_sb[:, k, :],
                                          start=(k == 0), stop=(k == KD - 1))
                mm.then_inc(fc_ready, 1)

            def ln_transpose(t, s):
                pe.wait_ge(ln2_done, t + 1)
                if not (isinstance(t, int) and t < 2):
                    pe.wait_ge(lnt_evac, t - 1)
                for k in range(KD):
                    tr = nc.tensor.transpose(bank[4 + s][:, k * P:(k + 1) * P], xn2_sb[s][:, k * P:(k + 1) * P],
                                             ident[:])
                tr.then_inc(lnt_ready, 1)

            def gate(t, s):
                pe.wait_ge(lnt_evac, t + 1)
                if not (isinstance(t, int) and t < 2):
                    pe.wait_ge(gate_evac, t - 1)
                for k in range(KD):
                    mm = nc.tensor.matmul(bank[6 + s][:, 0:NE], lnT[s][:, k * P:(k + 1) * P], gw_sb[:, k, :],
                                          start=(k == 0), stop=(k == KD - 1))
                mm.then_inc(gate_ready, 1)

            ot_transpose(0, 0, 0)
            for t in range(2):
                ot_transpose(t + 1, (t + 1) % 2, (t + 1) // 2)
                out_project(t, t)
            for t in range(2, 4):
                ln_transpose(t - 2, t % 2)
                ot_transpose(t + 1, (t + 1) % 2, (t + 1) // 2)
                out_project(t, t % 2)
                gate(t - 2, t % 2)
            with pe.Fori(2, TILES // 2 - 1) as i:
                for s in range(2):
                    ln_transpose(i * 2 + s - 2, s)
                    ot_transpose(i * 2 + (s + 1), 1 - s, i + (s + 1) // 2)
                    out_project(i * 2 + s, s)
                    gate(i * 2 + s - 2, s)
            for t in range(TILES - 2, TILES):
                ln_transpose(t - 2, t % 2)
                if t + 1 < TILES:
                    ot_transpose(t + 1, (t + 1) % 2, (t + 1) // 2)
                out_project(t, t % 2)
                gate(t - 2, t % 2)
            for t in range(TILES - 2, TILES):
                ln_transpose(t, t % 2)
                gate(t, t % 2)

            pe.wait_ge(gate_evac, TILES)
            pe.wait_ge(x2_done, TILES)
            pe.wait_ge(w_shared, 16 * 3 * SH)

            def gate_up(w, par, x_T, gu):
                if not (isinstance(w, int) and w < 2):
                    pe.wait_ge(h_done, w - 1)
                for which, ready in ((0, g_ready), (1, u_ready)):
                    for k in range(KD):
                        mm = nc.tensor.matmul(bank[GU_BANKS[par][which]][:, 0:F], x_T[:, k * P:(k + 1) * P],
                                              gu(k, which), start=(k == 0), stop=(k == KD - 1))
                    mm.then_inc(ready, 1)

            def down(w, par, n, ypar, dn, begin=True, end=True):
                pe.wait_ge(h_done, w + 1)
                pe.wait_ge(ht_evac, w)
                for j, (f0, fs) in enumerate(FT):
                    tr = nc.tensor.transpose(bank[HT_BANK][0:fs, j * P:(j + 1) * P], h_sb[par][:, f0:f0 + fs], ident[:])
                tr.then_inc(ht_ready, 1)
                pe.wait_ge(ht_evac, w + 1)
                if begin and not (isinstance(n, int) and n < 2):
                    pe.wait_ge(y_evac, n - 1)
                for j, (f0, fs) in enumerate(FT):
                    mm = nc.tensor.matmul(bank[Y_BANKS[ypar]][:], hT[par][0:fs, j, :], dn(j, fs),
                                          start=(begin and j == 0), stop=(end and j == len(FT) - 1))
                mm.then_inc(dn_done, 1)

            def shared_gu(c):
                return lambda k, which: words(SHGU0 + c * GU_W + (2 * k + which) * F, F)

            def shared_dn(c):
                return lambda j, fs: words(SHDN0 + c * DN_W + j * D, D)[0:fs]

            def routed_gu(m):
                off = pe.value_load(gu_off[0:1, bass.ds(m, 1)], min_val=0, max_val=(NE - 1) * GU_W)
                return lambda k, which: weights[:, bass.ds(off + (GU0 + (2 * k + which) * F), F)]

            def routed_dn(m):
                off = pe.value_load(dn_off[0:1, bass.ds(m, 1)], min_val=0, max_val=(NE - 1) * DN_W)
                return lambda j, fs: weights[0:fs, bass.ds(off + (DN0 + j * D), D)]

            def early_up(t, s, n, c):
                if c == 0:
                    pe.wait_ge(sx_ld[s], n * 16 + 16)
                gate_up(t * 2 + c, c, xT[s], shared_gu(c))

            def early_down(t, s, c):
                down(t * 2 + c, c, t, s, shared_dn(c), begin=(c == 0), end=(c == 1))

            early_up(0, 0, 0, 0)
            early_up(0, 0, 0, 1)
            early_down(0, 0, 0)
            pe.wait_ge(sel_done, 1)
            flat = sel[:].rearrange("p t e -> p (t e)")
            nc.tensor.matmul(bank[XT_BANK][:, 0:P], tri[:], flat, start=True, stop=True)
            nc.tensor.matmul(bank[XT_BANK][:, P:2 * P], ones[:], flat, start=True, stop=True).then_inc(pre_ready, 1)
            early_up(1, 1, 0, 0)
            early_down(0, 0, 1)
            early_up(1, 1, 0, 1)
            early_down(1, 1, 0)
            with pe.Fori(1, EARLY // 2) as i:
                for s in range(2):
                    early_up(i * 2 + s, s, i, 0)
                    early_down(i * 2 + s - 1, 1 - s, 1)
                    early_up(i * 2 + s, s, i, 1)
                    early_down(i * 2 + s, s, 0)

            pe.wait_ge(offs_done, 1)
            pe.wait_ge(w_routed, 16 * 4 * NE)

            def slot_transpose(m, s, n):
                pe.wait_ge(slot_ld[s], n * 16 + 16)
                if not (isinstance(m, int) and m == 0):
                    pe.wait_ge(xt_evac, m)
                for k in range(KD):
                    tr = nc.tensor.transpose(bank[XT_BANK][:, k * P:(k + 1) * P], tok_in[s][:, k * P:(k + 1) * P],
                                             ident[:])
                tr.then_inc(xt_ready, 1)

            def slot_up(m, s):
                pe.wait_ge(xt_evac, m + 1)
                gate_up(m + B0, s, xT[s], routed_gu(m))

            def slot_down(m, s):
                down(m + B0, s, m + YB0, (YB0 + s) % 2, routed_dn(m))

            pe.wait_ge(slots_done, 1)
            slot_transpose(0, 0, 0)
            slot_up(0, 0)
            early_down(EARLY - 1, (EARLY - 1) % 2, 1)
            slot_transpose(1, 1, 0)
            with pe.Fori(0, (SLOTS - 3) // 2) as i:
                for r in range(2):
                    m = i * 2 + (1 + r)
                    slot_transpose(m + 1, r, i + 1)
                    slot_up(m, 1 - r)
                    slot_down(m - 1, r)
            m = SLOTS - 2
            slot_transpose(m + 1, (m + 1) % 2, (m + 1) // 2)
            slot_up(m, m % 2)
            slot_down(m - 1, (m - 1) % 2)
            slot_up(m + 1, (m + 1) % 2)
            slot_down(m, m % 2)

            def late_up(m, s, n, c):
                if c == 0:
                    pe.wait_ge(sx_ld[s], n * 16 + (16 * EARLY // 2 + 16))
                gate_up(m * 2 + (C0 + c), (C0 + c) % 2, xT[s], shared_gu(c))

            def late_down(m, s, c):
                down(m * 2 + (C0 + c), (C0 + c) % 2, m + YC0, s, shared_dn(c), begin=(c == 0), end=(c == 1))

            late_up(0, 1, 0, 0)
            slot_down(SLOTS - 1, (SLOTS - 1) % 2)
            late_up(0, 1, 0, 1)
            late_down(0, YC0 % 2, 0)
            late_up(1, 0, 0, 0)
            late_down(0, YC0 % 2, 1)
            late_up(1, 0, 0, 1)
            late_down(1, (YC0 + 1) % 2, 0)
            with pe.Fori(1, (TILES - EARLY) // 2) as i:
                for r in range(2):
                    m = i * 2 + r
                    late_up(m, (r + 1) % 2, i, 0)
                    late_down(m - 1, (YC0 + r + 1) % 2, 1)
                    late_up(m, (r + 1) % 2, i, 1)
                    late_down(m, (YC0 + r) % 2, 0)
            late_down(TILES - EARLY - 1, (YC0 + TILES - EARLY - 1) % 2, 1)

        @block.vector
        def _(dve):
            def chain(start):
                count = [0]

                def link(ins, relay=False):
                    count[0] += 1
                    ins.then_inc(step, 1)
                    dve.wait_ge(step, start + count[0])
                    if relay:
                        dve.sem_inc(dve_passed, 1)
                link.count = count
                return link

            def newton(link, n):
                v, sd, a, b, r = var_e[:, 0:n], std[:, 0:n], rs_a[:, 0:n], rs_b[:, 0:n], rstd[:, 0:n]
                link(nc.vector.reciprocal(a, sd))
                link(nc.vector.tensor_tensor(b, a, a, ALU.mult))
                link(nc.vector.tensor_tensor(b, b, v, ALU.mult))
                link(nc.vector.tensor_scalar(b, b, -0.5, 1.5, ALU.mult, ALU.add))
                link(nc.vector.tensor_tensor(r, a, b, ALU.mult))

            dve.sem_inc(xT_free, 2)
            dve.sem_inc(rest_done, KQ)
            dve.sem_inc(v_free, 1)
            for stored in attn_st + x2_stored + xn2_stored + y_st:
                dve.sem_inc(stored, FREE)
            LN_STEPS = 7

            with dve.Fori(0, BLOCKS // 2) as i:
                for s in range(2):
                    n = i * 2 + s
                    link = chain(n * LN_STEPS)
                    dve.wait_ge(x_ld[s], i * 16 + 16)
                    for a in range(TPB):
                        st = nc.vector.bn_stats(stats[:, a, :], x_in[s][:, a, :])
                    link(st, relay=True)
                    for a in range(TPB):
                        st = nc.vector.bn_aggr(mv[:, a, :], stats[:, a, :])
                    link(st)
                    nc.vector.tensor_scalar(var_e[:], mv[:, :, 1], EPS, None, ALU.add).then_inc(var_done, 1)
                    dve.wait_ge(std_done, n + 1)
                    newton(link, TPB)
                    for a in range(TPB):
                        nc.vector.tensor_scalar(x_in[s][:, a, :], x_in[s][:, a, :], mv[:, a, 0:1], rstd[:, a:a + 1],
                                                ALU.subtract, ALU.mult).then_inc(ln_done, 1)
                    for l in range(KQ):
                        par = (KQ * s + l) % 2
                        dve.wait_ge(part1, n * KQ + (l + 1))
                        nc.vector.tensor_tensor(rest[par], bank[l][:], parts[par][:, 0, :],
                                                ALU.subtract).then_inc(rest_done, 1)

            links = BLOCKS * LN_STEPS

            def reduce(v, par, j, f):
                qt, pair = f // 2, f % 2
                dve.wait_ge(max_ready, v * (FILLS * UG) + (FILLS * j + f + 1))
                nc.vector.tensor_reduce(mx[par][:, HPG * j + 2 * pair:HPG * j + 2 * pair + 2, qt:qt + 1],
                                        bank[f % 2][:].rearrange("p (c k) -> p c k", c=2), AX.X,
                                        ALU.max).then_inc(max_done, 1)

            def neg_max_part(v, par, n):
                dve.wait_ge(mxt_ready, v + 1)
                dve.wait_ge(nm_out[par], n * 16)
                nc.vector.tensor_scalar(nm[par][:, 0, :], bank[7][0:2 * UH, 0:P], -1.0, None,
                                        ALU.mult).then_inc(nm_first, 1)
                dve.wait_ge(nm_first, v + 1)
                nc.vector.scalar_tensor_tensor(nm_rest[par], bank[7][0:2 * UH, 0:P], -1.0, nm[par][:, 0, :],
                                               ALU.mult, ALU.subtract).then_inc(nm_rest_done, 1)
                dve.wait_ge(nm_rest_done, v + 1)
                dve.sem_inc(ot_used, 1)

            def normalise(G, half, b, j):
                dve.wait_ge(ot_ready, G + 1)
                if j == 0:
                    dve.wait_ge(attn_st[half], b * 16 + FREE)
                src = bank[7][:, 0:2 * P].rearrange("p (q h c) -> p q h c", q=2, c=VW)
                nc.vector.reciprocal(o_rec, src[:, :, :, HD]).then_inc(rec_done, 1)
                dve.wait_ge(rec_done, G + 1)
                nc.vector.tensor_tensor(
                    attn_u[half][:, :, j * HPG * HD:(j + 1) * HPG * HD].rearrange("p q (h d) -> p q h d", d=HD),
                    src[:, :, :, 0:HD], o_rec.unsqueeze(3).broadcast_to([P, 2, HPG, HD]),
                    ALU.mult).then_inc(attn_done, 1)
                dve.wait_ge(attn_done, G + 1)
                dve.sem_inc(ot_used, 1)

            def attn_step(u, par, n, has_max=True, first=False):
                for j in range(UG):
                    for f in range(FILLS):
                        if has_max:
                            reduce(u + 2, par, j, f)
                    if not (first and j < 2):
                        if j < 2:
                            normalise(u * UG + (j - 2), 1 - par, n - 1 + par, j + 2)
                        else:
                            normalise(u * UG + (j - 2), par, n, j - 2)
                if has_max:
                    neg_max_part(u + 2, par, n + 1)

            for v in range(2):
                for j in range(UG):
                    for f in range(FILLS):
                        reduce(v, v, j, f)
                neg_max_part(v, v, 0)
            attn_step(0, 0, 0, first=True)
            with dve.Fori(0, 3) as i:
                for r in range(4):
                    attn_step(i * 4 + (1 + r), (1 + r) % 2, i * 2 + (1 + r) // 2)
            attn_step(13, 1, 6)
            attn_step(14, 0, 7, has_max=False)
            attn_step(15, 1, 7, has_max=False)
            for G in (UNITS * UG - 2, UNITS * UG - 1):
                normalise(G, 1, 7, G % UG)

            def residual_norm(t, s, n):
                link = chain(t * 7 + links)
                dve.wait_ge(fc_ready, t + 1)
                dve.wait_ge(xb_done, t + 1)
                dve.wait_ge(x2_stored[s], n * 16 + FREE)
                nc.vector.tensor_tensor(x2_sb[s], bank[2 + s][:], res_in[s], ALU.add).then_inc(x2_done, 1)
                dve.wait_ge(x2_done, t + 1)
                link(nc.vector.bn_stats(stats[:, 0, :], x2_sb[s]), relay=True)
                link(nc.vector.bn_aggr(mv[:, 0, :], stats[:, 0, :]))
                nc.vector.tensor_scalar(var_e[:, 0:1], mv[:, 0, 1:2], EPS, None, ALU.add).then_inc(var2_done, 1)
                dve.wait_ge(std2_done, t + 1)
                newton(link, 1)
                dve.wait_ge(xn2_stored[s], n * 16 + FREE)
                nc.vector.tensor_scalar(xn2_sb[s], x2_sb[s], mv[:, 0, 0:1], rstd[:, 0:1],
                                        ALU.subtract, ALU.mult).then_inc(ln2_done, 1)

            with dve.Fori(0, TILES // 2) as i:
                for s in range(2):
                    residual_norm(i * 2 + s, s, i)

            link = route_link = chain(links + 7 * TILES)

            def bc(ap, axis, n):
                shape = list(ap.shape)
                return ap.unsqueeze(axis).broadcast_to(shape[:axis] + [n] + shape[axis:])

            def hidden(w, par):
                dve.wait_ge(u_ready, w + 1)
                dve.wait_ge(sil_done, w + 1)
                if not (isinstance(w, int) and w < 2):
                    dve.wait_ge(ht_ready, w - 1)
                nc.vector.tensor_tensor(h_sb[par][:], bank[GU_BANKS[par][1]][:, 0:F], sil[par][:],
                                        ALU.mult).then_inc(h_done, 1)

            def softmax():
                dve.wait_ge(gate_evac, TILES)
                link(nc.vector.tensor_reduce(t_tile[:, 0, :], logits[:], AX.X, ALU.max))
                nc.vector.tensor_tensor(score[:], logits[:], bc(t_tile[:, 0, :], 2, NE), ALU.subtract).then_inc(soft_in, 1)
                dve.wait_ge(soft_exp, 1)
                link(nc.vector.tensor_reduce(t_tile[:, 1, :], score[:], AX.X, ALU.add))
                link(nc.vector.reciprocal(t_tile[:, 2, :], t_tile[:, 1, :]))
                link(nc.vector.tensor_tensor(score[:], score[:], bc(t_tile[:, 2, :], 2, NE), ALU.mult))

            def rank(out_, val, n):
                before = cmp_a[:, 0:TILES * n * n].rearrange("p (t i j) -> p t i j", t=TILES, i=n)
                equal = cmp_b[:, 0:TILES * n * n].rearrange("p (t i j) -> p t i j", t=TILES, i=n)
                nc.vector.tensor_tensor(before, bc(val, 2, n), bc(val, 3, n), ALU.is_gt)
                link(nc.vector.tensor_tensor(equal, bc(val, 2, n), bc(val, 3, n), ALU.is_equal))
                left = lower[:, 0:n, 0:n]
                link(nc.vector.tensor_tensor(equal, equal, bc(left, 1, TILES), ALU.mult))
                link(nc.vector.tensor_tensor(before, before, equal, ALU.add))
                link(nc.vector.tensor_reduce(out_, before, AX.X, ALU.add))

            def choose():
                for s in range(2):
                    dve.wait_ge(xn2_stored[s], FREE + 16 * TILES // 2)
                    dve.wait_ge(lnt_stored[s], FREE + 16 * TILES // 2)
                link(nc.vector.tensor_reduce(gmax[:], score[:].rearrange("p t (g e) -> p t g e", e=2), AX.X, ALU.max))
                rank(grank[:], gmax[:], NE // 2)
                link(nc.vector.tensor_scalar(grank[:], grank[:], 2.0, None, ALU.is_lt))
                link(nc.vector.tensor_tensor(score[:].rearrange("p t (g e) -> p t g e", e=2),
                                             score[:].rearrange("p t (g e) -> p t g e", e=2),
                                             bc(grank[:], 3, 2), ALU.mult))
                rank(pos[:], score[:], NE)
                nc.vector.tensor_scalar(sel[:], pos[:], 2.0, None, ALU.is_lt).then_inc(sel_done, 1)
                dve.wait_ge(sel_done, 1)
                link(nc.vector.tensor_tensor(wsel[:], score[:], sel[:], ALU.mult))

            def place():
                dve.wait_ge(pre_ready, 1)
                pre = bank[XT_BANK][:, 0:P].rearrange("p (t e) -> p t e", t=TILES)
                tot = bank[XT_BANK][:, P:2 * P].rearrange("p (t e) -> p t e", t=TILES)
                link(nc.vector.tensor_copy(run_a[:], tot))
                src, dst, d = run_a, run_b, 1
                while d < TILES:
                    nc.vector.tensor_copy(dst[:, 0:d, :], src[:, 0:d, :])
                    link(nc.vector.tensor_tensor(dst[:, d:, :], src[:, d:, :], src[:, 0:TILES - d, :], ALU.add))
                    src, dst, d = dst, src, 2 * d
                full = cmp_a[:, 0:NE * TILES].rearrange("p (e t) -> p e t", e=NE)
                link(nc.vector.tensor_scalar(run_c[:], iota_f[:, 0:TILES], float(P), None, ALU.mult))
                link(nc.vector.tensor_tensor(full, bc(src[:, TILES - 1, :], 2, TILES), bc(run_c[:], 1, NE), ALU.is_gt))
                link(nc.vector.tensor_reduce(cnt[:, 0, :], full, AX.X, ALU.add))
                link(nc.vector.tensor_copy(cnt[:, 1, :], cnt[:, 0, :]))
                a, b, d = 1, 2, 1
                while d < NE:
                    nc.vector.tensor_copy(cnt[:, b, 0:d], cnt[:, a, 0:d])
                    link(nc.vector.tensor_tensor(cnt[:, b, d:], cnt[:, a, d:], cnt[:, a, 0:NE - d], ALU.add))
                    a, b, d = b, a, 2 * d
                link(nc.vector.tensor_tensor(cnt[:, 3, :], cnt[:, a, :], cnt[:, 0, :], ALU.subtract))
                link(nc.vector.tensor_scalar(cnt[:, 3, :], cnt[:, 3, :], float(P), None, ALU.mult))
                link(nc.vector.tensor_tensor(pos[:], src[:], tot, ALU.subtract))
                link(nc.vector.tensor_tensor(pos[:], pos[:], pre, ALU.add))
                link(nc.vector.tensor_tensor(pos[:], pos[:], bc(cnt[:, 3, :], 1, TILES), ALU.add))
                link(nc.vector.tensor_tensor(pos[:], pos[:], sel[:], ALU.mult))
                nc.vector.tensor_reduce(t_tile[:, 0, :], pos[:], AX.X, ALU.max)
                link(nc.vector.tensor_reduce(t_tile[:, 1, :], pos[:], AX.X, ALU.add))
                link(nc.vector.tensor_tensor(t_tile[:, 2, :], t_tile[:, 1, :], t_tile[:, 0, :], ALU.subtract))
                nc.vector.tensor_copy(p1_i[:], t_tile[:, 0, :])
                nc.vector.tensor_copy(p2_i[:], t_tile[:, 2, :]).then_inc(slots_done, 1)
                link(nc.vector.tensor_tensor(run_a[:], pos[:], bc(t_tile[:, 0, :], 2, NE), ALU.is_equal))
                link(nc.vector.tensor_tensor(run_a[:], run_a[:], wsel[:], ALU.mult))
                nc.vector.tensor_reduce(w1[:], run_a[:], AX.X, ALU.add)
                link(nc.vector.tensor_tensor(run_b[:], wsel[:], run_a[:], ALU.subtract))
                link(nc.vector.tensor_reduce(w2[:], run_b[:], AX.X, ALU.add))
                ends = bc(cnt[:, a, :], 1, SLOTS + 1)
                cmp_e = tile_cmp[:].rearrange("p (m e) -> p m e", e=NE)
                link(nc.vector.tensor_tensor(cmp_e, bc(iota_f[:], 2, NE), ends, ALU.is_ge))
                link(nc.vector.tensor_reduce(slot_e[:, 0, :], cmp_e, AX.X, ALU.add))
                link(nc.vector.tensor_scalar(slot_e[:, 0, :], slot_e[:, 0, :], float(NE - 1), None, ALU.min))
                nc.vector.tensor_scalar(gu_off[:], slot_e[:, 0, :], float(GU_W), None, ALU.mult)
                nc.vector.tensor_scalar(dn_off[:], slot_e[:, 0, :], float(DN_W), None, ALU.mult).then_inc(offs_done, 1)

            def early_sum(t, s, n):
                dve.wait_ge(dn_done, t * 2 + 2)
                dve.wait_ge(x2_ld[s], n * 16 + 16)
                nc.vector.tensor_tensor(tok_in[s], bank[Y_BANKS[s]][:], tok_in[s], ALU.add).then_inc(y_evac, 1)

            softmax()
            choose()
            hidden(0, 0)
            hidden(1, 1)
            place()
            hidden(2, 0)
            early_sum(0, 0, 0)
            hidden(3, 1)
            with dve.Fori(1, EARLY // 2) as i:
                for s in range(2):
                    hidden(i * 4 + 2 * s, 0)
                    early_sum(i * 2 + s - 1, 1 - s, i + s - 1)
                    hidden(i * 4 + (2 * s + 1), 1)

            def slot_evac(m, s):
                dve.wait_ge(xt_ready, m + 1)
                dve.wait_ge(u_ready, m + (B0 - 1))
                nc.vector.tensor_copy(xT[s], bank[XT_BANK][:]).then_inc(xt_evac, 1)

            def slot_result(m, s, n):
                dve.wait_ge(dn_done, m + (B0 + 1))
                dve.wait_ge(y_st[s], n * 16 + FREE)
                nc.vector.tensor_copy(mid[s], bank[Y_BANKS[(YB0 + s) % 2]][:]).then_inc(y_evac, 1)

            for s in range(2):
                dve.wait_ge(sc_st[s], 32 * TILES // 2)
            slot_evac(0, 0)
            hidden(B0, 0)
            early_sum(EARLY - 1, 1, EARLY // 2 - 1)
            slot_evac(1, 1)
            with dve.Fori(0, (SLOTS - 3) // 2) as i:
                for r in range(2):
                    m = i * 2 + (1 + r)
                    slot_evac(m + 1, r)
                    hidden(m + B0, 1 - r)
                    slot_result(m - 1, r, i)
            m = SLOTS - 2
            slot_evac(m + 1, (m + 1) % 2)
            hidden(m + B0, m % 2)
            slot_result(m - 1, (m - 1) % 2, (m - 1) // 2)
            hidden(m + 1 + B0, (m + 1) % 2)
            slot_result(m, m % 2, m // 2)

            def early_out(m, base_):
                dve.wait_ge(cx2_ld[0], m * 16 + 16)
                dve.wait_ge(gat_ld[0], m * 32 + 32)
                dve_link = chain(base_)
                dve_link(nc.vector.scalar_tensor_tensor(tok_in[0], mid[0], w1[:, bass.ds(m, 1)], tok_in[0],
                                                        ALU.mult, ALU.add))
                nc.vector.scalar_tensor_tensor(late[0], late[0], w2[:, bass.ds(m, 1)], tok_in[0],
                                               ALU.mult, ALU.add).then_inc(out_done, 1)

            def late_out(m, ypar, base_):
                dve.wait_ge(cx2_ld[1], m * 16 + 16)
                dve.wait_ge(dn_done, m * 2 + (C0 + 2))
                nc.vector.tensor_tensor(tok_in[1], bank[Y_BANKS[ypar]][:], tok_in[1], ALU.add).then_inc(y_evac, 1)
                dve.wait_ge(y_evac, m + (YC0 + 1))
                dve.wait_ge(gat_ld[1], m * 32 + 32)
                dve_link = chain(base_)
                dve_link(nc.vector.scalar_tensor_tensor(tok_in[1], mid[1], w1[:, bass.ds(m + EARLY, 1)], tok_in[1],
                                                        ALU.mult, ALU.add))
                nc.vector.scalar_tensor_tensor(late[1], late[1], w2[:, bass.ds(m + EARLY, 1)], tok_in[1],
                                               ALU.mult, ALU.add).then_inc(out_done, 1)

            links4 = links + 7 * TILES + route_link.count[0]
            hidden(C0, C0 % 2)
            slot_result(SLOTS - 1, (SLOTS - 1) % 2, (SLOTS - 1) // 2)
            hidden(C0 + 1, (C0 + 1) % 2)
            hidden(C0 + 2, C0 % 2)
            early_out(0, links4)
            late_out(0, YC0 % 2, links4 + 1)
            hidden(C0 + 3, (C0 + 1) % 2)
            with dve.Fori(1, (TILES - EARLY) // 2) as i:
                for r in range(2):
                    m = i * 2 + r
                    hidden(m * 2 + C0, C0 % 2)
                    early_out(m - 1, (m - 1) * 2 + links4)
                    late_out(m - 1, (YC0 + r + 1) % 2, (m - 1) * 2 + (links4 + 1))
                    hidden(m * 2 + (C0 + 1), (C0 + 1) % 2)
            m = TILES - EARLY - 1
            early_out(m, m * 2 + links4)
            late_out(m, (YC0 + m) % 2, m * 2 + links4 + 1)


def _inputs(x, ctx, Wq, Wk, Wv, Wfc, bfc, gate, gate_w, up_w, down_w, sh_gate, sh_up, sh_down):
    import numpy as np

    def contraction_first(w):
        return np.ascontiguousarray(w.T.reshape(KD, P, -1).transpose(1, 0, 2))

    ctxT = np.ascontiguousarray(ctx.reshape(T, D).T.reshape(KD, P, BLOCKS, BT).transpose(2, 1, 0, 3))
    gates = np.concatenate([gate_w, sh_gate.reshape(SH, F, D)])
    ups = np.concatenate([up_w, sh_up.reshape(SH, F, D)])
    gu = np.stack([gates, ups], 1)
    gu = gu.reshape(NE + SH, 2, F, KD, P).transpose(0, 4, 3, 1, 2).reshape(NE + SH, P, GU_W)
    downs = np.concatenate([down_w, sh_down.reshape(D, SH, F).transpose(1, 0, 2)]).transpose(0, 2, 1)
    dn = downs[:, 0:2 * P].reshape(NE + SH, 2, P, D).transpose(0, 2, 1, 3).reshape(NE + SH, P, 2 * D)
    return {
        "x": np.ascontiguousarray(x.reshape(T, D)), "ctxT": ctxT, "wqT": contraction_first(Wq),
        "wkvT": np.ascontiguousarray(np.concatenate([contraction_first(Wk), contraction_first(Wv)], 2)),
        "wfcT": contraction_first(Wfc), "bfc": np.ascontiguousarray(bfc), "gwT": contraction_first(gate),
        "wgu": np.ascontiguousarray(gu), "wdn": np.ascontiguousarray(dn),
        "wdt": np.ascontiguousarray(downs[:, 2 * P:F]),
    }


def kernel(x, ctx_2048, L0_xattn_Wq, L0_xattn_Wk, L0_xattn_Wv, L0_xattn_Wfc, L0_xattn_bfc, L0_ffn_gate_weight,
           L0_ffn_gate_w, L0_ffn_up_w, L0_ffn_down_w, L0_ffn_sh_gate_w, L0_ffn_sh_up_w, L0_ffn_sh_down_w):
    import numpy as np
    import concourse.bacc as bacc
    from concourse.bass_utils import run_bass_kernel_spmd

    given = [np.asarray(a) for a in (x, ctx_2048, L0_xattn_Wq, L0_xattn_Wk, L0_xattn_Wv, L0_xattn_Wfc, L0_xattn_bfc,
                                     L0_ffn_gate_weight, L0_ffn_gate_w, L0_ffn_up_w, L0_ffn_down_w,
                                     L0_ffn_sh_gate_w, L0_ffn_sh_up_w, L0_ffn_sh_down_w)]
    arrays = {"in_" + k: v for k, v in _inputs(*given).items()}
    nc = bacc.Bacc("TRN2", target_bir_lowering=False, num_devices=1)
    args = [nc.dram_tensor(k, v.shape, mybir.dt.from_np(v.dtype), kind="ExternalInput").ap() for k, v in arrays.items()]
    out = nc.dram_tensor("out", (T, D), F32, kind="ExternalOutput").ap()
    build(nc, *args, out)
    got = run_bass_kernel_spmd(nc, [arrays], core_ids=[0])
    return got.results[0]["out"].reshape(BATCH, SEQ, D)
```

```python
from contextlib import ExitStack

import concourse.bass as bass
from concourse import mybir

F32 = mybir.dt.float32
BF16 = mybir.dt.bfloat16
I32 = mybir.dt.int32
ALU = mybir.AluOpType
ACT = mybir.ActivationFunctionType
AX = mybir.AxisListType

P = 128
D = 512
KD = D // P
BATCH, SEQ = 8, 256
T = BATCH * SEQ
TILES = T // P
HEADS, GROUPS, HD = 32, 8, 16
HPG = HEADS // GROUPS
SCALE = HD ** -0.5
EPS = 1e-5
NE, F = 8, 352
SH = 2
FT = [(0, 128), (128, 128), (256, 96)]
GU_W = KD * 2 * F
DN_W = len(FT) * D
SLOTS = 2 * T // P + NE - 1
BLOCKS, BT = 4, 512
TPB = BT // P
KQ = 1 + KD
PARTS_Q = (0, 0, 1, 1, 0, 2)
PARTS_K = (0, 1, 0, 1, 2, 0)
STACK = len(PARTS_Q) * HD
ROWS = STACK + 3
UH = HEADS // 2
UG = UH // HPG
UNITS = 2 * BATCH
FILLS = 4
VW = 32
FREE = 16
HELD = 5
P3_ROUNDS = TILES // 4 - 1
ZERO_FIRST = 15
EARLY = TILES // 2
PA, PB, PC = SH * EARLY, SLOTS, SH * (TILES - EARLY)


def build(nc, x, ctxT, wqT, wkvT, wfcT, bfc, gwT, wgu, wdn, wdt, out):
    def dram(name, shape, dt=F32):
        return nc.dram_tensor(name, shape, dt, kind="Internal").ap()

    q_parts = dram("q_parts", (3, D, T), BF16)
    k_parts = dram("k_parts", (3, P, T), BF16)
    v_dram = dram("v_dram", (TILES, P, GROUPS * VW))
    v_blocks = v_dram.rearrange("(n a) p c -> n p a c", a=TPB)
    neg_max = dram("neg_max", (UNITS, 3, 2 * UH, P), BF16)
    attn_dram = dram("attn_dram", (BATCH, 2, P, D))
    x2_dram = dram("x2_dram", (TILES, P, D))
    xn2_dram = dram("xn2_dram", (TILES, P, D))
    xnT_dram = dram("xnT_dram", (TILES, P, D))
    slot_x = dram("slot_x", (SLOTS * P, D))
    slot_y = dram("slot_y", (SLOTS * P, D))
    x_blocks = x.rearrange("(n a p) d -> n p a d", a=TPB, p=P)
    x_tiles = x.rearrange("(t p) d -> t p d", p=P)
    out_tiles = out.rearrange("(t p) d -> t p d", p=P)
    slot_x_tiles = slot_x.rearrange("(t p) d -> t p d", p=P)
    slot_y_tiles = slot_y.rearrange("(t p) d -> t p d", p=P)

    with ExitStack() as ctx:
        def sb(name, shape, dt=F32):
            return ctx.enter_context(nc.sbuf_tensor("sb_" + name, shape, dt))

        def sem(name):
            return ctx.enter_context(nc.semaphore(name))

        bank = [ctx.enter_context(nc.psum_tensor(f"bank{i}", [P, 512], F32)) for i in range(8)]

        weights = sb("weights", [P, (NE + SH) * (GU_W + DN_W)])
        GU0, DN0 = 0, NE * GU_W
        SHGU0 = NE * (GU_W + DN_W)
        SHDN0 = SHGU0 + SH * GU_W

        def words(at, n):
            return weights[:, at:at + n]

        q_words, k_words, v_words, p_words = UH * SEQ // 2, UG * SEQ // 2, 2 * UG * VW, 2 * HPG * SEQ
        P3_0 = SHGU0 - (KD * D + 4 * D + D)
        at = 0
        q_st = [words(at + s * q_words, q_words).bitcast(BF16).rearrange("p (h t) -> p h t", h=UH) for s in range(4)]
        at += 4 * q_words
        probs = [words(at + s * p_words, p_words).rearrange("p (k n) -> p k n", k=2) for s in range(2)]
        at += 2 * p_words
        P1_0 = at
        assert at <= GU0 + HELD * GU_W
        at = DN0 + (NE - HELD) * DN_W
        KV_0 = at
        k_st = [words(at + s * k_words, k_words).bitcast(BF16).rearrange("p (g t) -> p g t", g=UG) for s in range(4)]
        at += 4 * k_words
        v_st = [words(at + s * v_words, v_words).rearrange("p (k g c) -> p k g c", k=2, g=UG) for s in range(4)]
        at += 4 * v_words
        assert at <= P3_0
        x_in = [words(at + s * TPB * D, TPB * D).rearrange("p (a d) -> p a d", a=TPB) for s in range(2)]
        at += 2 * TPB * D
        xnT = [words(at + s * KD * BT, KD * BT).rearrange("p (k t) -> p k t", k=KD) for s in range(2)]
        at += 2 * KD * BT
        cxT = [words(at + s * KD * BT, KD * BT).rearrange("p (k t) -> p k t", k=KD) for s in range(2)]
        at += 2 * KD * BT
        assert at <= SHGU0 + SH * (GU_W + DN_W)
        at = P1_0
        wq_sb = words(at, KD * D).rearrange("p (k n) -> p k n", k=KD)
        at += KD * D
        wkv_sb = words(at, KD * 2 * P).rearrange("p (k n) -> p k n", k=KD)
        at += KD * 2 * P
        parts = [words(at + s * 768, 768).bitcast(BF16).rearrange("p (s t) -> p s t", s=3) for s in range(2)]
        at += 2 * 768
        rest = [words(at + s * BT, BT) for s in range(2)]
        at += 2 * BT
        v_blk = [words(at + s * TPB * GROUPS * VW, TPB * GROUPS * VW)
                 .rearrange("p (a g c) -> p a g c", a=TPB, g=GROUPS) for s in range(2)]
        at += 2 * TPB * GROUPS * VW
        assert at <= KV_0
        at = P3_0
        wfc_sb = words(at, KD * D).rearrange("p (k n) -> p k n", k=KD)
        at += KD * D
        a_in = [words(at + s * D, D) for s in range(2)]
        at += 2 * D
        oT = [words(at + s * D, D).rearrange("p (k t) -> p k t", k=KD) for s in range(2)]
        at += 2 * D
        bfc_sb = words(at, D)
        at += D
        assert at == SHGU0

        rows = sb("rows", [P, 8 * D])

        def row(i):
            return rows[:, i * D:(i + 1) * D]

        ident = sb("ident", [P, P])
        tri = sb("tri", [P, P])
        ones = sb("ones", [P, P])
        lower = sb("lower", [P, NE, NE])
        iota_f = sb("iota_f", [P, SLOTS + 1])
        gw_sb = sb("gw_sb", [P, KD, NE])
        zero_row = sb("zero_row", [P, D])
        stats = sb("stats", [P, TPB, 6])
        mv = sb("mv", [P, TPB, 2])
        var_e = sb("var_e", [P, TPB])
        std = sb("std", [P, TPB])
        rs_a = sb("rs_a", [P, TPB])
        rs_b = sb("rs_b", [P, TPB])
        rstd = sb("rstd", [P, TPB])
        attn_u = [row(i).rearrange("p (q n) -> p q n", q=2) for i in range(2)]
        o_raw = [rows[:, 2 * D + s * SEQ:2 * D + (s + 1) * SEQ] for s in range(2)]
        mx = [rows[:, 3 * D + s * 2 * UH:3 * D + (s + 1) * 2 * UH].rearrange("p (h q) -> p h q", h=UH) for s in range(2)]
        o_rec = rows[:, 3 * D + 4 * UH:3 * D + 4 * UH + 2 * HPG].rearrange("p (q h) -> p q h", q=2)
        nm = [rows[0:2 * UH, 4 * D + s * 192:4 * D + (s + 1) * 192].bitcast(BF16)
              .rearrange("p (s t) -> p s t", s=3) for s in range(2)]
        nm_rest = [rows[0:2 * UH, 5 * D + s * P:5 * D + (s + 1) * P] for s in range(2)]
        MXT = 2 * P
        res_in, x2_sb, xn2_sb = [row(0), row(1)], [row(2), row(3)], [row(4), row(5)]
        lnT = [row(6), row(7)]
        tok_in, xT, mid, late = [row(0), row(1)], [row(2), row(3)], [row(4), row(5)], [row(6), row(7)]
        scatter_in = mid + late
        slot_in = late
        first_xT = a_in
        cmp_a = rows[:, 4 * D:6 * D]
        cmp_b = rows[:, 6 * D:8 * D]
        h_sb = [sb(f"h{i}", [P, F]) for i in range(2)]
        sil = [sb(f"sil{i}", [P, F]) for i in range(2)]
        hT = [sb(f"hT{i}", [P, len(FT), P]) for i in range(2)]
        logits = sb("logits", [P, TILES, NE])
        score = sb("score", [P, TILES, NE])
        wsel = sb("wsel", [P, TILES, NE])
        sel = sb("sel", [P, TILES, NE])
        pos = sb("pos", [P, TILES, NE])
        run_a = sb("run_a", [P, TILES, NE])
        run_b = sb("run_b", [P, TILES, NE])
        t_tile = sb("t_tile", [P, 4, TILES])
        gmax = sb("gmax", [P, TILES, NE // 2])
        grank = sb("grank", [P, TILES, NE // 2])
        cnt = sb("cnt", [P, 6, NE])
        slot_e = sb("slot_e", [P, 2, SLOTS + 1])
        run_c = sb("run_c", [P, TILES])
        tile_cmp = sb("tile_cmp", [P, (SLOTS + 1) * NE])
        w1 = sb("w1", [P, TILES])
        w2 = sb("w2", [P, TILES])
        p1_i = sb("p1_i", [P, TILES], I32)
        p2_i = sb("p2_i", [P, TILES], I32)
        gu_off = sb("gu_off", [P, SLOTS + 1], I32)
        dn_off = sb("dn_off", [P, SLOTS + 1], I32)

        w_kv, w_q, w_fc, w_gate = sem("w_kv"), sem("w_q"), sem("w_fc"), sem("w_gate")
        w_shared, w_routed = sem("w_shared"), sem("w_routed")
        consts = sem("consts")
        zeroed = sem("zeroed")
        step = sem("step")
        pstep = sem("pstep")
        pool_passed, dve_passed = sem("pool_passed"), sem("dve_passed")
        x_ld = [sem(f"x_ld{s}") for s in range(2)]
        c_ld = [sem(f"c_ld{s}") for s in range(2)]
        var_done, std_done, ln_done = sem("var_done"), sem("std_done"), sem("ln_done")
        xT_ready, xT_free = sem("xT_ready"), sem("xT_free")
        kq_ready, v_ready, v_free = sem("kq_ready"), sem("v_ready"), sem("v_free")
        part1, rest_done, part3 = sem("part1"), sem("rest_done"), sem("part3")
        parts_st = [sem(f"parts_st{s}") for s in range(2)]
        v_st_dma = [sem(f"v_st_dma{s}") for s in range(2)]
        st_ld = [sem(f"st_ld{s}") for s in range(4)]
        kones = sem("kones")
        max_ready, max_done, mxt_ready = sem("max_ready"), sem("max_done"), sem("mxt_ready")
        ot_ready = sem("ot_ready")
        nm_first, nm_rest_done, nm_done, rec_done = sem("nm_first"), sem("nm_rest_done"), sem("nm_done"), sem("rec_done")
        nm_out = [sem(f"nm_out{s}") for s in range(2)]
        nm_in = [sem(f"nm_in{s}") for s in range(4)]
        st_ready, exp_done, pv_ready, pv_evac = sem("st_ready"), sem("exp_done"), sem("pv_ready"), sem("pv_evac")
        attn_done = sem("attn_done")
        attn_st = [sem(f"attn_st{s}") for s in range(2)]
        a_ld = [sem(f"a_ld{s}") for s in range(2)]
        r_ld = [sem(f"r_ld{s}") for s in range(2)]
        ota_ready, ota_evac, fc_ready, xb_done = sem("ota_ready"), sem("ota_evac"), sem("fc_ready"), sem("xb_done")
        x2_done, var2_done, std2_done, ln2_done = sem("x2_done"), sem("var2_done"), sem("std2_done"), sem("ln2_done")
        lnt_ready, lnt_evac, gate_ready, gate_evac = sem("lnt_ready"), sem("lnt_evac"), sem("gate_ready"), sem("gate_evac")
        x2_stored = [sem(f"x2_stored{s}") for s in range(2)]
        xn2_stored = [sem(f"xn2_stored{s}") for s in range(2)]
        lnt_stored = [sem(f"lnt_stored{s}") for s in range(2)]
        soft_in, soft_exp, sel_done, pre_ready, slots_done, offs_done = (
            sem("soft_in"), sem("soft_exp"), sem("sel_done"), sem("pre_ready"), sem("slots_done"), sem("offs_done"))
        sc_ld = [sem(f"sc_ld{s}") for s in range(4)]
        sc_st = [sem(f"sc_st{s}") for s in range(4)]
        sx_ld = [sem(f"sx_ld{s}") for s in range(2)]
        x2_ld = [sem(f"x2_ld{s}") for s in range(2)]
        base_st = [sem(f"base_st{s}") for s in range(2)]
        g_ready, u_ready, sil_done, h_done = sem("g_ready"), sem("u_ready"), sem("sil_done"), sem("h_done")
        ht_ready, ht_evac, dn_done, y_evac = sem("ht_ready"), sem("ht_evac"), sem("dn_done"), sem("y_evac")
        slot_ld = [sem(f"slot_ld{s}") for s in range(2)]
        xt_ready, xt_evac = sem("xt_ready"), sem("xt_evac")
        y_st = [sem(f"y_st{s}") for s in range(2)]
        cx2_ld = [sem(f"cx2_ld{s}") for s in range(2)]
        gat_ld = [sem(f"gat_ld{s}") for s in range(2)]
        out_done = sem("out_done")
        out_st = [sem(f"out_st{s}") for s in range(2)]

        B0, C0 = PA, PA + PB
        YB0, YC0 = EARLY, EARLY + SLOTS
        GU_BANKS = [(0, 1), (2, 3)]
        Y_BANKS = [4, 5]
        HT_BANK, XT_BANK = 6, 7

        block = ctx.enter_context(nc.Block())

        @block.sync
        def _(sp):
            def load_block(n):
                s = n % 2
                if n >= 2:
                    sp.wait_ge(v_ready, n - 1)
                sp.dma_start(cxT[s], ctxT[n]).then_inc(c_ld[s], 16)
                if n >= 2:
                    sp.wait_ge(xT_ready, TPB * (n - 1))
                sp.dma_start(x_in[s], x_blocks[n]).then_inc(x_ld[s], 16)

            sp.dma_start(wkv_sb, wkvT).then_inc(w_kv, 16)
            load_block(0)
            sp.dma_start(wq_sb, wqT).then_inc(w_q, 16)
            load_block(1)
            def store_parts(n, l):
                sp.wait_ge(part3, KQ * n + l + 1)
                dst = k_parts if l == 0 else q_parts[:, (l - 1) * P:l * P]
                par = (KQ * n + l) % 2
                sp.dma_start(dst[:, :, n * BT:(n + 1) * BT].rearrange("s p t -> p s t"),
                             parts[par]).then_inc(parts_st[par], 16)

            def load_gate_up(e, s):
                half = GU_W // 2
                sp.dma_start(weights[:, bass.ds(e * GU_W + (GU0 + s * half), half)],
                             wgu[bass.ds(e, 1), :, s * half:(s + 1) * half].rearrange("o p n -> (o p) n")
                             ).then_inc(w_routed, 16)

            def load_down(e):
                sp.dma_start(weights[:, bass.ds(e * DN_W + DN0, 2 * D)],
                             wdn[bass.ds(e, 1)].rearrange("o p n -> (o p) n")).then_inc(w_routed, 16)
                sp.dma_start(weights[0:FT[2][1], bass.ds(e * DN_W + (DN0 + 2 * D), D)],
                             wdt[bass.ds(e, 1)].rearrange("o p n -> (o p) n")).then_inc(w_routed, 16)

            def load_shared_gu(c):
                sp.dma_start(words(SHGU0 + c * GU_W, GU_W), wgu[NE + c]).then_inc(w_shared, 16)

            def load_shared_dn(c):
                dn = SHDN0 + c * DN_W
                sp.dma_start(words(dn, 2 * D), wdn[NE + c]).then_inc(w_shared, 16)
                sp.dma_start(words(dn + 2 * D, D)[0:FT[2][1]], wdt[NE + c]).then_inc(w_shared, 16)

            def zero_slots(first, n):
                sp.dma_start(slot_x_tiles[bass.ds(first, n)].rearrange("t p d -> p t d"),
                             zero_row[:].unsqueeze(1).broadcast_to([P, n, D])).then_inc(zeroed, 16)

            def load_unit(b, half, s):
                for i in range(len(PARTS_Q)):
                    sp.dma_start(
                        q_st[s][HD * i:HD * (i + 1)],
                        q_parts[PARTS_Q[i], half * UH * HD:(half + 1) * UH * HD, bass.ds(b * SEQ, SEQ)]
                        .rearrange("(h d) t -> d h t", d=HD)).then_inc(st_ld[s], 16)
                    sp.dma_start(
                        k_st[s][HD * i:HD * (i + 1)],
                        k_parts[PARTS_K[i], half * UG * HD:(half + 1) * UG * HD, bass.ds(b * SEQ, SEQ)]
                        .rearrange("(g d) t -> d g t", d=HD)).then_inc(st_ld[s], 16)
                for kt in range(2):
                    sp.dma_start(v_st[s][:, kt, :, :].rearrange("p g c -> p (g c)"),
                                 v_dram[bass.ds(b * 2 + kt, 1), :, half * UG * VW:(half + 1) * UG * VW]
                                 .rearrange("o p c -> (o p) c")).then_inc(st_ld[s], 16)

            for n in range(BLOCKS):
                if n + 2 < BLOCKS:
                    load_block(n + 2)
                if n == 0:
                    sp.wait_ge(consts, 1)
                if n == 2:
                    sp.wait_ge(parts_st[0], FREE + 16 * ((KQ + 1) // 2))
                    sp.wait_ge(parts_st[1], FREE + 16 * (KQ // 2))
                    sp.wait_ge(v_st_dma[0], FREE + 16)
                for l in range(KQ):
                    store_parts(n, l)
                    if n == 1:
                        zero_slots(l * (ZERO_FIRST // KQ), ZERO_FIRST // KQ)
                    if n >= 2 and l in (1, 3):
                        u = 2 * (n - 2) + l // 2
                        load_unit(u // 2, u % 2, u)

            for s in range(2):
                sp.wait_ge(parts_st[s], FREE + 16 * BLOCKS * KQ // 2)
                sp.wait_ge(v_st_dma[s], FREE + 16 * BLOCKS // 2)
            sp.wait_ge(kq_ready, KQ * BLOCKS)

            def neg_max_rows(v, s, par, n):
                sp.wait_ge(nm_out[par], 16 * (n + 1))
                sp.dma_start(q_st[s][STACK:ROWS].rearrange("p h t -> p (h t)"),
                             neg_max[bass.ds(v, 1)].rearrange("o s r c -> (o s) (r c)")).then_inc(nm_in[s], 16)

            def store_attn(u, b, half, n):
                sp.wait_ge(attn_done, UG * (u + 1))
                sp.dma_start(attn_dram[bass.ds(b, 1), :, :, half * UG * HPG * HD:(half + 1) * UG * HPG * HD]
                             .rearrange("o q p c -> p (o q) c"), attn_u[half]).then_inc(attn_st[half], 16)

            sp.dma_start(wfc_sb, wfcT).then_inc(w_fc, 16)
            sp.dma_start(bfc_sb, bfc.partition_broadcast(P)).then_inc(w_fc, 16)
            sp.dma_start(gw_sb[:], gwT).then_inc(w_gate, 16)
            for v in range(2):
                neg_max_rows(v, v, v, 0)
            load_shared_gu(0)
            load_shared_dn(0)
            STEP_ZERO = (SLOTS - ZERO_FIRST) // 12
            with sp.Fori(0, 3) as i:
                for r in range(4):
                    u = i * 4 + (1 + r)
                    sp.wait_ge(pv_ready, u * UG)
                    load_unit(i * 2 + (4 + r) // 2, r % 2, r % 4)
                    store_attn(i * 4 + r, i * 2 + r // 2, r % 2, None)
                    neg_max_rows(i * 4 + (2 + r), (2 + r) % 4, (2 + r) % 2, i * 2 + (2 + r) // 2)
                    zero_slots(i * (4 * STEP_ZERO) + (ZERO_FIRST + r * STEP_ZERO), STEP_ZERO)
                    if r in (0, 2):
                        load_gate_up(i + HELD, r // 2)
                    elif r == 1:
                        load_down(i)
            def load_attn(b, s):
                sp.dma_start(a_in[s], attn_dram[bass.ds(b, 1), s].rearrange("o p d -> (o p) d")).then_inc(a_ld[s], 16)

            for u in range(12, 16):
                store_attn(u, u // 2, u % 2, None)
                if u < 14:
                    neg_max_rows(u + 2, (u + 2) % 4, u % 2, 7)
                if u == 13:
                    for s in range(2):
                        sp.wait_ge(attn_st[s], FREE + 16)
                    for s in range(2):
                        load_attn(0, s)
                if u == 12:
                    load_shared_gu(1)
                    load_shared_dn(1)

            for s in range(2):
                sp.wait_ge(attn_st[s], FREE + 16 * BATCH)

            def load_res_rows(b, s):
                sp.dma_start(res_in[s], x_tiles[bass.ds(b * 2 + s, 1)].rearrange("o p d -> (o p) d")).then_inc(r_ld[s], 16)

            def tile_of(dram_tiles, t):
                return dram_tiles[bass.ds(t, 1)].rearrange("o p d -> (o p) d")

            def store_lnT(t, s):
                sp.wait_ge(lnt_evac, t + 1)
                sp.dma_start(tile_of(xnT_dram, t), lnT[s]).then_inc(lnt_stored[s], 16)

            def store_x2(t, s):
                sp.wait_ge(x2_done, t + 1)
                sp.dma_start(tile_of(x2_dram, t), x2_sb[s]).then_inc(x2_stored[s], 16)

            def store_xn2(t, s):
                sp.wait_ge(ln2_done, t + 1)
                sp.dma_start(tile_of(xn2_dram, t), xn2_sb[s]).then_inc(xn2_stored[s], 16)

            for s in range(2):
                load_res_rows(0, s)
            sp.wait_ge(ota_ready, 1)
            load_attn(1, 0)
            for t in range(2):
                sp.wait_ge(ota_ready, t + 2)
                load_attn((t + 3) // 2, (t + 3) % 2)
                store_x2(t, t)
                load_res_rows(1, t)
                store_xn2(t, t)

            def token_tile(i, s, more=True):
                if more:
                    sp.wait_ge(ota_ready, i * 2 + (s + 2))
                    load_attn(i + (1 + s), 1 - s)
                store_lnT(i * 2 + s - 2, s)
                store_x2(i * 2 + s, s)
                load_res_rows(i + 1, s)
                store_xn2(i * 2 + s, s)

            assert TILES == 2 + 4 * P3_ROUNDS + 2
            def four_tiles(i, last=False):
                for k in range(4):
                    token_tile(i * 2 + (1 + k // 2), k % 2, more=not (last and k == 3))
                    if k in (0, 2):
                        load_gate_up(i, k // 2)

            with sp.Fori(0, P3_ROUNDS - 1) as i:
                four_tiles(i)
            four_tiles(P3_ROUNDS - 1, last=True)
            for t in range(TILES - 2, TILES):
                store_lnT(t - 2, t % 2)
                store_x2(t, t % 2)
                sp.wait_ge(ota_ready, t + 1)
                sp.wait_ge(lnt_stored[t % 2], FREE + 16)
                sp.dma_start(first_xT[t % 2], xnT_dram[t % 2]).then_inc(sx_ld[t % 2], 16)
                store_xn2(t, t % 2)
            for t in range(TILES - 2, TILES):
                store_lnT(t, t % 2)

            for s in range(2):
                sp.wait_ge(lnt_stored[s], FREE + 16 * TILES // 2)
                sp.wait_ge(x2_stored[s], FREE + 16 * TILES // 2)
                sp.wait_ge(xn2_stored[s], FREE + 16 * TILES // 2)

            def load_shared(t, s):
                sp.dma_start(xT[s], tile_of(xnT_dram, t)).then_inc(sx_ld[s], 16)

            def load_res_x2(t, s):
                sp.dma_start(tok_in[s], tile_of(x2_dram, t)).then_inc(x2_ld[s], 16)

            def store_base(t, s):
                sp.wait_ge(y_evac, t + 1)
                sp.dma_start(tile_of(x2_dram, t), tok_in[s]).then_inc(base_st[s], 16)

            def load_slots(n, s):
                sp.dma_start(slot_in[s], tile_of(slot_x_tiles, n)).then_inc(slot_ld[s], 16)

            for t in range(2):
                load_res_x2(t, t)
                load_shared(t + 2, t)
            for t in range(EARLY):
                if t < 2 * (HELD - P3_ROUNDS):
                    load_gate_up(P3_ROUNDS + t // 2, t % 2)
                if t < HELD:
                    load_down(NE - HELD + t)
                if t == EARLY - 1:
                    for buf in range(4):
                        sp.wait_ge(sc_st[buf], 32 * TILES // 4)
                    for s in range(2):
                        load_slots(s, s)
                store_base(t, t % 2)
                if t + 2 < EARLY:
                    sp.wait_ge(base_st[t % 2], 16 * (t // 2 + 1))
                    if t >= 2:
                        load_shared(t + 2, t % 2)
                    load_res_x2(t + 2, t % 2)

            def store_slots(n, s):
                sp.wait_ge(y_evac, YB0 + 1 + n)
                sp.dma_start(tile_of(slot_y_tiles, n), mid[s]).then_inc(y_st[s], 16)

            sp.wait_ge(xt_ready, 1)
            load_slots(2, 0)
            with sp.Fori(0, (SLOTS - 3) // 2) as i:
                for s in range(2):
                    sp.wait_ge(xt_ready, i * 2 + (s + 2))
                    load_slots(i * 2 + (s + 3), 1 - s)
                    store_slots(i * 2 + s, s)
            for n in range(SLOTS - 3, SLOTS - 1):
                store_slots(n, n % 2)

            def load_late(m, s):
                sp.dma_start(xT[s], tile_of(xnT_dram, m + EARLY)).then_inc(sx_ld[s], 16)

            def load_res(t, s):
                sp.dma_start(tok_in[s], tile_of(x2_dram, t)).then_inc(cx2_ld[s], 16)

            def store_out(t, q, s):
                sp.wait_ge(out_done, q + 1)
                sp.dma_start(tile_of(out_tiles, t), late[s]).then_inc(out_st[s], 16)

            sp.wait_ge(u_ready, C0 - 1)
            load_late(0, 1)
            sp.wait_ge(u_ready, C0)
            load_late(1, 0)
            store_slots(SLOTS - 1, (SLOTS - 1) % 2)
            for s in range(2):
                sp.wait_ge(base_st[s], 16 * EARLY // 2)
            load_res(0, 0)
            load_res(EARLY, 1)
            with sp.Fori(0, EARLY // 2 - 1) as i:
                for r in range(2):
                    for s in range(2):
                        store_out(i * 2 + (r + s * EARLY), i * 4 + (2 * r + s), s)
                        load_res(i * 2 + (r + 1 + s * EARLY), s)
                    load_late(i * 2 + (r + 2), 1 - r)
            for m in range(EARLY - 2, EARLY):
                for s in range(2):
                    store_out(m + s * EARLY, 2 * m + s, s)
                    if m + 1 < EARLY:
                        load_res(m + 1 + s * EARLY, s)
            for s in range(2):
                sp.wait_ge(out_st[s], 16 * EARLY)

        @block.gpsimd
        def _(pool):
            def select(out_, pattern, op, base_, mult_):
                nc.gpsimd.affine_select(out=out_, in_=out_, compare_op=op, fill=0.0, base=base_,
                                        pattern=pattern, channel_multiplier=mult_).then_inc(pstep, 1)

            nc.gpsimd.memset(zero_row[:], 0.0).then_inc(consts, 1)
            for s in range(2):
                nc.gpsimd.memset(v_blk[s], 0.0)
            nc.gpsimd.memset(ident[:], 1.0)
            nc.gpsimd.memset(tri[:], 1.0)
            nc.gpsimd.memset(lower[:], 1.0)
            nc.gpsimd.memset(ones[:], 1.0).then_inc(pstep, 1)
            pool.wait_ge(pstep, 1)
            for s in range(2):
                nc.gpsimd.memset(v_blk[s][:, :, :, HD:HD + 1], 1.0).then_inc(pstep, 1)
            select(ident[:], [[-1, P]], ALU.is_equal, 0, 1)
            select(tri[:], [[1, P]], ALU.is_gt, 0, -1)
            select(lower[:], [[1, NE], [-1, NE]], ALU.is_gt, 0, 0)
            nc.gpsimd.iota(iota_f[:], [[1, SLOTS + 1]], base=0, channel_multiplier=0,
                           allow_small_or_imprecise_dtypes=True).then_inc(pstep, 1)
            pool.wait_ge(pstep, 7)
            nc.gpsimd.engine_nop().then_inc(consts, 1)
            for s in range(4):
                nc.gpsimd.memset(k_st[s][STACK:ROWS], 1.0).then_inc(kones, 1)
            pool.wait_ge(kones, 4)

            def cut(n, i, s, l):
                par = (KQ * s + l) % 2
                pool.wait_ge(rest_done, KQ * n + (KQ + l + 1))
                pool.sem_inc(pool_passed, 1)
                nc.gpsimd.tensor_copy(parts[par][:, 1, :], rest[par]).then_inc(pstep, 1)
                pool.wait_ge(pstep, KQ * n + (7 + l + 1))
                nc.gpsimd.tensor_tensor(parts[par][:, 2, :], rest[par], parts[par][:, 1, :],
                                        ALU.subtract).then_inc(part3, 1)

            with pool.Fori(0, BLOCKS // 2) as i:
                for s in range(2):
                    for l in range(KQ):
                        cut(i * 2 + s, i, s, l)

            pstep0 = 7 + KQ * BLOCKS

            def cut_max(v, par):
                pool.wait_ge(nm_rest_done, v + 1)
                pool.sem_inc(pool_passed, 1)
                nc.gpsimd.tensor_copy(nm[par][:, 1, :], nm_rest[par]).then_inc(pstep, 1)
                pool.wait_ge(pstep, v + (pstep0 + 1))
                nc.gpsimd.tensor_tensor(nm[par][:, 2, :], nm_rest[par], nm[par][:, 1, :],
                                        ALU.subtract).then_inc(nm_done, 1)
                pool.wait_ge(nm_done, v + 1)
                pool.sem_inc(pool_passed, 1)
                nc.gpsimd.dma_start(neg_max[bass.ds(v, 1)].rearrange("o s r c -> r (o s) c"),
                                    nm[par]).then_inc(nm_out[par], 16)

            with pool.Fori(0, UNITS // 2) as i:
                for s in range(2):
                    cut_max(i * 2 + s, s)

            pool.wait_ge(w_fc, 32)
            with pool.Fori(0, TILES // 2) as i:
                for s in range(2):
                    pool.wait_ge(r_ld[s], i * 16 + 16)
                    nc.gpsimd.tensor_tensor(res_in[s], res_in[s], bfc_sb, ALU.add).then_inc(xb_done, 1)

            pool.wait_ge(slots_done, 1)
            pool.wait_ge(zeroed, 16 * (KQ + 12))
            for s in range(2):
                pool.wait_ge(xn2_stored[s], FREE + 16 * TILES // 2)
            def load_scatter(t):
                nc.gpsimd.dma_start(scatter_in[t % 4], xn2_dram[t]).then_inc(sc_ld[t % 4], 16)

            for t in range(2):
                load_scatter(t)
            for t in range(TILES):
                pool.wait_ge(sc_ld[t % 4], 16 * (t // 4 + 1))
                for idx in (p1_i, p2_i):
                    nc.gpsimd.indirect_dma_start(
                        out=slot_x, out_offset=bass.IndirectOffsetOnAxis(ap=idx[:, t:t + 1], axis=0),
                        in_=scatter_in[t % 4], in_offset=None).then_inc(sc_st[t % 4], 16)
                if t + 2 < TILES:
                    if t >= 2:
                        pool.wait_ge(sc_st[(t - 2) % 4], 32 * ((t - 2) // 4 + 1))
                    load_scatter(t + 2)

            for s in range(2):
                pool.wait_ge(y_st[s], FREE + 16 * ((SLOTS + 1 - s) // 2))
            for q in range(2 * EARLY):
                s = q % 2
                t = q // 2 + s * EARLY
                if q >= 2:
                    pool.wait_ge(out_st[s], 16 * (q // 2))
                for buf, idx in ((mid[s], p1_i), (late[s], p2_i)):
                    nc.gpsimd.indirect_dma_start(
                        out=buf, out_offset=None, in_=slot_y,
                        in_offset=bass.IndirectOffsetOnAxis(ap=idx[:, t:t + 1], axis=0)).then_inc(gat_ld[s], 16)

        @block.scalar
        def _(act):
            for stored in parts_st + v_st_dma + lnt_stored:
                act.sem_inc(stored, FREE)
            act.wait_ge(consts, 2)

            def cut_first(n, i, s, l):
                par, uses = (KQ * s + l) % 2, (KQ * s + l) // 2
                act.wait_ge(kq_ready, KQ * n + (l + 1))
                act.wait_ge(parts_st[par], i * (16 * KQ) + (FREE + 16 * uses))
                nc.scalar.copy(parts[par][:, 0, :], bank[l][:]).then_inc(part1, 1)

            with act.Fori(0, BLOCKS // 2) as i:
                for s in range(2):
                    n = i * 2 + s
                    act.wait_ge(var_done, n + 1)
                    nc.scalar.activation(std[:], var_e[:], ACT.Sqrt).then_inc(std_done, 1)
                    cut_first(n, i, s, 0)
                    act.wait_ge(v_ready, n + 1)
                    act.wait_ge(v_st_dma[s], i * 16 + FREE)
                    nc.scalar.copy(v_blk[s][:, :, :, 0:HD],
                                   bank[5][:].rearrange("p (a g c) -> p a g c", a=TPB, g=GROUPS)).then_inc(v_free, 1)
                    for a in range(TPB):
                        act.wait_ge(xT_ready, n * TPB + (a + 1))
                        nc.scalar.copy(xnT[s][:, :, a * P:(a + 1) * P],
                                       bank[6 + a % 2][:].rearrange("p (k t) -> p k t", k=KD)).then_inc(xT_free, 1)
                    act.wait_ge(v_free, n + 2)
                    act.dma_start(v_blocks[bass.ds(n, 1)].rearrange("o p a c -> (o p) a c"),
                                  v_blk[s].rearrange("p a g c -> p a (g c)")).then_inc(v_st_dma[s], 16)
                    for l in range(1, KQ):
                        cut_first(n, i, s, l)

            def attn_act(G, fill_G=True, first=False, evac=True, par=0):
                if fill_G:
                    for f in range(FILLS):
                        kt, pair = f // 2, f % 2
                        act.wait_ge(st_ready, G * FILLS + (f + 1))
                        if f == 0 and not first:
                            act.wait_ge(pv_ready, G - 1)
                        nc.scalar.activation(probs[par][:, kt, pair * 512:(pair + 1) * 512], bank[2 + f][:], ACT.Exp,
                                             scale=SCALE).then_inc(exp_done, 1)
                if evac:
                    act.wait_ge(pv_ready, G)
                    if not first:
                        act.wait_ge(ot_ready, G - 2)
                    nc.scalar.copy(o_raw[1 - par], bank[6][:, 0:SEQ]).then_inc(pv_evac, 1)

            for G in range(UG):
                attn_act(G, first=(G < 3), evac=(G > 0), par=G % 2)
            with act.Fori(0, 3) as i:
                for r in range(4 * UG):
                    attn_act(i * (4 * UG) + (UG + r), par=r % 2)
            with act.Fori(0, 3) as i:
                for j in range(UG):
                    attn_act(i * UG + (13 * UG + j), par=j % 2)
            attn_act(UNITS * UG, fill_G=False, par=0)

            def ot_evac(t, s):
                act.wait_ge(ota_ready, t + 1)
                nc.scalar.copy(oT[s], bank[s][:].rearrange("p (k t) -> p k t", k=KD)).then_inc(ota_evac, 1)

            def lnt_out(t, s, stored):
                act.wait_ge(lnt_ready, t + 1)
                act.wait_ge(lnt_stored[s], stored * 16 + FREE)
                nc.scalar.copy(lnT[s], bank[4 + s][:]).then_inc(lnt_evac, 1)

            def gate_out(t, s):
                act.wait_ge(gate_ready, t + 1)
                nc.scalar.copy(logits[:, bass.ds(t, 1), :], bank[6 + s][:, 0:NE].unsqueeze(1)).then_inc(gate_evac, 1)

            def std2(t):
                act.wait_ge(var2_done, t + 1)
                nc.scalar.activation(std[:, 0:1], var_e[:, 0:1], ACT.Sqrt).then_inc(std2_done, 1)

            ot_evac(0, 0)
            for t in range(2):
                ot_evac(t + 1, (t + 1) % 2)
                std2(t)
            with act.Fori(1, TILES // 2 - 1) as i:
                for s in range(2):
                    lnt_out(i * 2 + s - 2, s, i - 1)
                    ot_evac(i * 2 + (s + 1), 1 - s)
                    std2(i * 2 + s)
                    gate_out(i * 2 + s - 2, s)
            for t in range(TILES - 2, TILES):
                lnt_out(t - 2, t % 2, t // 2 - 1)
                if t + 1 < TILES:
                    ot_evac(t + 1, (t + 1) % 2)
                std2(t)
                gate_out(t - 2, t % 2)
            def silu(w, par):
                act.wait_ge(g_ready, w + 1)
                if not (isinstance(w, int) and w < 2):
                    act.wait_ge(h_done, w - 1)
                nc.scalar.activation(sil[par][:], bank[GU_BANKS[par][0]][:, 0:F], ACT.Silu).then_inc(sil_done, 1)

            def ht_out(w, par):
                act.wait_ge(ht_ready, w + 1)
                if not (isinstance(w, int) and w < 2):
                    act.wait_ge(dn_done, w - 1)
                nc.scalar.copy(hT[par][:, 0:2, :], bank[HT_BANK][:, 0:2 * P].rearrange("p (j t) -> p j t", j=2))
                nc.scalar.copy(hT[par][0:FT[2][1], 2, :], bank[HT_BANK][0:FT[2][1], 2 * P:3 * P]).then_inc(ht_evac, 1)

            for t in range(TILES - 2, TILES):
                lnt_out(t, t % 2, t // 2)
                gate_out(t, t % 2)
                silu(t % 2, t % 2)
            act.wait_ge(soft_in, 1)
            nc.scalar.activation(score[:], score[:], ACT.Exp).then_inc(soft_exp, 1)
            ht_out(0, 0)
            silu(2, 0)
            ht_out(1, 1)
            TOTAL = PA + PB + PC
            with act.Fori(1, (TOTAL - 1) // 2) as i:
                for par in range(2):
                    silu(i * 2 + (par + 1), 1 - par)
                    ht_out(i * 2 + par, par)
            assert TOTAL % 2 == 1
            ht_out(TOTAL - 1, 0)

        @block.tensor
        def _(pe):
            pe.wait_ge(consts, 2)
            pe.wait_ge(w_kv, 16)

            def project(l, n, lhs, rhs_):
                if not (isinstance(n, int) and n == 0):
                    pe.wait_ge(rest_done, n * KQ + (l + 1))
                for k in range(KD):
                    mm = nc.tensor.matmul(bank[l][:], lhs(k), rhs_[:, k, :], start=(k == 0), stop=(k == KD - 1))
                mm.then_inc(kq_ready, 1)

            with pe.Fori(0, BLOCKS // 2) as i:
                for s in range(2):
                    n = i * 2 + s
                    pe.wait_ge(c_ld[s], i * 16 + 16)
                    project(0, n, lambda k: wkv_sb[:, k, 0:P], cxT[s])
                    pe.wait_ge(v_free, n + 1)
                    for a in range(TPB):
                        for k in range(KD):
                            mm = nc.tensor.matmul(bank[5][:, a * P:(a + 1) * P], cxT[s][:, k, a * P:(a + 1) * P],
                                                  wkv_sb[:, k, P:2 * P], start=(k == 0), stop=(k == KD - 1))
                    mm.then_inc(v_ready, 1)
                    for a in range(TPB):
                        pe.wait_ge(ln_done, n * TPB + (a + 1))
                        pe.wait_ge(xT_free, n * TPB + (a + 1))
                        for k in range(KD):
                            tr = nc.tensor.transpose(bank[6 + a % 2][:, k * P:(k + 1) * P],
                                                     x_in[s][:, a, k * P:(k + 1) * P], ident[:])
                        tr.then_inc(xT_ready, 1)
                    pe.wait_ge(w_q, 16)
                    pe.wait_ge(xT_free, n * TPB + (2 + TPB))
                    for m in range(KD):
                        project(1 + m, n, lambda k: wq_sb[:, k, m * P:(m + 1) * P], xnT[s])

            pe.wait_ge(rest_done, KQ * BLOCKS + 2)
            pe.wait_ge(xT_free, TILES + 2)

            def max_fill(v, s, j, f, first=False):
                qt, pair = f // 2, f % 2
                if not (first and j == 0 and f < 2):
                    pe.wait_ge(max_done, v * (FILLS * UG) + (FILLS * j + f - 1))
                for c in range(2):
                    mm = nc.tensor.matmul(bank[f % 2][:, c * SEQ:(c + 1) * SEQ],
                                          q_st[s][0:STACK, HPG * j + 2 * pair + c, qt * P:(qt + 1) * P],
                                          k_st[s][0:STACK, j, :], start=True, stop=True)
                mm.then_inc(max_ready, 1)

            def max_transpose(v, par):
                pe.wait_ge(max_done, v * (FILLS * UG) + FILLS * UG)
                if not (isinstance(v, int) and v < 2):
                    pe.wait_ge(attn_done, v * UG - 6)
                elif v == 1:
                    pe.wait_ge(nm_rest_done, 1)
                nc.tensor.transpose(bank[7][0:2 * UH, MXT:MXT + P], mx[par].rearrange("p h q -> p (h q)"),
                                    ident[:]).then_inc(mxt_ready, 1)

            def score_fill(G, s, j, f, first=False):
                kt, pair = f // 2, f % 2
                if not first:
                    pe.wait_ge(exp_done, G * FILLS + (f + 1 - FILLS))
                nc.tensor.matmul(bank[2 + f][:], k_st[s][0:ROWS, j, kt * P:(kt + 1) * P],
                                 q_st[s][0:ROWS, HPG * j + 2 * pair:HPG * j + 2 * pair + 2, :]
                                 .rearrange("p h t -> p (h t)"), start=True, stop=True).then_inc(st_ready, 1)

            def pv_part(G, s, j, f):
                kt = f // 2
                if f == 0:
                    pe.wait_ge(exp_done, G * FILLS + FILLS)
                    if not (isinstance(G, int) and G == 0):
                        pe.wait_ge(pv_evac, G)
                for c in (2 * (f % 2), 2 * (f % 2) + 1):
                    mm = nc.tensor.matmul(bank[6][VW * c:VW * (c + 1), 0:SEQ], v_st[s][:, kt, j, :],
                                          probs[j % 2][:, kt, c * SEQ:(c + 1) * SEQ],
                                          start=(kt == 0), stop=(kt == 1), tile_position=(0, VW * c))
                if f == FILLS - 1:
                    mm.then_inc(pv_ready, 1)

            def attn_transpose(G, par, unit=None):
                pe.wait_ge(pv_evac, G + 1)
                if not (isinstance(G, int) and G == 0):
                    pe.wait_ge(attn_done, G)
                if unit is not None:
                    pe.wait_ge(nm_rest_done, unit + 1)
                for qt in range(2):
                    tr = nc.tensor.transpose(bank[7][:, qt * P:(qt + 1) * P], o_raw[par][:, qt * P:(qt + 1) * P],
                                             ident[:])
                tr.then_inc(ot_ready, 1)

            def unit_ready(v, s, n):
                pe.wait_ge(st_ld[s], (n + 1) * (16 * (2 * len(PARTS_Q) + 2)))

            def attn_step(u, s, n, has_max=True, first=False, last=False):
                sv = (s + 2) % 4
                if has_max:
                    unit_ready(u + 2, sv, n + (s + 2) // 4)
                pe.wait_ge(nm_in[s], (n + 1) * 16)
                for j in range(UG):
                    G = u * UG + j
                    for f in range(FILLS):
                        if has_max:
                            max_fill(u + 2, sv, j, f)
                        score_fill(G, s, j, f, first=(first and j == 0))
                        if f in (1, 2) and not (first and j == 0):
                            for quarter in (2 * f - 2, 2 * f - 1):
                                pv_part(G - 1, s if j > 0 else (s - 1) % 4, (j - 1) % UG, quarter)
                        if j == 0 and f == 1 and not last:
                            max_transpose(u + 1, (s + 1) % 2)
                        if f == 3 and not (first and j < 2):
                            attn_transpose(G - 2, j % 2, unit=(u + 1 if j == 0 and not last else None))

            for v in range(2):
                unit_ready(v, v, 0)
                for j in range(UG):
                    for f in range(FILLS):
                        max_fill(v, v, j, f, first=(v == 0))
                        if v == 1 and j == 0 and f == 1:
                            max_transpose(0, 0)
            pe.wait_ge(rest_done, KQ * (BLOCKS + 1))
            pe.wait_ge(v_free, BLOCKS + 1)
            pe.wait_ge(kones, 4)
            attn_step(0, 0, 0, first=True)
            with pe.Fori(0, 3) as i:
                for r in range(4):
                    attn_step(i * 4 + (1 + r), (1 + r) % 4, i + (1 + r) // 4)
            attn_step(13, 1, 3)
            attn_step(14, 2, 3, has_max=False)
            attn_step(15, 3, 3, has_max=False, last=True)
            LAST = UNITS * UG - 1
            for f in range(FILLS):
                pv_part(LAST, 3, UG - 1, f)
            attn_transpose(LAST - 1, 0)
            attn_transpose(LAST, 1)

            pe.wait_ge(attn_done, LAST + 1)
            pe.wait_ge(w_fc, 16)
            pe.wait_ge(w_gate, 16)

            def ot_transpose(t, s, n):
                pe.wait_ge(a_ld[s], n * 16 + 16)
                if not (isinstance(t, int) and t < 2):
                    pe.wait_ge(ota_evac, t - 1)
                for k in range(KD):
                    tr = nc.tensor.transpose(bank[s][:, k * P:(k + 1) * P], a_in[s][:, k * P:(k + 1) * P], ident[:])
                tr.then_inc(ota_ready, 1)

            def out_project(t, s):
                pe.wait_ge(ota_evac, t + 1)
                if not (isinstance(t, int) and t < 2):
                    pe.wait_ge(x2_done, t - 1)
                for k in range(KD):
                    mm = nc.tensor.matmul(bank[2 + s][:], oT[s][:, k, :], wfc_sb[:, k, :],
                                          start=(k == 0), stop=(k == KD - 1))
                mm.then_inc(fc_ready, 1)

            def ln_transpose(t, s):
                pe.wait_ge(ln2_done, t + 1)
                if not (isinstance(t, int) and t < 2):
                    pe.wait_ge(lnt_evac, t - 1)
                for k in range(KD):
                    tr = nc.tensor.transpose(bank[4 + s][:, k * P:(k + 1) * P], xn2_sb[s][:, k * P:(k + 1) * P],
                                             ident[:])
                tr.then_inc(lnt_ready, 1)

            def gate(t, s):
                pe.wait_ge(lnt_evac, t + 1)
                if not (isinstance(t, int) and t < 2):
                    pe.wait_ge(gate_evac, t - 1)
                for k in range(KD):
                    mm = nc.tensor.matmul(bank[6 + s][:, 0:NE], lnT[s][:, k * P:(k + 1) * P], gw_sb[:, k, :],
                                          start=(k == 0), stop=(k == KD - 1))
                mm.then_inc(gate_ready, 1)

            ot_transpose(0, 0, 0)
            for t in range(2):
                ot_transpose(t + 1, (t + 1) % 2, (t + 1) // 2)
                out_project(t, t)
            for t in range(2, 4):
                ln_transpose(t - 2, t % 2)
                ot_transpose(t + 1, (t + 1) % 2, (t + 1) // 2)
                out_project(t, t % 2)
                gate(t - 2, t % 2)
            with pe.Fori(2, TILES // 2 - 1) as i:
                for s in range(2):
                    ln_transpose(i * 2 + s - 2, s)
                    ot_transpose(i * 2 + (s + 1), 1 - s, i + (s + 1) // 2)
                    out_project(i * 2 + s, s)
                    gate(i * 2 + s - 2, s)
            for t in range(TILES - 2, TILES):
                ln_transpose(t - 2, t % 2)
                if t + 1 < TILES:
                    ot_transpose(t + 1, (t + 1) % 2, (t + 1) // 2)
                out_project(t, t % 2)
                gate(t - 2, t % 2)


            def h_transpose(w, par):
                pe.wait_ge(h_done, w + 1)
                if not (isinstance(w, int) and w == 0):
                    pe.wait_ge(ht_evac, w)
                for j, (f0, fs) in enumerate(FT):
                    tr = nc.tensor.transpose(bank[HT_BANK][0:fs, j * P:(j + 1) * P], h_sb[par][:, f0:f0 + fs], ident[:])
                tr.then_inc(ht_ready, 1)

            def gate_up(w, par, x_T, gu):
                if not (isinstance(w, int) and w < 2):
                    pe.wait_ge(h_done, w - 1)
                for which, ready in ((0, g_ready), (1, u_ready)):
                    for k in range(KD):
                        mm = nc.tensor.matmul(bank[GU_BANKS[par][which]][:, 0:F], x_T[:, k * P:(k + 1) * P],
                                              gu(k, which), start=(k == 0), stop=(k == KD - 1))
                    mm.then_inc(ready, 1)
                    if which == 0 and not (isinstance(w, int) and w == 0):
                        h_transpose(w - 1, 1 - par)

            def down(w, par, n, ypar, dn, begin=True, end=True):
                pe.wait_ge(ht_evac, w + 1)
                if begin and not (isinstance(n, int) and n < 2):
                    pe.wait_ge(y_evac, n - 1)
                for j, (f0, fs) in enumerate(FT):
                    mm = nc.tensor.matmul(bank[Y_BANKS[ypar]][:], hT[par][0:fs, j, :], dn(j, fs),
                                          start=(begin and j == 0), stop=(end and j == len(FT) - 1))
                mm.then_inc(dn_done, 1)

            def shared_gu(c):
                return lambda k, which: words(SHGU0 + c * GU_W + (2 * k + which) * F, F)

            def shared_dn(c):
                return lambda j, fs: words(SHDN0 + c * DN_W + j * D, D)[0:fs]

            def routed_gu(m):
                off = pe.value_load(gu_off[0:1, bass.ds(m, 1)], min_val=0, max_val=(NE - 1) * GU_W)
                return lambda k, which: weights[:, bass.ds(off + (GU0 + (2 * k + which) * F), F)]

            def routed_dn(m):
                off = pe.value_load(dn_off[0:1, bass.ds(m, 1)], min_val=0, max_val=(NE - 1) * DN_W)
                return lambda j, fs: weights[0:fs, bass.ds(off + (DN0 + j * D), D)]

            def early_up(t, s, n, c):
                if c == 0:
                    pe.wait_ge(sx_ld[s], n * 16 + 16)
                gate_up(t * 2 + c, c, first_xT[s] if isinstance(t, int) else xT[s], shared_gu(c))

            def early_down(t, s, c):
                down(t * 2 + c, c, t, s, shared_dn(c), begin=(c == 0), end=(c == 1))

            pe.wait_ge(ota_evac, TILES)
            pe.wait_ge(w_shared, 16 * 3 * SH)
            ln_transpose(TILES - 2, 0)
            early_up(0, 0, 0, 0)
            gate(TILES - 2, 0)
            pe.wait_ge(x2_done, TILES)
            ln_transpose(TILES - 1, 1)
            pe.wait_ge(gate_evac, TILES - 1)
            early_up(0, 0, 0, 1)
            gate(TILES - 1, 1)
            pe.wait_ge(gate_evac, TILES)
            early_down(0, 0, 0)
            early_up(1, 1, 0, 0)
            pe.wait_ge(sel_done, 1)
            flat = sel[:].rearrange("p t e -> p (t e)")
            nc.tensor.matmul(bank[XT_BANK][:, 0:P], tri[:], flat, start=True, stop=True)
            nc.tensor.matmul(bank[XT_BANK][:, P:2 * P], ones[:], flat, start=True, stop=True).then_inc(pre_ready, 1)
            early_down(0, 0, 1)
            early_up(1, 1, 0, 1)
            early_down(1, 1, 0)
            with pe.Fori(1, EARLY // 2) as i:
                for s in range(2):
                    early_up(i * 2 + s, s, i, 0)
                    early_down(i * 2 + s - 1, 1 - s, 1)
                    early_up(i * 2 + s, s, i, 1)
                    early_down(i * 2 + s, s, 0)

            pe.wait_ge(offs_done, 1)
            pe.wait_ge(w_routed, 16 * 4 * NE)

            def slot_transpose(m, s, n):
                pe.wait_ge(slot_ld[s], n * 16 + 16)
                if not (isinstance(m, int) and m == 0):
                    pe.wait_ge(xt_evac, m)
                for k in range(KD):
                    tr = nc.tensor.transpose(bank[XT_BANK][:, k * P:(k + 1) * P], slot_in[s][:, k * P:(k + 1) * P],
                                             ident[:])
                tr.then_inc(xt_ready, 1)

            def slot_up(m, s):
                pe.wait_ge(xt_evac, m + 1)
                gate_up(m + B0, s, xT[s], routed_gu(m))

            def slot_down(m, s):
                down(m + B0, s, m + YB0, (YB0 + s) % 2, routed_dn(m))

            pe.wait_ge(slots_done, 1)
            slot_transpose(0, 0, 0)
            slot_up(0, 0)
            early_down(EARLY - 1, (EARLY - 1) % 2, 1)
            slot_transpose(1, 1, 0)
            with pe.Fori(0, (SLOTS - 3) // 2) as i:
                for r in range(2):
                    m = i * 2 + (1 + r)
                    slot_transpose(m + 1, r, i + 1)
                    slot_up(m, 1 - r)
                    slot_down(m - 1, r)
            m = SLOTS - 2
            slot_transpose(m + 1, (m + 1) % 2, (m + 1) // 2)
            slot_up(m, m % 2)
            slot_down(m - 1, (m - 1) % 2)
            slot_up(m + 1, (m + 1) % 2)
            slot_down(m, m % 2)

            def late_up(m, s, n, c):
                if c == 0:
                    pe.wait_ge(sx_ld[s], n * 16 + (16 * EARLY // 2 + 16))
                gate_up(m * 2 + (C0 + c), (C0 + c) % 2, xT[s], shared_gu(c))

            def late_down(m, s, c):
                down(m * 2 + (C0 + c), (C0 + c) % 2, m + YC0, s, shared_dn(c), begin=(c == 0), end=(c == 1))

            late_up(0, 1, 0, 0)
            slot_down(SLOTS - 1, (SLOTS - 1) % 2)
            late_up(0, 1, 0, 1)
            late_down(0, YC0 % 2, 0)
            late_up(1, 0, 0, 0)
            late_down(0, YC0 % 2, 1)
            late_up(1, 0, 0, 1)
            late_down(1, (YC0 + 1) % 2, 0)
            with pe.Fori(1, (TILES - EARLY) // 2) as i:
                for r in range(2):
                    m = i * 2 + r
                    late_up(m, (r + 1) % 2, i, 0)
                    late_down(m - 1, (YC0 + r + 1) % 2, 1)
                    late_up(m, (r + 1) % 2, i, 1)
                    late_down(m, (YC0 + r) % 2, 0)
            h_transpose(C0 + PC - 1, (C0 + PC - 1) % 2)
            late_down(TILES - EARLY - 1, (YC0 + TILES - EARLY - 1) % 2, 1)

        @block.vector
        def _(dve):
            def chain(start):
                count = [0]

                def link(ins, relay=False):
                    count[0] += 1
                    ins.then_inc(step, 1)
                    dve.wait_ge(step, start + count[0])
                    if relay:
                        dve.sem_inc(dve_passed, 1)
                link.count = count
                return link

            def newton(link, n):
                v, sd, a, b, r = var_e[:, 0:n], std[:, 0:n], rs_a[:, 0:n], rs_b[:, 0:n], rstd[:, 0:n]
                link(nc.vector.reciprocal(a, sd))
                link(nc.vector.tensor_tensor(b, a, a, ALU.mult))
                link(nc.vector.tensor_tensor(b, b, v, ALU.mult))
                link(nc.vector.tensor_scalar(b, b, -0.5, 1.5, ALU.mult, ALU.add))
                link(nc.vector.tensor_tensor(r, a, b, ALU.mult))

            dve.sem_inc(xT_free, 2)
            dve.sem_inc(rest_done, KQ)
            dve.sem_inc(v_free, 1)
            for stored in attn_st + x2_stored + xn2_stored + y_st:
                dve.sem_inc(stored, FREE)
            LN_STEPS = 7

            with dve.Fori(0, BLOCKS // 2) as i:
                for s in range(2):
                    n = i * 2 + s
                    link = chain(n * LN_STEPS)
                    dve.wait_ge(x_ld[s], i * 16 + 16)
                    for a in range(TPB):
                        st = nc.vector.bn_stats(stats[:, a, :], x_in[s][:, a, :])
                    link(st, relay=True)
                    for a in range(TPB):
                        st = nc.vector.bn_aggr(mv[:, a, :], stats[:, a, :])
                    link(st)
                    nc.vector.tensor_scalar(var_e[:], mv[:, :, 1], EPS, None, ALU.add).then_inc(var_done, 1)
                    dve.wait_ge(std_done, n + 1)
                    newton(link, TPB)
                    for a in range(TPB):
                        nc.vector.tensor_scalar(x_in[s][:, a, :], x_in[s][:, a, :], mv[:, a, 0:1], rstd[:, a:a + 1],
                                                ALU.subtract, ALU.mult).then_inc(ln_done, 1)
                    for l in range(KQ):
                        par = (KQ * s + l) % 2
                        dve.wait_ge(part1, n * KQ + (l + 1))
                        nc.vector.tensor_tensor(rest[par], bank[l][:], parts[par][:, 0, :],
                                                ALU.subtract).then_inc(rest_done, 1)

            links = BLOCKS * LN_STEPS

            def reduce(v, par, j, f):
                qt, pair = f // 2, f % 2
                dve.wait_ge(max_ready, v * (FILLS * UG) + (FILLS * j + f + 1))
                nc.vector.tensor_reduce(mx[par][:, HPG * j + 2 * pair:HPG * j + 2 * pair + 2, qt:qt + 1],
                                        bank[f % 2][:].rearrange("p (c k) -> p c k", c=2), AX.X,
                                        ALU.max).then_inc(max_done, 1)

            def neg_max_part(v, par, n):
                dve.wait_ge(mxt_ready, v + 1)
                if not (isinstance(n, int) and n == 0):
                    dve.wait_ge(nm_out[par], n * 16)
                nc.vector.tensor_scalar(nm[par][:, 0, :], bank[7][0:2 * UH, MXT:MXT + P], -1.0, None,
                                        ALU.mult).then_inc(nm_first, 1)
                dve.wait_ge(nm_first, v + 1)
                nc.vector.scalar_tensor_tensor(nm_rest[par], bank[7][0:2 * UH, MXT:MXT + P], -1.0, nm[par][:, 0, :],
                                               ALU.mult, ALU.subtract).then_inc(nm_rest_done, 1)

            def normalise(G, half, b, j):
                dve.wait_ge(ot_ready, G + 1)
                if j == 0:
                    dve.wait_ge(attn_st[half], b * 16 + FREE)
                src = bank[7][:, 0:2 * P].rearrange("p (q h c) -> p q h c", q=2, c=VW)
                nc.vector.reciprocal(o_rec, src[:, :, :, HD]).then_inc(rec_done, 1)
                dve.wait_ge(rec_done, G + 1)
                nc.vector.tensor_tensor(
                    attn_u[half][:, :, j * HPG * HD:(j + 1) * HPG * HD].rearrange("p q (h d) -> p q h d", d=HD),
                    src[:, :, :, 0:HD], o_rec.unsqueeze(3).broadcast_to([P, 2, HPG, HD]),
                    ALU.mult).then_inc(attn_done, 1)

            def attn_step(u, par, n, has_max=True, first=False, last=False):
                for j in range(UG):
                    for f in range(FILLS):
                        if has_max:
                            reduce(u + 2, par, j, f)
                        if f == 0 and not (first and j < 3):
                            if j < 3:
                                normalise(u * UG + (j - 3), 1 - par, n - 1 + par, j + 1)
                            else:
                                normalise(u * UG, par, n, 0)
                        if j == 0 and f == 2 and not last:
                            neg_max_part(u + 1, 1 - par, n + par)

            for v in range(2):
                for j in range(UG):
                    for f in range(FILLS):
                        reduce(v, v, j, f)
                        if v == 1 and j == 0 and f == 1:
                            neg_max_part(0, 0, 0)
            attn_step(0, 0, 0, first=True)
            with dve.Fori(0, 3) as i:
                for r in range(4):
                    attn_step(i * 4 + (1 + r), (1 + r) % 2, i * 2 + (1 + r) // 2)
            attn_step(13, 1, 6)
            attn_step(14, 0, 7, has_max=False)
            attn_step(15, 1, 7, has_max=False, last=True)
            for G in range(UNITS * UG - 3, UNITS * UG):
                normalise(G, 1, 7, G % UG)

            def residual_norm(t, s, n):
                link = chain(t * 7 + links)
                dve.wait_ge(fc_ready, t + 1)
                dve.wait_ge(xb_done, t + 1)
                dve.wait_ge(x2_stored[s], n * 16 + FREE)
                nc.vector.tensor_tensor(x2_sb[s], bank[2 + s][:], res_in[s], ALU.add).then_inc(x2_done, 1)
                dve.wait_ge(x2_done, t + 1)
                link(nc.vector.bn_stats(stats[:, 0, :], x2_sb[s]), relay=True)
                link(nc.vector.bn_aggr(mv[:, 0, :], stats[:, 0, :]))
                nc.vector.tensor_scalar(var_e[:, 0:1], mv[:, 0, 1:2], EPS, None, ALU.add).then_inc(var2_done, 1)
                dve.wait_ge(std2_done, t + 1)
                newton(link, 1)
                dve.wait_ge(xn2_stored[s], n * 16 + FREE)
                nc.vector.tensor_scalar(xn2_sb[s], x2_sb[s], mv[:, 0, 0:1], rstd[:, 0:1],
                                        ALU.subtract, ALU.mult).then_inc(ln2_done, 1)

            with dve.Fori(0, TILES // 2) as i:
                for s in range(2):
                    residual_norm(i * 2 + s, s, i)

            link = route_link = chain(links + 7 * TILES)

            def bc(ap, axis, n):
                shape = list(ap.shape)
                return ap.unsqueeze(axis).broadcast_to(shape[:axis] + [n] + shape[axis:])

            def hidden(w, par):
                dve.wait_ge(u_ready, w + 1)
                dve.wait_ge(sil_done, w + 1)
                if not (isinstance(w, int) and w < 2):
                    dve.wait_ge(ht_ready, w - 1)
                nc.vector.tensor_tensor(h_sb[par][:], bank[GU_BANKS[par][1]][:, 0:F], sil[par][:],
                                        ALU.mult).then_inc(h_done, 1)

            def softmax():
                dve.wait_ge(gate_evac, TILES)
                link(nc.vector.tensor_reduce(t_tile[:, 0, :], logits[:], AX.X, ALU.max))
                nc.vector.tensor_tensor(score[:], logits[:], bc(t_tile[:, 0, :], 2, NE), ALU.subtract).then_inc(soft_in, 1)
                dve.wait_ge(soft_exp, 1)
                link(nc.vector.tensor_reduce(t_tile[:, 1, :], score[:], AX.X, ALU.add))
                link(nc.vector.reciprocal(t_tile[:, 2, :], t_tile[:, 1, :]))
                link(nc.vector.tensor_tensor(score[:], score[:], bc(t_tile[:, 2, :], 2, NE), ALU.mult))

            def rank(out_, val, n):
                before = cmp_a[:, 0:TILES * n * n].rearrange("p (t i j) -> p t i j", t=TILES, i=n)
                equal = cmp_b[:, 0:TILES * n * n].rearrange("p (t i j) -> p t i j", t=TILES, i=n)
                nc.vector.tensor_tensor(before, bc(val, 2, n), bc(val, 3, n), ALU.is_gt)
                link(nc.vector.tensor_tensor(equal, bc(val, 2, n), bc(val, 3, n), ALU.is_equal))
                left = lower[:, 0:n, 0:n]
                link(nc.vector.tensor_tensor(equal, equal, bc(left, 1, TILES), ALU.mult))
                link(nc.vector.tensor_tensor(before, before, equal, ALU.add))
                link(nc.vector.tensor_reduce(out_, before, AX.X, ALU.add))

            def choose():
                for s in range(2):
                    dve.wait_ge(xn2_stored[s], FREE + 16 * TILES // 2)
                    dve.wait_ge(lnt_stored[s], FREE + 16 * TILES // 2)
                link(nc.vector.tensor_reduce(gmax[:], score[:].rearrange("p t (g e) -> p t g e", e=2), AX.X, ALU.max))
                rank(grank[:], gmax[:], NE // 2)
                link(nc.vector.tensor_scalar(grank[:], grank[:], 2.0, None, ALU.is_lt))
                link(nc.vector.tensor_tensor(score[:].rearrange("p t (g e) -> p t g e", e=2),
                                             score[:].rearrange("p t (g e) -> p t g e", e=2),
                                             bc(grank[:], 3, 2), ALU.mult))
                rank(pos[:], score[:], NE)
                nc.vector.tensor_scalar(sel[:], pos[:], 2.0, None, ALU.is_lt).then_inc(sel_done, 1)
                dve.wait_ge(sel_done, 1)
                link(nc.vector.tensor_tensor(wsel[:], score[:], sel[:], ALU.mult))

            def place():
                dve.wait_ge(pre_ready, 1)
                pre = bank[XT_BANK][:, 0:P].rearrange("p (t e) -> p t e", t=TILES)
                tot = bank[XT_BANK][:, P:2 * P].rearrange("p (t e) -> p t e", t=TILES)
                link(nc.vector.tensor_copy(run_a[:], tot))
                src, dst, d = run_a, run_b, 1
                while d < TILES:
                    nc.vector.tensor_copy(dst[:, 0:d, :], src[:, 0:d, :])
                    link(nc.vector.tensor_tensor(dst[:, d:, :], src[:, d:, :], src[:, 0:TILES - d, :], ALU.add))
                    src, dst, d = dst, src, 2 * d
                full = cmp_a[:, 0:NE * TILES].rearrange("p (e t) -> p e t", e=NE)
                link(nc.vector.tensor_scalar(run_c[:], iota_f[:, 0:TILES], float(P), None, ALU.mult))
                link(nc.vector.tensor_tensor(full, bc(src[:, TILES - 1, :], 2, TILES), bc(run_c[:], 1, NE), ALU.is_gt))
                link(nc.vector.tensor_reduce(cnt[:, 0, :], full, AX.X, ALU.add))
                link(nc.vector.tensor_copy(cnt[:, 1, :], cnt[:, 0, :]))
                a, b, d = 1, 2, 1
                while d < NE:
                    nc.vector.tensor_copy(cnt[:, b, 0:d], cnt[:, a, 0:d])
                    link(nc.vector.tensor_tensor(cnt[:, b, d:], cnt[:, a, d:], cnt[:, a, 0:NE - d], ALU.add))
                    a, b, d = b, a, 2 * d
                link(nc.vector.tensor_tensor(cnt[:, 3, :], cnt[:, a, :], cnt[:, 0, :], ALU.subtract))
                link(nc.vector.tensor_scalar(cnt[:, 3, :], cnt[:, 3, :], float(P), None, ALU.mult))
                link(nc.vector.tensor_tensor(pos[:], src[:], tot, ALU.subtract))
                link(nc.vector.tensor_tensor(pos[:], pos[:], pre, ALU.add))
                link(nc.vector.tensor_tensor(pos[:], pos[:], bc(cnt[:, 3, :], 1, TILES), ALU.add))
                link(nc.vector.tensor_tensor(pos[:], pos[:], sel[:], ALU.mult))
                nc.vector.tensor_reduce(t_tile[:, 0, :], pos[:], AX.X, ALU.max)
                link(nc.vector.tensor_reduce(t_tile[:, 1, :], pos[:], AX.X, ALU.add))
                link(nc.vector.tensor_tensor(t_tile[:, 2, :], t_tile[:, 1, :], t_tile[:, 0, :], ALU.subtract))
                nc.vector.tensor_copy(p1_i[:], t_tile[:, 0, :])
                nc.vector.tensor_copy(p2_i[:], t_tile[:, 2, :]).then_inc(slots_done, 1)
                link(nc.vector.tensor_tensor(run_a[:], pos[:], bc(t_tile[:, 0, :], 2, NE), ALU.is_equal))
                link(nc.vector.tensor_tensor(run_a[:], run_a[:], wsel[:], ALU.mult))
                nc.vector.tensor_reduce(w1[:], run_a[:], AX.X, ALU.add)
                link(nc.vector.tensor_tensor(run_b[:], wsel[:], run_a[:], ALU.subtract))
                link(nc.vector.tensor_reduce(w2[:], run_b[:], AX.X, ALU.add))
                ends = bc(cnt[:, a, :], 1, SLOTS + 1)
                cmp_e = tile_cmp[:].rearrange("p (m e) -> p m e", e=NE)
                link(nc.vector.tensor_tensor(cmp_e, bc(iota_f[:], 2, NE), ends, ALU.is_ge))
                link(nc.vector.tensor_reduce(slot_e[:, 0, :], cmp_e, AX.X, ALU.add))
                link(nc.vector.tensor_scalar(slot_e[:, 0, :], slot_e[:, 0, :], float(NE - 1), None, ALU.min))
                nc.vector.tensor_scalar(gu_off[:], slot_e[:, 0, :], float(GU_W), None, ALU.mult)
                nc.vector.tensor_scalar(dn_off[:], slot_e[:, 0, :], float(DN_W), None, ALU.mult).then_inc(offs_done, 1)

            def early_sum(t, s, n):
                dve.wait_ge(dn_done, t * 2 + 2)
                dve.wait_ge(x2_ld[s], n * 16 + 16)
                nc.vector.tensor_tensor(tok_in[s], bank[Y_BANKS[s]][:], tok_in[s], ALU.add).then_inc(y_evac, 1)

            hidden(0, 0)
            hidden(1, 1)
            softmax()
            choose()
            hidden(2, 0)
            place()
            early_sum(0, 0, 0)
            hidden(3, 1)
            with dve.Fori(1, EARLY // 2) as i:
                for s in range(2):
                    hidden(i * 4 + 2 * s, 0)
                    early_sum(i * 2 + s - 1, 1 - s, i + s - 1)
                    hidden(i * 4 + (2 * s + 1), 1)

            def slot_evac(m, s):
                dve.wait_ge(xt_ready, m + 1)
                dve.wait_ge(u_ready, m + (B0 - 1))
                nc.vector.tensor_copy(xT[s], bank[XT_BANK][:]).then_inc(xt_evac, 1)

            def slot_result(m, s, n):
                dve.wait_ge(dn_done, m + (B0 + 1))
                dve.wait_ge(y_st[s], n * 16 + FREE)
                nc.vector.tensor_copy(mid[s], bank[Y_BANKS[(YB0 + s) % 2]][:]).then_inc(y_evac, 1)

            for buf in range(4):
                dve.wait_ge(sc_st[buf], 32 * TILES // 4)
            slot_evac(0, 0)
            hidden(B0, 0)
            early_sum(EARLY - 1, 1, EARLY // 2 - 1)
            slot_evac(1, 1)
            with dve.Fori(0, (SLOTS - 3) // 2) as i:
                for r in range(2):
                    m = i * 2 + (1 + r)
                    slot_evac(m + 1, r)
                    hidden(m + B0, 1 - r)
                    slot_result(m - 1, r, i)
            m = SLOTS - 2
            slot_evac(m + 1, (m + 1) % 2)
            hidden(m + B0, m % 2)
            slot_result(m - 1, (m - 1) % 2, (m - 1) // 2)
            hidden(m + 1 + B0, (m + 1) % 2)
            slot_result(m, m % 2, m // 2)

            def early_out(m, base_):
                dve.wait_ge(cx2_ld[0], m * 16 + 16)
                dve.wait_ge(gat_ld[0], m * 32 + 32)
                dve_link = chain(base_)
                dve_link(nc.vector.scalar_tensor_tensor(tok_in[0], mid[0], w1[:, bass.ds(m, 1)], tok_in[0],
                                                        ALU.mult, ALU.add))
                nc.vector.scalar_tensor_tensor(late[0], late[0], w2[:, bass.ds(m, 1)], tok_in[0],
                                               ALU.mult, ALU.add).then_inc(out_done, 1)

            def late_out(m, ypar, base_):
                dve.wait_ge(cx2_ld[1], m * 16 + 16)
                dve.wait_ge(dn_done, m * 2 + (C0 + 2))
                nc.vector.tensor_tensor(tok_in[1], bank[Y_BANKS[ypar]][:], tok_in[1], ALU.add).then_inc(y_evac, 1)
                dve.wait_ge(y_evac, m + (YC0 + 1))
                dve.wait_ge(gat_ld[1], m * 32 + 32)
                dve_link = chain(base_)
                dve_link(nc.vector.scalar_tensor_tensor(tok_in[1], mid[1], w1[:, bass.ds(m + EARLY, 1)], tok_in[1],
                                                        ALU.mult, ALU.add))
                nc.vector.scalar_tensor_tensor(late[1], late[1], w2[:, bass.ds(m + EARLY, 1)], tok_in[1],
                                               ALU.mult, ALU.add).then_inc(out_done, 1)

            links4 = links + 7 * TILES + route_link.count[0]
            hidden(C0, C0 % 2)
            slot_result(SLOTS - 1, (SLOTS - 1) % 2, (SLOTS - 1) // 2)
            hidden(C0 + 1, (C0 + 1) % 2)
            hidden(C0 + 2, C0 % 2)
            early_out(0, links4)
            late_out(0, YC0 % 2, links4 + 1)
            hidden(C0 + 3, (C0 + 1) % 2)
            with dve.Fori(1, (TILES - EARLY) // 2) as i:
                for r in range(2):
                    m = i * 2 + r
                    hidden(m * 2 + C0, C0 % 2)
                    early_out(m - 1, (m - 1) * 2 + links4)
                    late_out(m - 1, (YC0 + r + 1) % 2, (m - 1) * 2 + (links4 + 1))
                    hidden(m * 2 + (C0 + 1), (C0 + 1) % 2)
            m = TILES - EARLY - 1
            early_out(m, m * 2 + links4)
            late_out(m, (YC0 + m) % 2, m * 2 + links4 + 1)


def _inputs(x, ctx, Wq, Wk, Wv, Wfc, bfc, gate, gate_w, up_w, down_w, sh_gate, sh_up, sh_down):
    import numpy as np

    def contraction_first(w):
        return np.ascontiguousarray(w.T.reshape(KD, P, -1).transpose(1, 0, 2))

    ctxT = np.ascontiguousarray(ctx.reshape(T, D).T.reshape(KD, P, BLOCKS, BT).transpose(2, 1, 0, 3))
    gates = np.concatenate([gate_w, sh_gate.reshape(SH, F, D)])
    ups = np.concatenate([up_w, sh_up.reshape(SH, F, D)])
    gu = np.stack([gates, ups], 1)
    gu = gu.reshape(NE + SH, 2, F, KD, P).transpose(0, 4, 3, 1, 2).reshape(NE + SH, P, GU_W)
    downs = np.concatenate([down_w, sh_down.reshape(D, SH, F).transpose(1, 0, 2)]).transpose(0, 2, 1)
    dn = downs[:, 0:2 * P].reshape(NE + SH, 2, P, D).transpose(0, 2, 1, 3).reshape(NE + SH, P, 2 * D)
    return {
        "x": np.ascontiguousarray(x.reshape(T, D)), "ctxT": ctxT, "wqT": contraction_first(Wq),
        "wkvT": np.ascontiguousarray(np.concatenate([contraction_first(Wk), contraction_first(Wv)], 2)),
        "wfcT": contraction_first(Wfc), "bfc": np.ascontiguousarray(bfc), "gwT": contraction_first(gate),
        "wgu": np.ascontiguousarray(gu), "wdn": np.ascontiguousarray(dn),
        "wdt": np.ascontiguousarray(downs[:, 2 * P:F]),
    }


def kernel(x, ctx_2048, L0_xattn_Wq, L0_xattn_Wk, L0_xattn_Wv, L0_xattn_Wfc, L0_xattn_bfc, L0_ffn_gate_weight,
           L0_ffn_gate_w, L0_ffn_up_w, L0_ffn_down_w, L0_ffn_sh_gate_w, L0_ffn_sh_up_w, L0_ffn_sh_down_w):
    import numpy as np
    import concourse.bacc as bacc
    from concourse.bass_utils import run_bass_kernel_spmd

    given = [np.asarray(a) for a in (x, ctx_2048, L0_xattn_Wq, L0_xattn_Wk, L0_xattn_Wv, L0_xattn_Wfc, L0_xattn_bfc,
                                     L0_ffn_gate_weight, L0_ffn_gate_w, L0_ffn_up_w, L0_ffn_down_w,
                                     L0_ffn_sh_gate_w, L0_ffn_sh_up_w, L0_ffn_sh_down_w)]
    arrays = {"in_" + k: v for k, v in _inputs(*given).items()}
    nc = bacc.Bacc("TRN2", target_bir_lowering=False, num_devices=1)
    args = [nc.dram_tensor(k, v.shape, mybir.dt.from_np(v.dtype), kind="ExternalInput").ap() for k, v in arrays.items()]
    out = nc.dram_tensor("out", (T, D), F32, kind="ExternalOutput").ap()
    build(nc, *args, out)
    got = run_bass_kernel_spmd(nc, [arrays], core_ids=[0])
    return got.results[0]["out"].reshape(BATCH, SEQ, D)
```

```python
from contextlib import ExitStack

import concourse.bass as bass
from concourse import mybir

F32 = mybir.dt.float32
BF16 = mybir.dt.bfloat16
I32 = mybir.dt.int32
F16 = mybir.dt.float16
ALU = mybir.AluOpType
ACT = mybir.ActivationFunctionType
AX = mybir.AxisListType

P = 128
D = 512
KD = D // P
BATCH, SEQ = 8, 256
T = BATCH * SEQ
TILES = T // P
HEADS, GROUPS, HD = 32, 8, 16
HPG = HEADS // GROUPS
SCALE = HD ** -0.5
EPS = 1e-5
NE, F = 8, 352
SH = 2
FT = [(0, 128), (128, 128), (256, 96)]
GU_W = KD * 2 * F
HALF = GU_W // 2
CUTS = 2 * (NE + SH)
X_SCALE = 1024.0
TOP_EXP = 14
DN_W = len(FT) * D
SLOTS = 2 * T // P + NE - 1
BLOCKS, BT = 4, 512
TPB = BT // P
KQ = 1 + KD
PARTS_Q = (0, 0, 1, 1, 0, 2)
PARTS_K = (0, 1, 0, 1, 2, 0)
STACK = len(PARTS_Q) * HD
ROWS = STACK + 3
UH = HEADS // 2
UG = UH // HPG
UNITS = 2 * BATCH
FILLS = 4
VW = 32
FREE = 16
HELD = 5
CUTS_P2 = CUTS - 2 * HELD
EARLY = TILES // 2
PA, PB, PC = SH * EARLY, SLOTS, SH * (TILES - EARLY)


def build(nc, x, ctxT, wqT, wkvT, wfcT, bfc, gwT, wgu, wdn, wdt, out):
    def dram(name, shape, dt=F32):
        return nc.dram_tensor(name, shape, dt, kind="Internal").ap()

    q_parts = dram("q_parts", (3, D, T), BF16)
    k_parts = dram("k_parts", (3, P, T), BF16)
    v_dram = dram("v_dram", (TILES, P, GROUPS * VW))
    v_blocks = v_dram.rearrange("(n a) p c -> n p a c", a=TPB)
    neg_max = dram("neg_max", (UNITS, 3, 2 * UH, P), BF16)
    attn_dram = dram("attn_dram", (BATCH, 2, P, D))
    x2_dram = dram("x2_dram", (TILES, P, D))
    xn2_dram = dram("xn2_dram", (TILES, P, D))
    xnT_dram = dram("xnT_dram", (TILES, P, 2 * D), F16)
    slot_x = dram("slot_x", (SLOTS * P, D))
    slot_y = dram("slot_y", (SLOTS * P, D))
    x_blocks = x.rearrange("(n a p) d -> n p a d", a=TPB, p=P)
    x_tiles = x.rearrange("(t p) d -> t p d", p=P)
    out_tiles = out.rearrange("(t p) d -> t p d", p=P)
    slot_x_tiles = slot_x.rearrange("(t p) d -> t p d", p=P)
    slot_y_tiles = slot_y.rearrange("(t p) d -> t p d", p=P)

    with ExitStack() as ctx:
        def sb(name, shape, dt=F32):
            return ctx.enter_context(nc.sbuf_tensor("sb_" + name, shape, dt))

        def sem(name):
            return ctx.enter_context(nc.semaphore(name))

        bank = [ctx.enter_context(nc.psum_tensor(f"bank{i}", [P, 512], F32)) for i in range(8)]

        weights = sb("weights", [P, (NE + SH) * (GU_W + DN_W)])
        GU0, DN0 = 0, NE * GU_W
        SHGU0 = NE * (GU_W + DN_W)
        SHDN0 = SHGU0 + SH * GU_W

        def words(at, n):
            return weights[:, at:at + n]

        weights16 = weights[:].bitcast(F16)

        def cut_place(h):
            e = h // 2
            at = 2 * (GU0 + e * GU_W if e < NE else SHGU0 + (e - NE) * GU_W) + h % 2 * HALF
            return weights16[:, at:at + HALF], weights16[:, at + GU_W:at + GU_W + HALF]

        q_words, k_words, v_words, p_words = UH * SEQ // 2, UG * SEQ // 2, 2 * UG * VW, 2 * HPG * SEQ
        P3_0 = SHGU0 - (KD * D + 4 * D + D)
        at = 0
        q_st = [words(at + s * q_words, q_words).bitcast(BF16).rearrange("p (h t) -> p h t", h=UH) for s in range(4)]
        at += 4 * q_words
        probs = [words(at + s * p_words, p_words).rearrange("p (k n) -> p k n", k=2) for s in range(2)]
        at += 2 * p_words
        P1_0 = at
        assert at <= GU0 + HELD * GU_W
        at = DN0 + (NE - HELD) * DN_W
        KV_0 = at
        k_st = [words(at + s * k_words, k_words).bitcast(BF16).rearrange("p (g t) -> p g t", g=UG) for s in range(4)]
        at += 4 * k_words
        v_st = [words(at + s * v_words, v_words).rearrange("p (k g c) -> p k g c", k=2, g=UG) for s in range(4)]
        at += 4 * v_words
        assert at <= P3_0
        x_in = [words(at + s * TPB * D, TPB * D).rearrange("p (a d) -> p a d", a=TPB) for s in range(2)]
        at += 2 * TPB * D
        xnT = [words(at + s * KD * BT, KD * BT).rearrange("p (k t) -> p k t", k=KD) for s in range(2)]
        at += 2 * KD * BT
        cxT = [words(at + s * KD * BT, KD * BT).rearrange("p (k t) -> p k t", k=KD) for s in range(2)]
        at += 2 * KD * BT
        assert at <= SHGU0 + SH * (GU_W + DN_W)
        at = P1_0
        wq_sb = words(at, KD * D).rearrange("p (k n) -> p k n", k=KD)
        at += KD * D
        wkv_sb = words(at, KD * 2 * P).rearrange("p (k n) -> p k n", k=KD)
        at += KD * 2 * P
        parts = [words(at + s * 768, 768).bitcast(BF16).rearrange("p (s t) -> p s t", s=3) for s in range(3)]
        at += 3 * 768
        rest = [words(at + s * BT, BT) for s in range(3)]
        at += 3 * BT
        v_blk = [words(at + s * TPB * GROUPS * VW, TPB * GROUPS * VW)
                 .rearrange("p (a g c) -> p a g c", a=TPB, g=GROUPS) for s in range(2)]
        at += 2 * TPB * GROUPS * VW
        max_stage = [words(at + s * HALF, HALF) for s in range(2)]
        at += 2 * HALF
        assert at <= KV_0
        assert P1_0 + HALF <= GU0 + HELD * GU_W
        stage_p2 = [words(P1_0, HALF), words(P3_0 + KD * D, HALF)]
        stage_p3 = [words(KV_0 + s * HALF, HALF) for s in range(2)]
        assert KV_0 + 2 * HALF <= P3_0
        at = P3_0
        wfc_sb = words(at, KD * D).rearrange("p (k n) -> p k n", k=KD)
        at += KD * D
        a_in = [words(at + s * D, D) for s in range(2)]
        at += 2 * D
        oT = [words(at + s * D, D).rearrange("p (k t) -> p k t", k=KD) for s in range(2)]
        at += 2 * D
        bfc_sb = words(at, D)
        at += D
        assert at == SHGU0

        rows = sb("rows", [P, 8 * D])

        def row(i):
            return rows[:, i * D:(i + 1) * D]

        ident = sb("ident", [P, P])
        tri = sb("tri", [P, P])
        ones = sb("ones", [P, P])
        lower = sb("lower", [P, NE, NE])
        iota_f = sb("iota_f", [P, SLOTS + 1])
        gw_sb = sb("gw_sb", [P, KD, NE])
        zero_row = sb("zero_row", [P, D])
        ln16_sb = sb("ln16_sb", [P, D])
        half_max = sb("half_max", [P, CUTS])
        w_max = sb("w_max", [P, NE + SH])
        w_max_all = sb("w_max_all", [NE + SH, 1])
        w_exp = sb("w_exp", [P, NE + SH], I32)
        w_scale_i = sb("w_scale_i", [P, NE + SH], I32)
        w_inv_i = sb("w_inv_i", [P, NE + SH], I32)
        w_scale, w_inv = w_scale_i[:].bitcast(F32), w_inv_i[:].bitcast(F32)
        inv_slot = sb("inv_slot", [P, SLOTS + 1])
        inv_now = sb("inv_now", [P, 2])
        stats = sb("stats", [P, TPB, 6])
        mv = sb("mv", [P, TPB, 2])
        var_e = sb("var_e", [P, TPB])
        std = sb("std", [P, TPB])
        rs_a = sb("rs_a", [P, TPB])
        rs_b = sb("rs_b", [P, TPB])
        rstd = sb("rstd", [P, TPB])
        attn_u = [row(i).rearrange("p (q n) -> p q n", q=2) for i in range(2)]
        o_raw = [rows[:, 2 * D + s * SEQ:2 * D + (s + 1) * SEQ] for s in range(2)]
        mx = [rows[:, 3 * D + s * 2 * UH:3 * D + (s + 1) * 2 * UH].rearrange("p (h q) -> p h q", h=UH) for s in range(2)]
        o_rec = rows[:, 3 * D + 4 * UH:3 * D + 4 * UH + 2 * HPG].rearrange("p (q h) -> p q h", q=2)
        nm = [rows[0:2 * UH, 4 * D + s * 192:4 * D + (s + 1) * 192].bitcast(BF16)
              .rearrange("p (s t) -> p s t", s=3) for s in range(2)]
        nm_rest = [rows[0:2 * UH, 5 * D + s * P:5 * D + (s + 1) * P] for s in range(2)]
        MXT = 2 * P
        res_in, x2_sb, xn2_sb = [row(0), row(1)], [row(2), row(3)], [row(4), row(5)]
        lnT = [row(6), row(7)]
        ln16 = [zero_row[:].bitcast(F16), ln16_sb[:].bitcast(F16)]
        w_max_rows = row(6)[0:NE + SH, 0:P]
        tok_in, xT, mid, late = [row(0), row(1)], [row(2), row(3)], [row(4), row(5)], [row(6), row(7)]
        scatter_in = mid + late
        slot_in = late
        first_xT = [a.bitcast(F16) for a in a_in]
        xT = [x.bitcast(F16) for x in xT]
        late_xT = [x.bitcast(F16) for x in tok_in]
        gather_1, gather_2, res_out = [[words((4 * j + q) * D, D) for q in range(4)] for j in range(3)]
        cmp_a = rows[:, 4 * D:6 * D]
        cmp_b = rows[:, 6 * D:8 * D]
        h_sb = [sb(f"h{i}", [P, F]) for i in range(2)]
        sil = [sb(f"sil{i}", [P, F]) for i in range(2)]
        hT = [sb(f"hT{i}", [P, len(FT), P]) for i in range(2)]
        logits = sb("logits", [P, TILES, NE])
        score = sb("score", [P, TILES, NE])
        wsel = sb("wsel", [P, TILES, NE])
        sel = sb("sel", [P, TILES, NE])
        pos = sb("pos", [P, TILES, NE])
        run_a = sb("run_a", [P, TILES, NE])
        run_b = sb("run_b", [P, TILES, NE])
        t_tile = sb("t_tile", [P, 4, TILES])
        gmax = sb("gmax", [P, TILES, NE // 2])
        grank = sb("grank", [P, TILES, NE // 2])
        cnt = sb("cnt", [P, 6, NE])
        slot_e = sb("slot_e", [P, 1, SLOTS + 1])
        run_c = t_tile[:, 3, :]
        tile_cmp = sb("tile_cmp", [P, (SLOTS + 1) * NE])
        w1 = sb("w1", [P, TILES])
        w2 = sb("w2", [P, TILES])
        p1_i = sb("p1_i", [P, TILES], I32)
        p2_i = sb("p2_i", [P, TILES], I32)
        gu_off = sb("gu_off", [P, SLOTS + 1], I32)
        dn_off = sb("dn_off", [P, SLOTS + 1], I32)

        w_q, w_fc, w_gate = sem("w_q"), sem("w_fc"), sem("w_gate")
        w_shared, w_routed = sem("w_shared"), sem("w_routed")
        consts = sem("consts")
        zeroed = sem("zeroed")
        step = sem("step")
        pstep = sem("pstep")
        pool_passed, dve_passed = sem("pool_passed"), sem("dve_passed")
        x_ld = [sem(f"x_ld{s}") for s in range(2)]
        c_ld = [sem(f"c_ld{s}") for s in range(2)]
        c_first = [sem(f"c_first{k}") for k in range(KD)]
        var_done, std_done, ln_done = sem("var_done"), sem("std_done"), sem("ln_done")
        xT_ready, xT_free = sem("xT_ready"), sem("xT_free")
        kq_ready, v_ready, v_free = sem("kq_ready"), sem("v_ready"), sem("v_free")
        part1, rest_done, part3 = sem("part1"), sem("rest_done"), sem("part3")
        parts_st = [sem(f"parts_st{b}") for b in range(3)]
        v_st_dma = [sem(f"v_st_dma{s}") for s in range(2)]
        st_ld = [sem(f"st_ld{s}") for s in range(4)]
        kones = sem("kones")
        max_ready, max_done, mxt_ready = sem("max_ready"), sem("max_done"), sem("mxt_ready")
        ot_ready = sem("ot_ready")
        nm_first, nm_rest_done, nm_done, rec_done = sem("nm_first"), sem("nm_rest_done"), sem("nm_done"), sem("rec_done")
        nm_out = [sem(f"nm_out{s}") for s in range(2)]
        nm_in = [sem(f"nm_in{s}") for s in range(4)]
        st_ready, exp_done, pv_ready, pv_evac = sem("st_ready"), sem("exp_done"), sem("pv_ready"), sem("pv_evac")
        attn_done = sem("attn_done")
        attn_st = [sem(f"attn_st{s}") for s in range(2)]
        a_ld = [sem(f"a_ld{s}") for s in range(2)]
        r_ld = [sem(f"r_ld{s}") for s in range(2)]
        ota_ready, ota_evac, fc_ready, xb_done = sem("ota_ready"), sem("ota_evac"), sem("fc_ready"), sem("xb_done")
        x2_done, var2_done, std2_done, ln2_done = sem("x2_done"), sem("var2_done"), sem("std2_done"), sem("ln2_done")
        lnt_ready, lnt_evac, gate_ready, gate_evac = sem("lnt_ready"), sem("lnt_evac"), sem("gate_ready"), sem("gate_evac")
        x2_stored = [sem(f"x2_stored{s}") for s in range(2)]
        xn2_stored = [sem(f"xn2_stored{s}") for s in range(2)]
        lnt_stored = [sem(f"lnt_stored{s}") for s in range(2)]
        max_ld = [sem(f"max_ld{s}") for s in range(2)]
        half_max_done, w_max_done, w_max_t, w_max_b0, w_max_b, w_max_tt, scale_done = (
            sem("half_max_done"), sem("w_max_done"), sem("w_max_t"), sem("w_max_b0"), sem("w_max_b"), sem("w_max_tt"), sem("scale_done"))
        gu_ld = [sem(f"gu_ld{s}") for s in range(2)]
        gu_first, gu_scaled, gu_cut, gu_cut_v = sem("gu_first"), sem("gu_scaled"), sem("gu_cut"), sem("gu_cut_v")
        ln16_done, xt_first = sem("ln16_done"), sem("xt_first")
        soft_in, soft_exp, sel_done, pre_ready, slots_done, offs_done = (
            sem("soft_in"), sem("soft_exp"), sem("sel_done"), sem("pre_ready"), sem("slots_done"), sem("offs_done"))
        sc_ld = [sem(f"sc_ld{s}") for s in range(4)]
        sc_st = [sem(f"sc_st{s}") for s in range(4)]
        sx_ld = [sem(f"sx_ld{s}") for s in range(2)]
        x2_ld = [sem(f"x2_ld{s}") for s in range(2)]
        base_st = [sem(f"base_st{s}") for s in range(2)]
        g_ready, u_ready, sil_done, h_done = sem("g_ready"), sem("u_ready"), sem("sil_done"), sem("h_done")
        ht_ready, ht_evac, dn_done, y_evac = sem("ht_ready"), sem("ht_evac"), sem("dn_done"), sem("y_evac")
        slot_ld = [sem(f"slot_ld{s}") for s in range(2)]
        xt_ready, xt_evac = sem("xt_ready"), sem("xt_evac")
        y_st = [sem(f"y_st{s}") for s in range(2)]
        lx_ld = [sem(f"lx_ld{s}") for s in range(2)]
        cx2_ld = [sem(f"cx2_ld{q}") for q in range(4)]
        gat_ld = [sem(f"gat_ld{q}") for q in range(4)]
        out_done = sem("out_done")
        out_st = [sem(f"out_st{q}") for q in range(4)]

        B0, C0 = PA, PA + PB
        YB0, YC0 = EARLY, EARLY + SLOTS
        GU_BANKS = [(0, 1), (2, 3)]
        Y_BANKS = [4, 5]
        HT_BANK, XT_BANK = 6, 7

        def shared_inv(c):
            return w_inv[:, NE + c:NE + c + 1]

        block = ctx.enter_context(nc.Block())

        @block.sync
        def _(sp):
            def load_block(n):
                s = n % 2
                if n >= 2:
                    sp.wait_ge(v_ready, n - 1)
                if n == 0:
                    for k in range(KD):
                        sp.dma_start(wkv_sb[:, k, :], wkvT[:, k, :]).then_inc(c_first[k], 16)
                        sp.dma_start(cxT[s][:, k, :], ctxT[n, :, k, :]).then_inc(c_first[k], 16)
                else:
                    sp.dma_start(cxT[s], ctxT[n]).then_inc(c_ld[s], 16)
                if n >= 2:
                    sp.wait_ge(xT_ready, TPB * (n - 1))
                sp.dma_start(x_in[s], x_blocks[n]).then_inc(x_ld[s], 16)

            def load_half(h):
                if h >= 2:
                    sp.wait_ge(half_max_done, h - 1)
                sp.dma_start(max_stage[h % 2], wgu[h // 2, :, h % 2 * HALF:(h % 2 + 1) * HALF]).then_inc(max_ld[h % 2], 16)

            load_block(0)
            sp.dma_start(wq_sb, wqT).then_inc(w_q, 16)
            load_block(1)
            for h in range(2):
                load_half(h)
            def store_parts(n, l):
                sp.wait_ge(part3, KQ * n + l + 1)
                dst = k_parts if l == 0 else q_parts[:, (l - 1) * P:l * P]
                par = (KQ * n + l) % 3
                sp.dma_start(dst[:, :, n * BT:(n + 1) * BT].rearrange("s p t -> p s t"),
                             parts[par]).then_inc(parts_st[par], 16)

            def load_down(e):
                sp.dma_start(weights[:, bass.ds(e * DN_W + DN0, 2 * D)],
                             wdn[bass.ds(e, 1)].rearrange("o p n -> (o p) n")).then_inc(w_routed, 16)
                sp.dma_start(weights[0:FT[2][1], bass.ds(e * DN_W + (DN0 + 2 * D), D)],
                             wdt[bass.ds(e, 1)].rearrange("o p n -> (o p) n")).then_inc(w_routed, 16)

            def load_shared_dn(c):
                dn = SHDN0 + c * DN_W
                sp.dma_start(words(dn, 2 * D), wdn[NE + c]).then_inc(w_shared, 16)
                sp.dma_start(words(dn + 2 * D, D)[0:FT[2][1]], wdt[NE + c]).then_inc(w_shared, 16)

            def zero_slots(first, n):
                sp.dma_start(slot_x_tiles[bass.ds(first, n)].rearrange("t p d -> p t d"),
                             zero_row[:].unsqueeze(1).broadcast_to([P, n, D])).then_inc(zeroed, 16)

            def load_unit(b, half, s):
                for i in range(len(PARTS_Q)):
                    sp.dma_start(
                        q_st[s][HD * i:HD * (i + 1)],
                        q_parts[PARTS_Q[i], half * UH * HD:(half + 1) * UH * HD, bass.ds(b * SEQ, SEQ)]
                        .rearrange("(h d) t -> d h t", d=HD)).then_inc(st_ld[s], 16)
                    sp.dma_start(
                        k_st[s][HD * i:HD * (i + 1)],
                        k_parts[PARTS_K[i], half * UG * HD:(half + 1) * UG * HD, bass.ds(b * SEQ, SEQ)]
                        .rearrange("(g d) t -> d g t", d=HD)).then_inc(st_ld[s], 16)
                for kt in range(2):
                    sp.dma_start(v_st[s][:, kt, :, :].rearrange("p g c -> p (g c)"),
                                 v_dram[bass.ds(b * 2 + kt, 1), :, half * UG * VW:(half + 1) * UG * VW]
                                 .rearrange("o p c -> (o p) c")).then_inc(st_ld[s], 16)

            first_units = {(2, 1): (0,), (2, 3): (1,), (3, 4): (2,)}
            for n in range(BLOCKS):
                if n + 2 < BLOCKS:
                    load_block(n + 2)
                if n == 2:
                    for b in range(3):
                        sp.wait_ge(parts_st[b], FREE + 16 * len(range(b, KQ, 3)))
                    sp.wait_ge(v_st_dma[0], FREE + 16)
                for l in range(KQ):
                    store_parts(n, l)
                    if KQ * n + l + 2 < CUTS:
                        load_half(KQ * n + l + 2)
                    for u in first_units.get((n, l), ()):
                        load_unit(u // 2, u % 2, u)

            for s in range(2):
                sp.wait_ge(v_st_dma[s], FREE + 16 * BLOCKS // 2)
            for b in range(3):
                sp.wait_ge(parts_st[b], FREE + 16 * len(range(b, BLOCKS * KQ, 3)))
            sp.wait_ge(kq_ready, KQ * BLOCKS)

            def neg_max_rows(v, s, par, n):
                sp.wait_ge(nm_out[par], 16 * (n + 1))
                sp.dma_start(q_st[s][STACK:ROWS].rearrange("p h t -> p (h t)"),
                             neg_max[bass.ds(v, 1)].rearrange("o s r c -> (o s) (r c)")).then_inc(nm_in[s], 16)

            def store_attn(u, b, half, n):
                sp.wait_ge(attn_done, UG * (u + 1))
                sp.dma_start(attn_dram[bass.ds(b, 1), :, :, half * UG * HPG * HD:(half + 1) * UG * HPG * HD]
                             .rearrange("o q p c -> p (o q) c"), attn_u[half]).then_inc(attn_st[half], 16)

            sp.dma_start(wfc_sb, wfcT).then_inc(w_fc, 16)
            sp.dma_start(bfc_sb, bfc.partition_broadcast(P)).then_inc(w_fc, 16)
            sp.dma_start(gw_sb[:], gwT).then_inc(w_gate, 16)
            neg_max_rows(0, 0, 0, 0)
            load_unit(1, 1, 3)
            neg_max_rows(1, 1, 1, 0)
            load_shared_dn(0)
            sp.wait_ge(consts, 1)
            STEP_ZERO = SLOTS // 13
            zero_slots(0, STEP_ZERO)
            with sp.Fori(0, 3) as i:
                for r in range(4):
                    u = i * 4 + (1 + r)
                    sp.wait_ge(pv_ready, u * UG)
                    load_unit(i * 2 + (4 + r) // 2, r % 2, r % 4)
                    store_attn(i * 4 + r, i * 2 + r // 2, r % 2, None)
                    neg_max_rows(i * 4 + (2 + r), (2 + r) % 4, (2 + r) % 2, i * 2 + (2 + r) // 2)
                    zero_slots(i * (4 * STEP_ZERO) + (1 + r) * STEP_ZERO, STEP_ZERO)
                    if r == 1:
                        load_down(i)
            def load_attn(b, s):
                sp.dma_start(a_in[s], attn_dram[bass.ds(b, 1), s].rearrange("o p d -> (o p) d")).then_inc(a_ld[s], 16)

            def load_res_rows(b, s):
                sp.dma_start(res_in[s], x_tiles[bass.ds(b * 2 + s, 1)].rearrange("o p d -> (o p) d")).then_inc(r_ld[s], 16)

            for u in range(12, 16):
                if u == 15:
                    sp.wait_ge(attn_st[0], FREE + 16 * BATCH)
                    load_res_rows(0, 0)
                store_attn(u, u // 2, u % 2, None)
                if u < 14:
                    neg_max_rows(u + 2, (u + 2) % 4, u % 2, 7)
                if u == 13:
                    for s in range(2):
                        sp.wait_ge(attn_st[s], FREE + 16)
                    sp.wait_ge(gu_cut, CUTS_P2)
                    for s in range(2):
                        load_attn(0, s)
                if u == 12:
                    load_shared_dn(1)

            sp.wait_ge(attn_st[1], FREE + 16 * 2)
            sp.wait_ge(ota_ready, 1)
            load_attn(1, 0)
            sp.wait_ge(attn_st[1], FREE + 16 * BATCH)
            load_res_rows(0, 1)

            def tile_of(dram_tiles, t):
                return dram_tiles[bass.ds(t, 1)].rearrange("o p d -> (o p) d")

            def store_lnT(t, s):
                sp.wait_ge(ln16_done, t + 1)
                sp.dma_start(tile_of(xnT_dram, t), ln16[s]).then_inc(lnt_stored[s], 16)

            def store_x2(t, s):
                sp.wait_ge(x2_done, t + 1)
                sp.dma_start(tile_of(x2_dram, t), x2_sb[s]).then_inc(x2_stored[s], 16)

            def store_xn2(t, s):
                sp.wait_ge(ln2_done, t + 1)
                sp.dma_start(tile_of(xn2_dram, t), xn2_sb[s]).then_inc(xn2_stored[s], 16)

            for t in range(2):
                sp.wait_ge(ota_ready, t + 2)
                load_attn((t + 3) // 2, (t + 3) % 2)
                store_x2(t, t)
                load_res_rows(1, t)
                store_xn2(t, t)

            def token_tile(i, s, more=True):
                if more:
                    sp.wait_ge(ota_ready, i * 2 + (s + 2))
                    load_attn(i + (1 + s), 1 - s)
                store_lnT(i * 2 + s - 2, s)
                store_x2(i * 2 + s, s)
                load_res_rows(i + 1, s)
                store_xn2(i * 2 + s, s)

            LAST_PAIR = TILES // 2 - 2
            with sp.Fori(1, LAST_PAIR) as i:
                for s in range(2):
                    token_tile(i, s)
            token_tile(LAST_PAIR, 0)
            token_tile(LAST_PAIR, 1, more=False)
            for t in range(TILES - 2, TILES):
                store_lnT(t - 2, t % 2)
                store_x2(t, t % 2)
                sp.wait_ge(ota_ready, t + 1)
                sp.wait_ge(lnt_stored[t % 2], FREE + 16)
                sp.dma_start(first_xT[t % 2], xnT_dram[t % 2]).then_inc(sx_ld[t % 2], 16)
                store_xn2(t, t % 2)
            for t in range(TILES - 2, TILES):
                store_lnT(t, t % 2)

            for s in range(2):
                sp.wait_ge(lnt_stored[s], FREE + 16 * TILES // 2)
                sp.wait_ge(x2_stored[s], FREE + 16 * TILES // 2)
                sp.wait_ge(xn2_stored[s], FREE + 16 * TILES // 2)

            def load_shared(t, s):
                sp.dma_start(xT[s], tile_of(xnT_dram, t)).then_inc(sx_ld[s], 16)

            def load_res_x2(t, s):
                sp.dma_start(tok_in[s], tile_of(x2_dram, t)).then_inc(x2_ld[s], 16)

            def store_base(t, s):
                sp.wait_ge(y_evac, t + 1)
                sp.dma_start(tile_of(x2_dram, t), tok_in[s]).then_inc(base_st[s], 16)

            def load_slots(n, s):
                sp.dma_start(slot_in[s], tile_of(slot_x_tiles, n)).then_inc(slot_ld[s], 16)

            for t in range(2):
                load_res_x2(t, t)
                load_shared(t + 2, t)
            for t in range(EARLY):
                if t == 0:
                    sp.wait_ge(gu_cut, CUTS - HELD)
                    sp.wait_ge(gu_cut_v, HELD)
                if t < HELD:
                    load_down(NE - HELD + t)
                if t == EARLY - 1:
                    for buf in range(4):
                        sp.wait_ge(sc_st[buf], 32 * TILES // 4)
                    for s in range(2):
                        load_slots(s, s)
                    sp.wait_ge(xt_ready, 1)
                    load_slots(2, 0)
                store_base(t, t % 2)
                if t + 2 < EARLY:
                    sp.wait_ge(base_st[t % 2], 16 * (t // 2 + 1))
                    if t >= 2:
                        load_shared(t + 2, t % 2)
                    load_res_x2(t + 2, t % 2)

            def load_late(m, s):
                sp.dma_start(late_xT[s], tile_of(xnT_dram, m + EARLY)).then_inc(lx_ld[s], 16)

            for s in range(2):
                sp.wait_ge(base_st[s], 16 * EARLY // 2)
                load_late(s, s)

            def store_slots(n, s):
                sp.wait_ge(y_evac, YB0 + 1 + n)
                sp.dma_start(tile_of(slot_y_tiles, n), mid[s]).then_inc(y_st[s], 16)

            with sp.Fori(0, (SLOTS - 3) // 2) as i:
                for s in range(2):
                    sp.wait_ge(xt_ready, i * 2 + (s + 2))
                    load_slots(i * 2 + (s + 3), 1 - s)
                    store_slots(i * 2 + s, s)
            for n in range(SLOTS - 3, SLOTS - 1):
                store_slots(n, n % 2)

            store_slots(SLOTS - 1, (SLOTS - 1) % 2)

            def load_res(t, q):
                sp.dma_start(res_out[q], tile_of(x2_dram, t)).then_inc(cx2_ld[q], 16)

            def store_out(t, done, q):
                sp.wait_ge(out_done, done + 1)
                sp.dma_start(tile_of(out_tiles, t), gather_2[q]).then_inc(out_st[q], 16)

            for m in range(2):
                for s in range(2):
                    load_res(m + s * EARLY, 2 * m + s)
            with sp.Fori(0, EARLY // 2 - 1) as i:
                for r in range(2):
                    sp.wait_ge(u_ready, i * 4 + (C0 + 2 * r + 2))
                    load_late(i * 2 + (r + 2), r)
                    for s in range(2):
                        store_out(i * 2 + (r + s * EARLY), i * 4 + (2 * r + s), 2 * r + s)
                        load_res(i * 2 + (r + 2 + s * EARLY), 2 * r + s)
            for m in range(EARLY - 2, EARLY):
                for s in range(2):
                    store_out(m + s * EARLY, 2 * m + s, 2 * (m % 2) + s)
            for q in range(4):
                sp.wait_ge(out_st[q], 16 * EARLY // 2)

        @block.gpsimd
        def _(pool):
            def select(out_, pattern, op, base_, mult_):
                nc.gpsimd.affine_select(out=out_, in_=out_, compare_op=op, fill=0.0, base=base_,
                                        pattern=pattern, channel_multiplier=mult_).then_inc(pstep, 1)

            nc.gpsimd.memset(zero_row[:], 0.0).then_inc(consts, 1)
            for s in range(2):
                nc.gpsimd.memset(v_blk[s], 0.0)
            nc.gpsimd.memset(ident[:], 1.0)
            nc.gpsimd.memset(tri[:], 1.0)
            nc.gpsimd.memset(lower[:], 1.0)
            nc.gpsimd.memset(ones[:], 1.0).then_inc(pstep, 1)
            pool.wait_ge(pstep, 1)
            for s in range(2):
                nc.gpsimd.memset(v_blk[s][:, :, :, HD:HD + 1], 1.0).then_inc(pstep, 1)
            select(ident[:], [[-1, P]], ALU.is_equal, 0, 1)
            select(tri[:], [[1, P]], ALU.is_gt, 0, -1)
            select(lower[:], [[1, NE], [-1, NE]], ALU.is_gt, 0, 0)
            nc.gpsimd.iota(iota_f[:], [[1, SLOTS + 1]], base=0, channel_multiplier=0,
                           allow_small_or_imprecise_dtypes=True).then_inc(pstep, 1)
            pool.wait_ge(pstep, 7)
            nc.gpsimd.engine_nop().then_inc(consts, 1)
            for s in range(4):
                nc.gpsimd.memset(k_st[s][STACK:ROWS], 1.0).then_inc(kones, 1)
            pool.wait_ge(kones, 4)

            for tile in range(KQ * BLOCKS):
                par = tile % 3
                pool.wait_ge(rest_done, KQ + tile + 1)
                nc.gpsimd.tensor_copy(parts[par][:, 1, :], rest[par]).then_inc(pstep, 1)
                pool.wait_ge(pstep, 7 + tile + 1)
                nc.gpsimd.tensor_tensor(parts[par][:, 2, :], rest[par], parts[par][:, 1, :],
                                        ALU.subtract).then_inc(part3, 1)

            pstep0 = 7 + KQ * BLOCKS

            def cut_max(v, par):
                pool.wait_ge(nm_rest_done, v + 1)
                pool.sem_inc(pool_passed, 1)
                nc.gpsimd.tensor_copy(nm[par][:, 1, :], nm_rest[par]).then_inc(pstep, 1)
                pool.wait_ge(pstep, v + (pstep0 + 1))
                nc.gpsimd.tensor_tensor(nm[par][:, 2, :], nm_rest[par], nm[par][:, 1, :],
                                        ALU.subtract).then_inc(nm_done, 1)
                pool.wait_ge(nm_done, v + 1)
                pool.sem_inc(pool_passed, 1)
                nc.gpsimd.dma_start(neg_max[bass.ds(v, 1)].rearrange("o s r c -> r (o s) c"),
                                    nm[par]).then_inc(nm_out[par], 16)

            cut_order = list(range(2 * HELD, CUTS)) + list(range(2 * HELD))

            def load_cut(c):
                h = cut_order[c]
                stage = (stage_p2 if c < CUTS_P2 else stage_p3)[c % 2]
                nc.gpsimd.dma_start(stage, wgu[h // 2, :, h % 2 * HALF:(h % 2 + 1) * HALF]).then_inc(gu_ld[c % 2], 16)

            def scaled_weights(c):
                return (stage_p2 if c < CUTS_P2 else stage_p3)[c % 2], w_scale[:, cut_order[c] // 2:cut_order[c] // 2 + 1]

            def scale_weights(c):
                stage, scale = scaled_weights(c)
                pool.wait_ge(gu_first, c + 1)
                nc.gpsimd.tensor_tensor(stage, stage, scale.broadcast_to([P, HALF]), ALU.mult).then_inc(gu_scaled, 1)

            def pool_cuts(c):
                return c + 1 if c < CUTS_P2 else CUTS_P2 + (c - CUTS_P2) // 2 + 1

            def second_part(c):
                stage, _ = scaled_weights(c)
                high, low = cut_place(cut_order[c])
                pool.wait_ge(gu_scaled, pool_cuts(c))
                nc.gpsimd.tensor_tensor(low, stage, high, ALU.subtract).then_inc(gu_cut, 1)
                pool.wait_ge(gu_cut, pool_cuts(c))

            def cut_weights(c):
                stage, scale = scaled_weights(c)
                high, _ = cut_place(cut_order[c])
                pool.wait_ge(gu_ld[c % 2], 16 * (c // 2 + 1))
                nc.gpsimd.tensor_tensor(high, stage, scale.broadcast_to([P, HALF]), ALU.mult).then_inc(gu_first, 1)
                scale_weights(c)
                second_part(c)
                if c + 2 < CUTS_P2:
                    load_cut(c + 2)

            cut_max(0, 0)
            pool.wait_ge(kq_ready, KQ * BLOCKS)
            pool.wait_ge(scale_done, 1)
            for c in range(2):
                load_cut(c)
            for v in range(1, UNITS):
                cut_max(v, v % 2)
                if 2 <= v < 2 + CUTS_P2:
                    cut_weights(v - 2)

            pool.wait_ge(attn_done, UNITS * UG)
            for c in range(CUTS_P2, CUTS_P2 + 2):
                load_cut(c)
            for c in range(CUTS_P2, CUTS):
                if (c - CUTS_P2) % 2 == 0:
                    scale_weights(c)
                    second_part(c)
                else:
                    pool.wait_ge(gu_cut_v, (c - CUTS_P2) // 2 + 1)
                if c + 2 < CUTS:
                    load_cut(c + 2)

            pool.wait_ge(slots_done, 1)
            pool.wait_ge(zeroed, 16 * 13)
            for s in range(2):
                pool.wait_ge(xn2_stored[s], FREE + 16 * TILES // 2)
            def load_scatter(t):
                nc.gpsimd.dma_start(scatter_in[t % 4], xn2_dram[t]).then_inc(sc_ld[t % 4], 16)

            for t in range(2):
                load_scatter(t)
            for t in range(TILES):
                pool.wait_ge(sc_ld[t % 4], 16 * (t // 4 + 1))
                for idx in (p1_i, p2_i):
                    nc.gpsimd.indirect_dma_start(
                        out=slot_x, out_offset=bass.IndirectOffsetOnAxis(ap=idx[:, t:t + 1], axis=0),
                        in_=scatter_in[t % 4], in_offset=None).then_inc(sc_st[t % 4], 16)
                if t + 2 < TILES:
                    if t >= 2:
                        pool.wait_ge(sc_st[(t - 2) % 4], 32 * ((t - 2) // 4 + 1))
                    load_scatter(t + 2)

            for s in range(2):
                pool.wait_ge(y_st[s], FREE + 16 * ((SLOTS + 1 - s) // 2))
            for q in range(2 * EARLY):
                t, buf = q // 2 + q % 2 * EARLY, q % 4
                if q >= 4:
                    pool.wait_ge(out_st[buf], 16 * (q // 4))
                for to, idx in ((gather_1[buf], p1_i), (gather_2[buf], p2_i)):
                    nc.gpsimd.indirect_dma_start(
                        out=to, out_offset=None, in_=slot_y,
                        in_offset=bass.IndirectOffsetOnAxis(ap=idx[:, t:t + 1], axis=0)).then_inc(gat_ld[buf], 16)

        @block.scalar
        def _(act):
            for stored in parts_st + v_st_dma + lnt_stored:
                act.sem_inc(stored, FREE)
            act.wait_ge(consts, 2)

            def cut_first(n, l):
                par, uses = (KQ * n + l) % 3, (KQ * n + l) // 3
                act.wait_ge(kq_ready, KQ * n + l + 1)
                act.wait_ge(parts_st[par], FREE + 16 * uses)
                nc.scalar.copy(parts[par][:, 0, :], bank[l][:]).then_inc(part1, 1)

            def std_block(n):
                act.wait_ge(var_done, n + 1)
                nc.scalar.activation(std[:], var_e[:], ACT.Sqrt).then_inc(std_done, 1)

            std_block(0)
            for n in range(BLOCKS):
                s = n % 2
                cut_first(n, 0)
                act.wait_ge(v_ready, n + 1)
                act.wait_ge(v_st_dma[s], FREE + 16 * (n // 2))
                nc.scalar.copy(v_blk[s][:, :, :, 0:HD],
                               bank[5][:].rearrange("p (a g c) -> p a g c", a=TPB, g=GROUPS)).then_inc(v_free, 1)
                for a in range(TPB):
                    act.wait_ge(xT_ready, n * TPB + a + 1)
                    nc.scalar.copy(xnT[s][:, :, a * P:(a + 1) * P],
                                   bank[6 + a % 2][:].rearrange("p (k t) -> p k t", k=KD)).then_inc(xT_free, 1)
                act.wait_ge(v_free, n + 2)
                act.dma_start(v_blocks[n], v_blk[s].rearrange("p a g c -> p a (g c)")).then_inc(v_st_dma[s], 16)
                if n + 1 < BLOCKS:
                    std_block(n + 1)
                for l in range(1, KQ):
                    cut_first(n, l)

            def attn_act(G, fill_G=True, first=False, evac=True, par=0):
                if fill_G:
                    for f in range(FILLS):
                        kt, pair = f // 2, f % 2
                        act.wait_ge(st_ready, G * FILLS + (f + 1))
                        if f == 0 and not first:
                            act.wait_ge(pv_ready, G - 1)
                        nc.scalar.activation(probs[par][:, kt, pair * 512:(pair + 1) * 512], bank[2 + f][:], ACT.Exp,
                                             scale=SCALE).then_inc(exp_done, 1)
                if evac:
                    act.wait_ge(pv_ready, G)
                    if not first:
                        act.wait_ge(ot_ready, G - 2)
                    nc.scalar.copy(o_raw[1 - par], bank[6][:, 0:SEQ]).then_inc(pv_evac, 1)

            for G in range(UG):
                attn_act(G, first=(G < 3), evac=(G > 0), par=G % 2)
            with act.Fori(0, 3) as i:
                for r in range(4 * UG):
                    attn_act(i * (4 * UG) + (UG + r), par=r % 2)
            with act.Fori(0, 3) as i:
                for j in range(UG):
                    attn_act(i * UG + (13 * UG + j), par=j % 2)
            attn_act(UNITS * UG, fill_G=False, par=0)

            act.wait_ge(zeroed, 16 * 13)

            def ot_evac(t, s):
                act.wait_ge(ota_ready, t + 1)
                nc.scalar.copy(oT[s], bank[s][:].rearrange("p (k t) -> p k t", k=KD)).then_inc(ota_evac, 1)

            def lnt_out(t, s, stored):
                act.wait_ge(lnt_ready, t + 1)
                act.wait_ge(lnt_stored[s], stored * 16 + FREE)
                nc.scalar.activation(ln16[s][:, 0:D], bank[4 + s][:], ACT.Copy, scale=X_SCALE)
                nc.scalar.copy(lnT[s], bank[4 + s][:]).then_inc(lnt_evac, 1)

            def gate_out(t, s):
                act.wait_ge(gate_ready, t + 1)
                nc.scalar.copy(logits[:, bass.ds(t, 1), :], bank[6 + s][:, 0:NE].unsqueeze(1)).then_inc(gate_evac, 1)

            def std2(t):
                act.wait_ge(var2_done, t + 1)
                nc.scalar.activation(std[:, 0:1], var_e[:, 0:1], ACT.Sqrt).then_inc(std2_done, 1)

            ot_evac(0, 0)
            for t in range(2):
                ot_evac(t + 1, (t + 1) % 2)
                std2(t)
            def first_part(e, half):
                act.wait_ge(gu_ld[half], e * 16 + (16 * CUTS_P2 // 2 + 16))
                nc.scalar.activation(weights16[:, bass.ds(e * (2 * GU_W) + (2 * GU0 + half * HALF), HALF)],
                                     stage_p3[half], ACT.Copy, scale=w_scale[:, bass.ds(e, 1)]).then_inc(gu_first, 1)

            with act.Fori(1, HELD + 1) as i:
                for s in range(2):
                    lnt_out(i * 2 + s - 2, s, i - 1)
                    ot_evac(i * 2 + (s + 1), 1 - s)
                    std2(i * 2 + s)
                    gate_out(i * 2 + s - 2, s)
                    first_part(i - 1, s)
            assert HELD + 1 == TILES // 2 - 2 and CUTS_P2 % 2 == 0
            for t in range(2 * HELD + 2, TILES - 2):
                lnt_out(t - 2, t % 2, t // 2 - 1)
                ot_evac(t + 1, (t + 1) % 2)
                std2(t)
                gate_out(t - 2, t % 2)
            for t in range(TILES - 2, TILES):
                lnt_out(t - 2, t % 2, t // 2 - 1)
                if t + 1 < TILES:
                    ot_evac(t + 1, (t + 1) % 2)
                std2(t)
                gate_out(t - 2, t % 2)
            def silu(w, par, inv):
                act.wait_ge(g_ready, w + 1)
                if not (isinstance(w, int) and w < 2):
                    act.wait_ge(h_done, w - 1)
                nc.scalar.activation(sil[par][:], bank[GU_BANKS[par][0]][:, 0:F], ACT.Silu,
                                     scale=inv).then_inc(sil_done, 1)

            def ht_out(w, par):
                act.wait_ge(ht_ready, w + 1)
                if not (isinstance(w, int) and w < 2):
                    act.wait_ge(dn_done, w - 1)
                nc.scalar.copy(hT[par][:, 0:2, :], bank[HT_BANK][:, 0:2 * P].rearrange("p (j t) -> p j t", j=2))
                nc.scalar.copy(hT[par][0:FT[2][1], 2, :], bank[HT_BANK][0:FT[2][1], 2 * P:3 * P]).then_inc(ht_evac, 1)

            for t in range(TILES - 2, TILES):
                lnt_out(t, t % 2, t // 2)
                gate_out(t, t % 2)
                silu(t % 2, t % 2, shared_inv(t % 2))
            act.wait_ge(soft_in, 1)
            nc.scalar.activation(score[:], score[:], ACT.Exp).then_inc(soft_exp, 1)
            ht_out(0, 0)
            silu(2, 0, shared_inv(0))
            ht_out(1, 1)
            TOTAL = PA + PB + PC
            assert TOTAL % 2 == 1 and B0 % 2 == 0 and C0 % 2 == 1
            with act.Fori(1, B0 // 2 - 1) as i:
                for par in range(2):
                    silu(i * 2 + (par + 1), 1 - par, shared_inv(1 - par))
                    ht_out(i * 2 + par, par)
            silu(B0 - 1, 1, shared_inv(1))
            ht_out(B0 - 2, 0)
            silu(B0, 0, inv_now[:, 0:1])
            ht_out(B0 - 1, 1)
            with act.Fori(B0 // 2, C0 // 2) as i:
                for par in range(2):
                    silu(i * 2 + (par + 1), 1 - par, inv_now[:, 1 - par:2 - par])
                    ht_out(i * 2 + par, par)
            with act.Fori(C0 // 2, (TOTAL - 1) // 2) as i:
                for par in range(2):
                    silu(i * 2 + (par + 1), 1 - par, shared_inv(par))
                    ht_out(i * 2 + par, par)
            ht_out(TOTAL - 1, 0)

        @block.tensor
        def _(pe):
            pe.wait_ge(consts, 2)

            def project(l, n, lhs, rhs_, between=None, first=False):
                if n > 0:
                    pe.wait_ge(rest_done, n * KQ + l + 1)
                for k in range(KD):
                    if first:
                        pe.wait_ge(c_first[k], 32)
                    mm = nc.tensor.matmul(bank[l][:], lhs(k), rhs_[:, k, :], start=(k == 0), stop=(k == KD - 1))
                    if k == KD - 1:
                        mm.then_inc(kq_ready, 1)
                    if between is not None and k % 2 == 1:
                        between(k // 2)

            def max_fill(v, s, j, f, banks=(0, 1)):
                qt, pair = f // 2, f % 2
                if not (isinstance(v, int) and v == 0 and j == 0 and f < 2):
                    pe.wait_ge(max_done, v * (FILLS * UG) + (FILLS * j + f - 1))
                for c in range(2):
                    mm = nc.tensor.matmul(bank[banks[f % 2]][:, c * SEQ:(c + 1) * SEQ],
                                          q_st[s][0:STACK, HPG * j + 2 * pair + c, qt * P:(qt + 1) * P],
                                          k_st[s][0:STACK, j, :], start=True, stop=True)
                mm.then_inc(max_ready, 1)

            def unit_ready(v, s, n):
                pe.wait_ge(st_ld[s], (n + 1) * (16 * (2 * len(PARTS_Q) + 2)))

            for n in range(BLOCKS):
                s = n % 2
                if n > 0:
                    pe.wait_ge(c_ld[s], 16 * ((n + 1) // 2))
                project(0, n, lambda k: wkv_sb[:, k, 0:P], cxT[s], first=(n == 0))
                pe.wait_ge(v_free, n + 1)
                for a in range(TPB):
                    for k in range(KD):
                        mm = nc.tensor.matmul(bank[5][:, a * P:(a + 1) * P], cxT[s][:, k, a * P:(a + 1) * P],
                                              wkv_sb[:, k, P:2 * P], start=(k == 0), stop=(k == KD - 1))
                mm.then_inc(v_ready, 1)
                for a in range(TPB):
                    pe.wait_ge(ln_done, n * TPB + a + 1)
                    pe.wait_ge(xT_free, n * TPB + a + 1)
                    for k in range(KD):
                        tr = nc.tensor.transpose(bank[6 + a % 2][:, k * P:(k + 1) * P],
                                                 x_in[s][:, a, k * P:(k + 1) * P], ident[:])
                    tr.then_inc(xT_ready, 1)
                pe.wait_ge(w_q, 16)
                pe.wait_ge(xT_free, n * TPB + 2 + TPB)
                last = n == BLOCKS - 1
                if last:
                    unit_ready(0, 0, 0)
                for m in range(KD):
                    project(1 + m, n, lambda k: wq_sb[:, k, m * P:(m + 1) * P], xnT[s],
                            between=(lambda h: [max_fill(0, 0, m, f, (6, 7)) for f in (2 * h, 2 * h + 1)]) if last else None)

            pe.wait_ge(rest_done, KQ * BLOCKS + 2)
            pe.wait_ge(xT_free, TILES + 2)

            def max_transpose(v, par):
                pe.wait_ge(max_done, v * (FILLS * UG) + FILLS * UG)
                if not (isinstance(v, int) and v < 2):
                    pe.wait_ge(attn_done, v * UG - 6)
                elif v == 1:
                    pe.wait_ge(nm_rest_done, 1)
                nc.tensor.transpose(bank[7][0:2 * UH, MXT:MXT + P], mx[par].rearrange("p h q -> p (h q)"),
                                    ident[:]).then_inc(mxt_ready, 1)

            def score_fill(G, s, j, f, first=False):
                kt, pair = f // 2, f % 2
                if not first:
                    pe.wait_ge(exp_done, G * FILLS + (f + 1 - FILLS))
                nc.tensor.matmul(bank[2 + f][:], k_st[s][0:ROWS, j, kt * P:(kt + 1) * P],
                                 q_st[s][0:ROWS, HPG * j + 2 * pair:HPG * j + 2 * pair + 2, :]
                                 .rearrange("p h t -> p (h t)"), start=True, stop=True).then_inc(st_ready, 1)

            def pv_part(G, s, j, f):
                kt = f // 2
                if f == 0:
                    pe.wait_ge(exp_done, G * FILLS + FILLS)
                    if not (isinstance(G, int) and G == 0):
                        pe.wait_ge(pv_evac, G)
                for c in (2 * (f % 2), 2 * (f % 2) + 1):
                    mm = nc.tensor.matmul(bank[6][VW * c:VW * (c + 1), 0:SEQ], v_st[s][:, kt, j, :],
                                          probs[j % 2][:, kt, c * SEQ:(c + 1) * SEQ],
                                          start=(kt == 0), stop=(kt == 1), tile_position=(0, VW * c))
                if f == FILLS - 1:
                    mm.then_inc(pv_ready, 1)

            def attn_transpose(G, par, unit=None):
                pe.wait_ge(pv_evac, G + 1)
                if not (isinstance(G, int) and G == 0):
                    pe.wait_ge(attn_done, G)
                if unit is not None:
                    pe.wait_ge(nm_rest_done, unit + 1)
                for qt in range(2):
                    tr = nc.tensor.transpose(bank[7][:, qt * P:(qt + 1) * P], o_raw[par][:, qt * P:(qt + 1) * P],
                                             ident[:])
                tr.then_inc(ot_ready, 1)

            def attn_step(u, s, n, has_max=True, first=False, last=False):
                sv = (s + 2) % 4
                if has_max:
                    unit_ready(u + 2, sv, n + (s + 2) // 4)
                pe.wait_ge(nm_in[s], (n + 1) * 16)
                for j in range(UG):
                    G = u * UG + j
                    for f in range(FILLS):
                        if has_max:
                            max_fill(u + 2, sv, j, f)
                        score_fill(G, s, j, f, first=(first and j == 0))
                        if f in (1, 2) and not (first and j == 0):
                            for quarter in (2 * f - 2, 2 * f - 1):
                                pv_part(G - 1, s if j > 0 else (s - 1) % 4, (j - 1) % UG, quarter)
                        if j == 0 and f == 1 and not last:
                            max_transpose(u + 1, (s + 1) % 2)
                        if f == 3 and not (first and j < 2):
                            attn_transpose(G - 2, j % 2, unit=(u + 1 if j == 0 and not last else None))

            unit_ready(1, 1, 0)
            for j in range(UG):
                for f in range(FILLS):
                    max_fill(1, 1, j, f)
                    if j == 0 and f == 0:
                        max_transpose(0, 0)
                    if j == 1 and f == 1:
                        pe.wait_ge(w_max_done, 1)
                        nc.tensor.transpose(bank[6][0:NE + SH, 0:P], w_max[:], ident[:]).then_inc(w_max_t, 1)
            pe.wait_ge(w_max_b, 1)
            nc.tensor.transpose(bank[6][:, P:P + NE + SH], w_max_rows, ident[0:NE + SH, 0:NE + SH]).then_inc(w_max_tt, 1)
            pe.wait_ge(scale_done, 1)
            pe.wait_ge(rest_done, KQ * (BLOCKS + 1))
            pe.wait_ge(v_free, BLOCKS + 1)
            pe.wait_ge(kones, 4)
            attn_step(0, 0, 0, first=True)
            with pe.Fori(0, 3) as i:
                for r in range(4):
                    attn_step(i * 4 + (1 + r), (1 + r) % 4, i + (1 + r) // 4)
            attn_step(13, 1, 3)
            attn_step(14, 2, 3, has_max=False)
            attn_step(15, 3, 3, has_max=False, last=True)
            LAST = UNITS * UG - 1
            for f in range(FILLS):
                pv_part(LAST, 3, UG - 1, f)
            attn_transpose(LAST - 1, 0)
            attn_transpose(LAST, 1)

            pe.wait_ge(attn_done, LAST + 1)
            pe.wait_ge(w_fc, 16)
            pe.wait_ge(w_gate, 16)

            def ot_transpose(t, s, n):
                pe.wait_ge(a_ld[s], n * 16 + 16)
                if not (isinstance(t, int) and t < 2):
                    pe.wait_ge(ota_evac, t - 1)
                for k in range(KD):
                    tr = nc.tensor.transpose(bank[s][:, k * P:(k + 1) * P], a_in[s][:, k * P:(k + 1) * P], ident[:])
                tr.then_inc(ota_ready, 1)

            def out_project(t, s):
                pe.wait_ge(ota_evac, t + 1)
                if not (isinstance(t, int) and t < 2):
                    pe.wait_ge(x2_done, t - 1)
                for k in range(KD):
                    mm = nc.tensor.matmul(bank[2 + s][:], oT[s][:, k, :], wfc_sb[:, k, :],
                                          start=(k == 0), stop=(k == KD - 1))
                mm.then_inc(fc_ready, 1)

            def ln_transpose(t, s):
                pe.wait_ge(ln2_done, t + 1)
                if not (isinstance(t, int) and t < 2):
                    pe.wait_ge(lnt_evac, t - 1)
                for k in range(KD):
                    tr = nc.tensor.transpose(bank[4 + s][:, k * P:(k + 1) * P], xn2_sb[s][:, k * P:(k + 1) * P],
                                             ident[:])
                tr.then_inc(lnt_ready, 1)

            def gate(t, s):
                pe.wait_ge(lnt_evac, t + 1)
                if not (isinstance(t, int) and t < 2):
                    pe.wait_ge(gate_evac, t - 1)
                for k in range(KD):
                    mm = nc.tensor.matmul(bank[6 + s][:, 0:NE], lnT[s][:, k * P:(k + 1) * P], gw_sb[:, k, :],
                                          start=(k == 0), stop=(k == KD - 1))
                mm.then_inc(gate_ready, 1)

            ot_transpose(0, 0, 0)
            for t in range(2):
                ot_transpose(t + 1, (t + 1) % 2, (t + 1) // 2)
                out_project(t, t)
            for t in range(2, 4):
                ln_transpose(t - 2, t % 2)
                ot_transpose(t + 1, (t + 1) % 2, (t + 1) // 2)
                out_project(t, t % 2)
                gate(t - 2, t % 2)
            with pe.Fori(2, TILES // 2 - 1) as i:
                for s in range(2):
                    ln_transpose(i * 2 + s - 2, s)
                    ot_transpose(i * 2 + (s + 1), 1 - s, i + (s + 1) // 2)
                    out_project(i * 2 + s, s)
                    gate(i * 2 + s - 2, s)
            for t in range(TILES - 2, TILES):
                ln_transpose(t - 2, t % 2)
                if t + 1 < TILES:
                    ot_transpose(t + 1, (t + 1) % 2, (t + 1) // 2)
                out_project(t, t % 2)
                gate(t - 2, t % 2)


            def h_transpose(w, par):
                pe.wait_ge(h_done, w + 1)
                if not (isinstance(w, int) and w == 0):
                    pe.wait_ge(ht_evac, w)
                for j, (f0, fs) in enumerate(FT):
                    tr = nc.tensor.transpose(bank[HT_BANK][0:fs, j * P:(j + 1) * P], h_sb[par][:, f0:f0 + fs], ident[:])
                tr.then_inc(ht_ready, 1)

            def gate_up(w, par, x_T, gu):
                if not (isinstance(w, int) and w < 2):
                    pe.wait_ge(h_done, w - 1)
                for which, ready in ((0, g_ready), (1, u_ready)):
                    for k in range(KD):
                        for n, (xp, wp) in enumerate(((0, 0), (0, 1), (1, 0))):
                            mm = nc.tensor.matmul(bank[GU_BANKS[par][which]][:, 0:F],
                                                  x_T[:, xp * D + k * P:xp * D + (k + 1) * P], gu(wp, k, which),
                                                  start=(k == 0 and n == 0), stop=(k == KD - 1 and n == 2))
                    mm.then_inc(ready, 1)
                    if which == 0 and not (isinstance(w, int) and w == 0):
                        h_transpose(w - 1, 1 - par)

            def down(w, par, n, ypar, dn, begin=True, end=True):
                pe.wait_ge(ht_evac, w + 1)
                if begin and not (isinstance(n, int) and n < 2):
                    pe.wait_ge(y_evac, n - 1)
                for j, (f0, fs) in enumerate(FT):
                    mm = nc.tensor.matmul(bank[Y_BANKS[ypar]][:], hT[par][0:fs, j, :], dn(j, fs),
                                          start=(begin and j == 0), stop=(end and j == len(FT) - 1))
                mm.then_inc(dn_done, 1)

            def shared_gu(c):
                def columns(part, k, which):
                    at = 2 * (SHGU0 + c * GU_W) + part * GU_W + (2 * k + which) * F
                    return weights16[:, at:at + F]
                return columns

            def shared_dn(c):
                return lambda j, fs: words(SHDN0 + c * DN_W + j * D, D)[0:fs]

            def routed_gu(m):
                off = pe.value_load(gu_off[0:1, bass.ds(m, 1)], min_val=0, max_val=(NE - 1) * 2 * GU_W)
                return lambda part, k, which: weights16[:, bass.ds(off + (2 * GU0 + part * GU_W + (2 * k + which) * F), F)]

            def routed_dn(m):
                off = pe.value_load(dn_off[0:1, bass.ds(m, 1)], min_val=0, max_val=(NE - 1) * DN_W)
                return lambda j, fs: weights[0:fs, bass.ds(off + (DN0 + j * D), D)]

            def early_up(t, s, n, c):
                if c == 0:
                    pe.wait_ge(sx_ld[s], n * 16 + 16)
                gate_up(t * 2 + c, c, first_xT[s] if isinstance(t, int) and t < 2 else xT[s], shared_gu(c))

            def early_down(t, s, c):
                down(t * 2 + c, c, t, s, shared_dn(c), begin=(c == 0), end=(c == 1))

            pe.wait_ge(ota_evac, TILES)
            pe.wait_ge(w_shared, 16 * 2 * SH)
            pe.wait_ge(gu_cut, CUTS_P2)
            ln_transpose(TILES - 2, 0)
            early_up(0, 0, 0, 0)
            gate(TILES - 2, 0)
            pe.wait_ge(x2_done, TILES)
            ln_transpose(TILES - 1, 1)
            pe.wait_ge(gate_evac, TILES - 1)
            early_up(0, 0, 0, 1)
            gate(TILES - 1, 1)
            pe.wait_ge(gate_evac, TILES)
            early_down(0, 0, 0)
            early_up(1, 1, 0, 0)
            pe.wait_ge(sel_done, 1)
            flat = sel[:].rearrange("p t e -> p (t e)")
            nc.tensor.matmul(bank[XT_BANK][:, 0:P], tri[:], flat, start=True, stop=True)
            nc.tensor.matmul(bank[XT_BANK][:, P:2 * P], ones[:], flat, start=True, stop=True).then_inc(pre_ready, 1)
            early_down(0, 0, 1)
            early_up(1, 1, 0, 1)
            early_down(1, 1, 0)

            def early_tile(t, s, n, before_last=None):
                early_up(t, s, n, 0)
                early_down(t - 1, 1 - s, 1)
                early_up(t, s, n, 1)
                if before_last is not None:
                    before_last()
                early_down(t, s, 0)

            with pe.Fori(1, EARLY // 2 - 1) as i:
                for s in range(2):
                    early_tile(i * 2 + s, s, i)
            early_tile(EARLY - 2, 0, EARLY // 2 - 1)


            def slot_transpose(m, s, n):
                pe.wait_ge(slot_ld[s], n * 16 + 16)
                if not (isinstance(m, int) and m == 0):
                    pe.wait_ge(xt_evac, m)
                for k in range(KD):
                    tr = nc.tensor.transpose(bank[XT_BANK][:, k * P:(k + 1) * P], slot_in[s][:, k * P:(k + 1) * P],
                                             ident[:])
                tr.then_inc(xt_ready, 1)

            def slot_up(m, s):
                pe.wait_ge(xt_evac, m + 1)
                gate_up(m + B0, s, xT[s], routed_gu(m))

            def slot_down(m, s):
                down(m + B0, s, m + YB0, (YB0 + s) % 2, routed_dn(m))

            pe.wait_ge(slots_done, 1)
            early_tile(EARLY - 1, 1, EARLY // 2 - 1, before_last=lambda: slot_transpose(0, 0, 0))
            slot_transpose(1, 1, 0)
            pe.wait_ge(offs_done, 1)
            pe.wait_ge(w_routed, 16 * 2 * NE)
            pe.wait_ge(gu_cut, CUTS - HELD)
            pe.wait_ge(gu_cut_v, HELD)
            slot_up(0, 0)
            early_down(EARLY - 1, (EARLY - 1) % 2, 1)
            with pe.Fori(0, (SLOTS - 3) // 2) as i:
                for r in range(2):
                    m = i * 2 + (1 + r)
                    slot_transpose(m + 1, r, i + 1)
                    slot_up(m, 1 - r)
                    slot_down(m - 1, r)
            m = SLOTS - 2
            slot_transpose(m + 1, (m + 1) % 2, (m + 1) // 2)
            slot_up(m, m % 2)
            slot_down(m - 1, (m - 1) % 2)
            slot_up(m + 1, (m + 1) % 2)
            slot_down(m, m % 2)

            def late_up(m, s, n, c):
                if c == 0:
                    pe.wait_ge(lx_ld[s], n * 16 + 16)
                gate_up(m * 2 + (C0 + c), (C0 + c) % 2, late_xT[s], shared_gu(c))

            def late_down(m, s, c):
                down(m * 2 + (C0 + c), (C0 + c) % 2, m + YC0, s, shared_dn(c), begin=(c == 0), end=(c == 1))

            late_up(0, 0, 0, 0)
            slot_down(SLOTS - 1, (SLOTS - 1) % 2)
            late_up(0, 0, 0, 1)
            late_down(0, YC0 % 2, 0)
            late_up(1, 1, 0, 0)
            late_down(0, YC0 % 2, 1)
            late_up(1, 1, 0, 1)
            late_down(1, (YC0 + 1) % 2, 0)
            with pe.Fori(1, (TILES - EARLY) // 2) as i:
                for r in range(2):
                    m = i * 2 + r
                    late_up(m, r, i, 0)
                    late_down(m - 1, (YC0 + r + 1) % 2, 1)
                    late_up(m, r, i, 1)
                    late_down(m, (YC0 + r) % 2, 0)
            h_transpose(C0 + PC - 1, (C0 + PC - 1) % 2)
            late_down(TILES - EARLY - 1, (YC0 + TILES - EARLY - 1) % 2, 1)

        @block.vector
        def _(dve):
            def chain(start):
                count = [0]

                def link(ins, relay=False):
                    count[0] += 1
                    ins.then_inc(step, 1)
                    dve.wait_ge(step, start + count[0])
                    if relay:
                        dve.sem_inc(dve_passed, 1)
                link.count = count
                return link

            def newton(link, n):
                v, sd, a, b, r = var_e[:, 0:n], std[:, 0:n], rs_a[:, 0:n], rs_b[:, 0:n], rstd[:, 0:n]
                link(nc.vector.reciprocal(a, sd))
                link(nc.vector.tensor_tensor(b, a, a, ALU.mult))
                link(nc.vector.tensor_tensor(b, b, v, ALU.mult))
                link(nc.vector.tensor_scalar(b, b, -0.5, 1.5, ALU.mult, ALU.add))
                link(nc.vector.tensor_tensor(r, a, b, ALU.mult))

            dve.sem_inc(xT_free, 2)
            dve.sem_inc(rest_done, KQ)
            dve.sem_inc(v_free, 1)
            for stored in attn_st + x2_stored + xn2_stored + y_st:
                dve.sem_inc(stored, FREE)
            LN_STEPS = 7

            def norm_block(n):
                s = n % 2
                link = chain(n * LN_STEPS)
                dve.wait_ge(x_ld[s], 16 * (n // 2 + 1))
                for a in range(TPB):
                    st = nc.vector.bn_stats(stats[:, a, :], x_in[s][:, a, :])
                link(st)
                for a in range(TPB):
                    st = nc.vector.bn_aggr(mv[:, a, :], stats[:, a, :])
                link(st)
                nc.vector.tensor_scalar(var_e[:], mv[:, :, 1], EPS, None, ALU.add).then_inc(var_done, 1)
                dve.wait_ge(std_done, n + 1)
                newton(link, TPB)
                for a in range(TPB):
                    nc.vector.tensor_scalar(x_in[s][:, a, :], x_in[s][:, a, :], mv[:, a, 0:1], rstd[:, a:a + 1],
                                            ALU.subtract, ALU.mult).then_inc(ln_done, 1)

            def reduce(v, par, j, f, banks=(0, 1)):
                qt, pair = f // 2, f % 2
                dve.wait_ge(max_ready, v * (FILLS * UG) + (FILLS * j + f + 1))
                nc.vector.tensor_reduce(mx[par][:, HPG * j + 2 * pair:HPG * j + 2 * pair + 2, qt:qt + 1],
                                        bank[banks[f % 2]][:].rearrange("p (c k) -> p c k", c=2), AX.X,
                                        ALU.max).then_inc(max_done, 1)

            def cut_rest(n, l):
                par, half = (KQ * n + l) % 3, (KQ * n + l) % 2
                dve.wait_ge(part1, n * KQ + l + 1)
                nc.vector.tensor_tensor(rest[par], bank[l][:], parts[par][:, 0, :], ALU.subtract).then_inc(rest_done, 1)
                dve.wait_ge(max_ld[half], 16 * ((KQ * n + l) // 2 + 1))
                nc.vector.tensor_reduce(half_max[:, n * KQ + l:n * KQ + l + 1], max_stage[half], AX.X, ALU.max,
                                        apply_absolute_value=True).then_inc(half_max_done, 1)

            norm_block(0)
            for n in range(BLOCKS - 1):
                for l in range(KQ):
                    cut_rest(n, l)
                    if l == 0:
                        norm_block(n + 1)
            for l in range(KQ):
                if l >= 1:
                    for f in (0, 1):
                        reduce(0, 0, l - 1, f, (6, 7))
                if l >= 2 or l == 0:
                    cut_rest(BLOCKS - 1, max(l - 1, 0))
                if l >= 1:
                    for f in (2, 3):
                        reduce(0, 0, l - 1, f, (6, 7))
            cut_rest(BLOCKS - 1, KQ - 1)

            links = BLOCKS * LN_STEPS

            def neg_max_part(v, par, n):
                dve.wait_ge(mxt_ready, v + 1)
                if not (isinstance(n, int) and n == 0):
                    dve.wait_ge(nm_out[par], n * 16)
                nc.vector.tensor_scalar(nm[par][:, 0, :], bank[7][0:2 * UH, MXT:MXT + P], -1.0, None,
                                        ALU.mult).then_inc(nm_first, 1)
                dve.wait_ge(nm_first, v + 1)
                nc.vector.scalar_tensor_tensor(nm_rest[par], bank[7][0:2 * UH, MXT:MXT + P], -1.0, nm[par][:, 0, :],
                                               ALU.mult, ALU.subtract).then_inc(nm_rest_done, 1)

            def normalise(G, half, b, j):
                dve.wait_ge(ot_ready, G + 1)
                if j == 0:
                    dve.wait_ge(attn_st[half], b * 16 + FREE)
                src = bank[7][:, 0:2 * P].rearrange("p (q h c) -> p q h c", q=2, c=VW)
                nc.vector.reciprocal(o_rec, src[:, :, :, HD]).then_inc(rec_done, 1)
                dve.wait_ge(rec_done, G + 1)
                nc.vector.tensor_tensor(
                    attn_u[half][:, :, j * HPG * HD:(j + 1) * HPG * HD].rearrange("p q (h d) -> p q h d", d=HD),
                    src[:, :, :, 0:HD], o_rec.unsqueeze(3).broadcast_to([P, 2, HPG, HD]),
                    ALU.mult).then_inc(attn_done, 1)

            def attn_step(u, par, n, has_max=True, first=False, last=False):
                for j in range(UG):
                    for f in range(FILLS):
                        if has_max:
                            reduce(u + 2, par, j, f)
                        if f == 0 and not (first and j < 3):
                            if j < 3:
                                normalise(u * UG + (j - 3), 1 - par, n - 1 + par, j + 1)
                            else:
                                normalise(u * UG, par, n, 0)
                        if j == 0 and f == 2 and not last:
                            neg_max_part(u + 1, 1 - par, n + par)

            assert CUTS == KQ * BLOCKS
            dve.wait_ge(half_max_done, CUTS)
            nc.vector.tensor_reduce(w_max[:], half_max[:].rearrange("p (e h) -> p e h", h=2), AX.X,
                                    ALU.max).then_inc(w_max_done, 1)
            for j in range(UG):
                for f in range(FILLS):
                    reduce(1, 1, j, f)
                    if j == 0 and f == 0:
                        neg_max_part(0, 0, 0)
                    if j == 2 and f == 1:
                        dve.wait_ge(w_max_t, 1)
                        nc.vector.tensor_reduce(w_max_all[:], bank[6][0:NE + SH, 0:P], AX.X, ALU.max).then_inc(w_max_b0, 1)
                        dve.wait_ge(w_max_b0, 1)
                        nc.vector.tensor_copy(w_max_rows, w_max_all[:].broadcast_to([NE + SH, P])).then_inc(w_max_b, 1)
            link = chain(links)
            dve.wait_ge(w_max_tt, 1)
            link(nc.vector.tensor_scalar(w_max[:], bank[6][:, P:P + NE + SH], 2.0 ** -100, None, ALU.max))
            link(nc.vector.tensor_scalar(w_exp[:], w_max[:].bitcast(I32), 0x7F800000, None, ALU.bitwise_and))
            nc.vector.tensor_scalar(w_scale_i[:], w_exp[:], -1.0, float((2 * 127 + TOP_EXP) << 23), ALU.mult, ALU.add)
            nc.vector.tensor_scalar(w_inv_i[:], w_exp[:], float((TOP_EXP + 10) << 23), None,
                                    ALU.subtract).then_inc(scale_done, 1)
            links += link.count[0]
            attn_step(0, 0, 0, first=True)
            with dve.Fori(0, 3) as i:
                for r in range(4):
                    attn_step(i * 4 + (1 + r), (1 + r) % 2, i * 2 + (1 + r) // 2)
            attn_step(13, 1, 6)
            attn_step(14, 0, 7, has_max=False)
            attn_step(15, 1, 7, has_max=False, last=True)
            for G in range(UNITS * UG - 3, UNITS * UG):
                normalise(G, 1, 7, G % UG)

            def cut_rows(t, s):
                dve.wait_ge(lnt_evac, t + 1)
                nc.vector.scalar_tensor_tensor(ln16[s][:, D:2 * D], lnT[s], X_SCALE, ln16[s][:, 0:D],
                                               ALU.mult, ALU.subtract).then_inc(ln16_done, 1)

            def residual_norm(t, s, n):
                link = chain(t * 7 + links)
                dve.wait_ge(fc_ready, t + 1)
                dve.wait_ge(xb_done, t + 1)
                dve.wait_ge(x2_stored[s], n * 16 + FREE)
                nc.vector.tensor_tensor(x2_sb[s], bank[2 + s][:], res_in[s], ALU.add).then_inc(x2_done, 1)
                dve.wait_ge(x2_done, t + 1)
                link(nc.vector.bn_stats(stats[:, 0, :], x2_sb[s]), relay=True)
                link(nc.vector.bn_aggr(mv[:, 0, :], stats[:, 0, :]))
                nc.vector.tensor_scalar(var_e[:, 0:1], mv[:, 0, 1:2], EPS, None, ALU.add).then_inc(var2_done, 1)
                if not (isinstance(t, int) and t < 2):
                    cut_rows(t - 2, s)
                dve.wait_ge(std2_done, t + 1)
                newton(link, 1)
                dve.wait_ge(xn2_stored[s], n * 16 + FREE)
                nc.vector.tensor_scalar(xn2_sb[s], x2_sb[s], mv[:, 0, 0:1], rstd[:, 0:1],
                                        ALU.subtract, ALU.mult).then_inc(ln2_done, 1)

            def add_bias(s, n):
                dve.wait_ge(r_ld[s], n * 16 + 16)
                nc.vector.tensor_tensor(res_in[s], res_in[s], bfc_sb, ALU.add).then_inc(xb_done, 1)

            dve.wait_ge(w_fc, 32)
            add_bias(0, 0)
            for t in range(2):
                residual_norm(t, t, 0)
                add_bias(1 - t, t)
            def second_part(e):
                at = e * (2 * GU_W) + (2 * GU0 + HALF)
                dve.wait_ge(gu_first, e * 2 + (CUTS_P2 + 2))
                dve.sem_inc(dve_passed, 1)
                nc.vector.scalar_tensor_tensor(weights16[:, bass.ds(at + GU_W, HALF)], stage_p3[1],
                                               w_scale[:, bass.ds(e, 1)], weights16[:, bass.ds(at, HALF)],
                                               ALU.mult, ALU.subtract).then_inc(gu_cut_v, 1)

            with dve.Fori(1, HELD + 1) as i:
                for s in range(2):
                    residual_norm(i * 2 + s, s, i)
                    add_bias(1 - s, i + s)
                second_part(i - 1)
            for t in range(2 * HELD + 2, TILES):
                residual_norm(t, t % 2, t // 2)
                if t + 1 < TILES:
                    add_bias((t + 1) % 2, (t + 1) // 2)
            for t in range(TILES - 2, TILES):
                cut_rows(t, t % 2)

            link = route_link = chain(links + 7 * TILES)

            def bc(ap, axis, n):
                shape = list(ap.shape)
                return ap.unsqueeze(axis).broadcast_to(shape[:axis] + [n] + shape[axis:])

            def hidden(w, par, inv):
                dve.wait_ge(u_ready, w + 1)
                dve.wait_ge(sil_done, w + 1)
                if not (isinstance(w, int) and w < 2):
                    dve.wait_ge(ht_ready, w - 1)
                nc.vector.scalar_tensor_tensor(h_sb[par][:], bank[GU_BANKS[par][1]][:, 0:F], inv, sil[par][:],
                                               ALU.mult, ALU.mult).then_inc(h_done, 1)

            def softmax():
                dve.wait_ge(gate_evac, TILES)
                link(nc.vector.tensor_reduce(t_tile[:, 0, :], logits[:], AX.X, ALU.max))
                nc.vector.tensor_tensor(score[:], logits[:], bc(t_tile[:, 0, :], 2, NE), ALU.subtract).then_inc(soft_in, 1)
                dve.wait_ge(soft_exp, 1)
                link(nc.vector.tensor_reduce(t_tile[:, 1, :], score[:], AX.X, ALU.add))
                link(nc.vector.reciprocal(t_tile[:, 2, :], t_tile[:, 1, :]))
                link(nc.vector.tensor_tensor(score[:], score[:], bc(t_tile[:, 2, :], 2, NE), ALU.mult))

            def rank(out_, val, n):
                before = cmp_a[:, 0:TILES * n * n].rearrange("p (t i j) -> p t i j", t=TILES, i=n)
                equal = cmp_b[:, 0:TILES * n * n].rearrange("p (t i j) -> p t i j", t=TILES, i=n)
                nc.vector.tensor_tensor(before, bc(val, 2, n), bc(val, 3, n), ALU.is_gt)
                link(nc.vector.tensor_tensor(equal, bc(val, 2, n), bc(val, 3, n), ALU.is_equal))
                left = lower[:, 0:n, 0:n]
                link(nc.vector.tensor_tensor(equal, equal, bc(left, 1, TILES), ALU.mult))
                link(nc.vector.tensor_tensor(before, before, equal, ALU.add))
                link(nc.vector.tensor_reduce(out_, before, AX.X, ALU.add))

            def choose():
                for s in range(2):
                    dve.wait_ge(xn2_stored[s], FREE + 16 * TILES // 2)
                    dve.wait_ge(lnt_stored[s], FREE + 16 * TILES // 2)
                link(nc.vector.tensor_reduce(gmax[:], score[:].rearrange("p t (g e) -> p t g e", e=2), AX.X, ALU.max))
                rank(grank[:], gmax[:], NE // 2)
                link(nc.vector.tensor_scalar(grank[:], grank[:], 2.0, None, ALU.is_lt))
                link(nc.vector.tensor_tensor(score[:].rearrange("p t (g e) -> p t g e", e=2),
                                             score[:].rearrange("p t (g e) -> p t g e", e=2),
                                             bc(grank[:], 3, 2), ALU.mult))
                rank(pos[:], score[:], NE)
                nc.vector.tensor_scalar(sel[:], pos[:], 2.0, None, ALU.is_lt).then_inc(sel_done, 1)
                dve.wait_ge(sel_done, 1)
                link(nc.vector.tensor_tensor(wsel[:], score[:], sel[:], ALU.mult))

            def place():
                dve.wait_ge(pre_ready, 1)
                pre = bank[XT_BANK][:, 0:P].rearrange("p (t e) -> p t e", t=TILES)
                tot = bank[XT_BANK][:, P:2 * P].rearrange("p (t e) -> p t e", t=TILES)
                link(nc.vector.tensor_copy(run_a[:], tot))
                src, dst, d = run_a, run_b, 1
                while d < TILES:
                    nc.vector.tensor_copy(dst[:, 0:d, :], src[:, 0:d, :])
                    link(nc.vector.tensor_tensor(dst[:, d:, :], src[:, d:, :], src[:, 0:TILES - d, :], ALU.add))
                    src, dst, d = dst, src, 2 * d
                full = cmp_a[:, 0:NE * TILES].rearrange("p (e t) -> p e t", e=NE)
                link(nc.vector.tensor_scalar(run_c, iota_f[:, 0:TILES], float(P), None, ALU.mult))
                link(nc.vector.tensor_tensor(full, bc(src[:, TILES - 1, :], 2, TILES), bc(run_c, 1, NE), ALU.is_gt))
                link(nc.vector.tensor_reduce(cnt[:, 0, :], full, AX.X, ALU.add))
                link(nc.vector.tensor_copy(cnt[:, 1, :], cnt[:, 0, :]))
                a, b, d = 1, 2, 1
                while d < NE:
                    nc.vector.tensor_copy(cnt[:, b, 0:d], cnt[:, a, 0:d])
                    link(nc.vector.tensor_tensor(cnt[:, b, d:], cnt[:, a, d:], cnt[:, a, 0:NE - d], ALU.add))
                    a, b, d = b, a, 2 * d
                link(nc.vector.tensor_tensor(cnt[:, 3, :], cnt[:, a, :], cnt[:, 0, :], ALU.subtract))
                link(nc.vector.tensor_scalar(cnt[:, 3, :], cnt[:, 3, :], float(P), None, ALU.mult))
                link(nc.vector.tensor_tensor(pos[:], src[:], tot, ALU.subtract))
                link(nc.vector.tensor_tensor(pos[:], pos[:], pre, ALU.add))
                link(nc.vector.tensor_tensor(pos[:], pos[:], bc(cnt[:, 3, :], 1, TILES), ALU.add))
                link(nc.vector.tensor_tensor(pos[:], pos[:], sel[:], ALU.mult))
                nc.vector.tensor_reduce(t_tile[:, 0, :], pos[:], AX.X, ALU.max)
                link(nc.vector.tensor_reduce(t_tile[:, 1, :], pos[:], AX.X, ALU.add))
                link(nc.vector.tensor_tensor(t_tile[:, 2, :], t_tile[:, 1, :], t_tile[:, 0, :], ALU.subtract))
                nc.vector.tensor_copy(p1_i[:], t_tile[:, 0, :])
                nc.vector.tensor_copy(p2_i[:], t_tile[:, 2, :]).then_inc(slots_done, 1)
                link(nc.vector.tensor_tensor(run_a[:], pos[:], bc(t_tile[:, 0, :], 2, NE), ALU.is_equal))
                link(nc.vector.tensor_tensor(run_a[:], run_a[:], wsel[:], ALU.mult))
                nc.vector.tensor_reduce(w1[:], run_a[:], AX.X, ALU.add)
                link(nc.vector.tensor_tensor(run_b[:], wsel[:], run_a[:], ALU.subtract))
                link(nc.vector.tensor_reduce(w2[:], run_b[:], AX.X, ALU.add))
                ends = bc(cnt[:, a, :], 1, SLOTS + 1)
                cmp_e = tile_cmp[:].rearrange("p (m e) -> p m e", e=NE)
                link(nc.vector.tensor_tensor(cmp_e, bc(iota_f[:], 2, NE), ends, ALU.is_ge))
                link(nc.vector.tensor_reduce(slot_e[:, 0, :], cmp_e, AX.X, ALU.add))
                link(nc.vector.tensor_scalar(slot_e[:, 0, :], slot_e[:, 0, :], float(NE - 1), None, ALU.min))
                link(nc.vector.tensor_tensor(cmp_e, bc(iota_f[:, 0:NE], 1, SLOTS + 1), bc(slot_e[:, 0, :], 2, NE),
                                             ALU.is_equal))
                link(nc.vector.tensor_tensor(cmp_e, cmp_e, bc(w_inv[:, 0:NE], 1, SLOTS + 1), ALU.mult))
                link(nc.vector.tensor_reduce(inv_slot[:], cmp_e, AX.X, ALU.add))
                nc.vector.tensor_scalar(gu_off[:], slot_e[:, 0, :], 2.0 * GU_W, None, ALU.mult)
                nc.vector.tensor_scalar(dn_off[:], slot_e[:, 0, :], float(DN_W), None, ALU.mult).then_inc(offs_done, 1)

            def early_sum(t, s, n):
                dve.wait_ge(dn_done, t * 2 + 2)
                dve.wait_ge(x2_ld[s], n * 16 + 16)
                nc.vector.tensor_tensor(tok_in[s], bank[Y_BANKS[s]][:], tok_in[s], ALU.add).then_inc(y_evac, 1)

            hidden(0, 0, shared_inv(0))
            hidden(1, 1, shared_inv(1))
            softmax()
            choose()
            hidden(2, 0, shared_inv(0))
            place()
            early_sum(0, 0, 0)
            hidden(3, 1, shared_inv(1))
            with dve.Fori(1, EARLY // 2) as i:
                for s in range(2):
                    hidden(i * 4 + 2 * s, 0, shared_inv(0))
                    early_sum(i * 2 + s - 1, 1 - s, i + s - 1)
                    hidden(i * 4 + (2 * s + 1), 1, shared_inv(1))

            def slot_evac(m, s):
                dve.wait_ge(xt_ready, m + 1)
                dve.wait_ge(u_ready, m + (B0 - 1))
                nc.vector.tensor_scalar(xT[s][:, 0:D], bank[XT_BANK][:], X_SCALE, None, ALU.mult).then_inc(xt_first, 1)
                dve.wait_ge(xt_first, m + 1)
                nc.vector.scalar_tensor_tensor(xT[s][:, D:2 * D], bank[XT_BANK][:], X_SCALE, xT[s][:, 0:D],
                                               ALU.mult, ALU.subtract)
                nc.vector.tensor_copy(inv_now[:, s:s + 1], inv_slot[:, bass.ds(m, 1)]).then_inc(xt_evac, 1)

            def slot_result(m, s, n):
                dve.wait_ge(dn_done, m + (B0 + 1))
                dve.wait_ge(y_st[s], n * 16 + FREE)
                nc.vector.tensor_copy(mid[s], bank[Y_BANKS[(YB0 + s) % 2]][:]).then_inc(y_evac, 1)

            for buf in range(4):
                dve.wait_ge(sc_st[buf], 32 * TILES // 4)
            slot_evac(0, 0)
            slot_evac(1, 1)
            hidden(B0, 0, inv_now[:, 0:1])
            early_sum(EARLY - 1, 1, EARLY // 2 - 1)
            with dve.Fori(0, (SLOTS - 3) // 2) as i:
                for r in range(2):
                    m = i * 2 + (1 + r)
                    slot_evac(m + 1, r)
                    hidden(m + B0, 1 - r, inv_now[:, 1 - r:2 - r])
                    slot_result(m - 1, r, i)
            m = SLOTS - 2
            slot_evac(m + 1, (m + 1) % 2)
            hidden(m + B0, m % 2, inv_now[:, m % 2:m % 2 + 1])
            slot_result(m - 1, (m - 1) % 2, (m - 1) // 2)
            hidden(m + 1 + B0, (m + 1) % 2, inv_now[:, (m + 1) % 2:(m + 1) % 2 + 1])
            slot_result(m, m % 2, m // 2)

            def early_out(m, q, n, base_):
                dve.wait_ge(cx2_ld[q], n * 16 + 16)
                dve.wait_ge(gat_ld[q], n * 32 + 32)
                dve_link = chain(base_)
                dve_link(nc.vector.scalar_tensor_tensor(res_out[q], gather_1[q], w1[:, bass.ds(m, 1)], res_out[q],
                                                        ALU.mult, ALU.add))
                nc.vector.scalar_tensor_tensor(gather_2[q], gather_2[q], w2[:, bass.ds(m, 1)], res_out[q],
                                               ALU.mult, ALU.add).then_inc(out_done, 1)

            def late_out(m, ypar, q, n, base_):
                dve.wait_ge(cx2_ld[q], n * 16 + 16)
                dve.wait_ge(dn_done, m * 2 + (C0 + 2))
                nc.vector.tensor_tensor(res_out[q], bank[Y_BANKS[ypar]][:], res_out[q], ALU.add).then_inc(y_evac, 1)
                dve.wait_ge(y_evac, m + (YC0 + 1))
                dve.wait_ge(gat_ld[q], n * 32 + 32)
                dve_link = chain(base_)
                dve_link(nc.vector.scalar_tensor_tensor(res_out[q], gather_1[q], w1[:, bass.ds(m + EARLY, 1)],
                                                        res_out[q], ALU.mult, ALU.add))
                nc.vector.scalar_tensor_tensor(gather_2[q], gather_2[q], w2[:, bass.ds(m + EARLY, 1)], res_out[q],
                                               ALU.mult, ALU.add).then_inc(out_done, 1)

            links4 = links + 7 * TILES + route_link.count[0]
            hidden(C0, C0 % 2, shared_inv(0))
            slot_result(SLOTS - 1, (SLOTS - 1) % 2, (SLOTS - 1) // 2)
            hidden(C0 + 1, (C0 + 1) % 2, shared_inv(1))
            hidden(C0 + 2, C0 % 2, shared_inv(0))
            early_out(0, 0, 0, links4)
            late_out(0, YC0 % 2, 1, 0, links4 + 1)
            hidden(C0 + 3, (C0 + 1) % 2, shared_inv(1))
            with dve.Fori(1, (TILES - EARLY) // 2) as i:
                for r in range(2):
                    m = i * 2 + r
                    hidden(m * 2 + C0, C0 % 2, shared_inv(0))
                    early_out(m - 1, 2 * (1 - r), i + r - 1, (m - 1) * 2 + links4)
                    late_out(m - 1, (YC0 + r + 1) % 2, 2 * (1 - r) + 1, i + r - 1, (m - 1) * 2 + (links4 + 1))
                    hidden(m * 2 + (C0 + 1), (C0 + 1) % 2, shared_inv(1))
            m = TILES - EARLY - 1
            early_out(m, 2 * (m % 2), m // 2, m * 2 + links4)
            late_out(m, (YC0 + m) % 2, 2 * (m % 2) + 1, m // 2, m * 2 + links4 + 1)


def _inputs(x, ctx, Wq, Wk, Wv, Wfc, bfc, gate, gate_w, up_w, down_w, sh_gate, sh_up, sh_down):
    import numpy as np

    def contraction_first(w):
        return np.ascontiguousarray(w.T.reshape(KD, P, -1).transpose(1, 0, 2))

    ctxT = np.ascontiguousarray(ctx.reshape(T, D).T.reshape(KD, P, BLOCKS, BT).transpose(2, 1, 0, 3))
    gates = np.concatenate([gate_w, sh_gate.reshape(SH, F, D)])
    ups = np.concatenate([up_w, sh_up.reshape(SH, F, D)])
    gu = np.stack([gates, ups], 1)
    gu = gu.reshape(NE + SH, 2, F, KD, P).transpose(0, 4, 3, 1, 2).reshape(NE + SH, P, GU_W)
    downs = np.concatenate([down_w, sh_down.reshape(D, SH, F).transpose(1, 0, 2)]).transpose(0, 2, 1)
    dn = downs[:, 0:2 * P].reshape(NE + SH, 2, P, D).transpose(0, 2, 1, 3).reshape(NE + SH, P, 2 * D)
    return {
        "x": np.ascontiguousarray(x.reshape(T, D)), "ctxT": ctxT, "wqT": contraction_first(Wq),
        "wkvT": np.ascontiguousarray(np.concatenate([contraction_first(Wk), contraction_first(Wv)], 2)),
        "wfcT": contraction_first(Wfc), "bfc": np.ascontiguousarray(bfc), "gwT": contraction_first(gate),
        "wgu": np.ascontiguousarray(gu), "wdn": np.ascontiguousarray(dn),
        "wdt": np.ascontiguousarray(downs[:, 2 * P:F]),
    }


def kernel(x, ctx_2048, L0_xattn_Wq, L0_xattn_Wk, L0_xattn_Wv, L0_xattn_Wfc, L0_xattn_bfc, L0_ffn_gate_weight,
           L0_ffn_gate_w, L0_ffn_up_w, L0_ffn_down_w, L0_ffn_sh_gate_w, L0_ffn_sh_up_w, L0_ffn_sh_down_w):
    import numpy as np
    import concourse.bacc as bacc
    from concourse.bass_utils import run_bass_kernel_spmd

    given = [np.asarray(a) for a in (x, ctx_2048, L0_xattn_Wq, L0_xattn_Wk, L0_xattn_Wv, L0_xattn_Wfc, L0_xattn_bfc,
                                     L0_ffn_gate_weight, L0_ffn_gate_w, L0_ffn_up_w, L0_ffn_down_w,
                                     L0_ffn_sh_gate_w, L0_ffn_sh_up_w, L0_ffn_sh_down_w)]
    arrays = {"in_" + k: v for k, v in _inputs(*given).items()}
    nc = bacc.Bacc("TRN2", target_bir_lowering=False, num_devices=1)
    args = [nc.dram_tensor(k, v.shape, mybir.dt.from_np(v.dtype), kind="ExternalInput").ap() for k, v in arrays.items()]
    out = nc.dram_tensor("out", (T, D), F32, kind="ExternalOutput").ap()
    build(nc, *args, out)
    got = run_bass_kernel_spmd(nc, [arrays], core_ids=[0])
    return got.results[0]["out"].reshape(BATCH, SEQ, D)
```
